# Optimizing a Trainium2 kernel written in Bass

```python
import numpy as np
import jax
import jax.numpy as jnp

def _softmax(x, axis=-1):
    return jax.nn.softmax(x, axis=axis)

def _gelu(x):
    return jax.nn.gelu(x, approximate=True)

def _silu(x):
    return jax.nn.silu(x)

def _sigmoid(x):
    return jax.nn.sigmoid(x)

def _layernorm(x, axis=-1, eps=1e-05):
    m = jnp.mean(x, axis=axis, keepdims=True)
    v = jnp.var(x, axis=axis, keepdims=True)
    return (x - m) / jnp.sqrt(v + eps)

def _scatter_add(tgt, idx, src, axis=0):
    return tgt.at[idx].add(src)

def _segment_sum(src, seg, n):
    return jax.ops.segment_sum(src, seg, n)
kernel_name = 'mk_gnn_ffn_d2_gnn_r8_db3a78'

def setup_inputs(seed: int=0):
    np.random.seed(seed)
    _w = jnp.asarray

    def _rec_inputs():
        import jax
        import jax.numpy as jnp
        _gk = jax.random.key(seed)
        x = 7.22e-05 + 1 * jax.random.normal(jax.random.fold_in(_gk, 1), (1250, 512), jnp.float32)
        src = jax.random.randint(jax.random.fold_in(_gk, 2), (20000,), 0, 1250, jnp.int32)
        dst = jax.random.randint(jax.random.fold_in(_gk, 3), (20000,), 0, 1250, jnp.int32)
        _o = jnp.argsort(dst, stable=True)
        src = src[_o]
        dst = dst[_o]
        edge_attr_2 = 0.00222621 + 0.99962 * jax.random.normal(jax.random.fold_in(_gk, 11), (20000, 2), jnp.float32)
        return (x, src, dst, edge_attr_2)
    x, src, dst, edge_attr_2 = _rec_inputs()

    def _L0_gnn_setup():
        import jax, jax.numpy as jnp
        import numpy as np
        N, E, D, ED, L = (2048, 32768, 512, 2, 3)
        EPS = 1e-05
        SLOPE = 0.2

        def _segment_softmax(logits, seg, n):
            m = jax.ops.segment_max(logits, seg, num_segments=n)
            m = jnp.where(jnp.isfinite(m), m, 0.0)
            ex = jnp.exp(logits - m[seg])
            den = jax.ops.segment_sum(ex, seg, num_segments=n)
            return ex / (den[seg] + 1e-16)

        def _forward(x, edge_attr, Wl, bl, Wr, br, We, att, b_out, gamma, beta, edge_index):
            n = x.shape[0]
            src, dst = (edge_index[0], edge_index[1])
            ones = jnp.ones((src.shape[0],), x.dtype)
            cnt = jax.ops.segment_sum(ones, dst, num_segments=n)
            mean_ea = jax.ops.segment_sum(edge_attr, dst, num_segments=n) / jnp.maximum(cnt, 1.0)[:, None]
            loop = jnp.arange(n, dtype=edge_index.dtype)
            src2 = jnp.concatenate([src, loop])
            dst2 = jnp.concatenate([dst, loop])
            ea2 = jnp.concatenate([edge_attr, mean_ea], axis=0)
            for k in range(Wl.shape[0]):
                xl = x @ Wl[k] + bl[k]
                xr = x @ Wr[k] + br[k]
                ef = ea2 @ We[k]
                m = jax.nn.leaky_relu(xl[src2] + xr[dst2] + ef, SLOPE)
                logit = m @ att[k]
                alpha = _segment_softmax(logit, dst2, n)
                out = jax.ops.segment_sum(xl[src2] * alpha[:, None], dst2, num_segments=n) + b_out[k]
                h = out + x
                mu = jnp.mean(h, axis=-1, keepdims=True)
                var = jnp.var(h, axis=-1, keepdims=True)
                h = (h - mu) * jax.lax.rsqrt(var + EPS) * gamma[k] + beta[k]
                x = jax.nn.relu(h)
            return x
        key = jax.random.key(seed)
        ks = jax.random.split(key, 8)
        s = np.float32(1.0 / np.sqrt(D))
        return dict(x=jax.random.normal(ks[0], (N, D), jnp.float32), edge_attr=jax.random.normal(ks[1], (E, ED), jnp.float32), Wl=jax.random.normal(ks[2], (L, D, D), jnp.float32) * s, bl=jnp.zeros((L, D), jnp.float32), Wr=jax.random.normal(ks[3], (L, D, D), jnp.float32) * s, br=jnp.zeros((L, D), jnp.float32), We=jax.random.normal(ks[4], (L, ED, D), jnp.float32) * s, att=jax.random.normal(ks[5], (L, D), jnp.float32) * s, b_out=jnp.zeros((L, D), jnp.float32), gamma=jnp.ones((L, D), jnp.float32), beta=jnp.zeros((L, D), jnp.float32), edge_index=jax.random.randint(ks[6], (2, E), 0, N, dtype=jnp.int32))
    _L0_gnn_all = _L0_gnn_setup()
    _L0_gnn_in = {k: v for k, v in _L0_gnn_all.items() if k in ('Wl', 'bl', 'Wr', 'br', 'We', 'att', 'b_out', 'gamma', 'beta')}
    del _L0_gnn_all

    def _L0_ffn_setup():
        import jax, jax.numpy as jnp
        import numpy as np
        B, S, D, H, E, K = (2, 256, 512, 1024, 8, 2)

        def _moe(x, router_w, w_gate, w_up, w_down):
            bsz, seq, d = x.shape
            flat = x.reshape(-1, d)
            logits = flat @ router_w.T
            topk_vals, topk_idx = jax.lax.top_k(logits, K)
            topk_w = jax.nn.softmax(topk_vals, axis=-1)
            s = flat.shape[0]
            dense_w = jnp.zeros((s, E), dtype=flat.dtype).at[jnp.arange(s)[:, None], topk_idx].add(topk_w)
            g = jnp.einsum('sd,edh->esh', flat, w_gate)
            u = jnp.einsum('sd,edh->esh', flat, w_up)
            y = jnp.einsum('esh,ehd->esd', jax.nn.silu(g) * u, w_down)
            out = jnp.einsum('esd,se->sd', y, dense_w)
            return out.reshape(bsz, seq, d)
        key = jax.random.key(seed)
        k1, k2, k3, k4, k5 = jax.random.split(key, 5)
        return {'x': jax.random.normal(k1, (B, S, D), dtype=jnp.float32), 'router_w': jax.random.normal(k2, (E, D), dtype=jnp.float32) * D ** (-0.5), 'w_gate': jax.random.normal(k3, (E, D, H), dtype=jnp.float32) * D ** (-0.5), 'w_up': jax.random.normal(k4, (E, D, H), dtype=jnp.float32) * D ** (-0.5), 'w_down': jax.random.normal(k5, (E, H, D), dtype=jnp.float32) * H ** (-0.5)}
    _L0_ffn_all = _L0_ffn_setup()
    _L0_ffn_in = {k: v for k, v in _L0_ffn_all.items() if k in ('router_w', 'w_gate', 'w_up', 'w_down')}
    del _L0_ffn_all

    def _L1_gnn_setup():
        import jax, jax.numpy as jnp
        import numpy as np
        N = 1250
        E = 20000
        H = 4
        C = 256
        D_IN = 512
        D_OUT = 512
        NEG_SLOPE = 0.2

        def gat_conv(x, src, dst, W, a_src, a_dst, bias):
            n = x.shape[0]
            h = (x @ W).reshape(n, H, C)
            al_s = jnp.einsum('nhc,hc->nh', h, a_src)
            al_d = jnp.einsum('nhc,hc->nh', h, a_dst)
            e = jax.nn.leaky_relu(al_s[src] + al_d[dst], NEG_SLOPE)
            emax = jax.ops.segment_max(e, dst, num_segments=n)
            w = jnp.exp(e - emax[dst])
            denom = jax.ops.segment_sum(w, dst, num_segments=n)
            alpha = w / denom[dst]
            out = jax.ops.segment_sum(h[src] * alpha[:, :, None], dst, num_segments=n)
            return out.reshape(n, H * C) + bias
        key = jax.random.key(seed)
        ks = jax.random.split(key, 13)
        s = 0.05
        return {'x': jax.random.normal(ks[0], (N, D_IN), jnp.float32), 'edge_index': jax.random.randint(ks[1], (2, E), 0, N, dtype=jnp.int32), 'W1': jax.random.normal(ks[2], (D_IN, H * C), jnp.float32) * s, 'a_src1': jax.random.normal(ks[3], (H, C), jnp.float32) * s, 'a_dst1': jax.random.normal(ks[4], (H, C), jnp.float32) * s, 'b1': jnp.zeros((H * C,), jnp.float32), 'W2': jax.random.normal(ks[5], (H * C, H * C), jnp.float32) * s, 'a_src2': jax.random.normal(ks[6], (H, C), jnp.float32) * s, 'a_dst2': jax.random.normal(ks[7], (H, C), jnp.float32) * s, 'b2': jnp.zeros((H * C,), jnp.float32), 'Wfc': jax.random.normal(ks[8], (H * C, D_OUT), jnp.float32) * s, 'bfc': jnp.zeros((D_OUT,), jnp.float32)}
    _L1_gnn_all = _L1_gnn_setup()
    _L1_gnn_in = {k: v for k, v in _L1_gnn_all.items() if k in ('W1', 'a_src1', 'a_dst1', 'b1', 'W2', 'a_src2', 'a_dst2', 'b2', 'Wfc', 'bfc')}
    del _L1_gnn_all

    def _L1_ffn_setup():
        import jax, jax.numpy as jnp
        import numpy as np
        B, T, D, F, E, K = (8, 1024, 512, 256, 8, 2)

        def _moe_forward(x, Wr, br, W1, b1, W2, b2):
            Bx, Tx, Dx = x.shape
            xf = x.reshape(-1, Dx)
            logits = xf @ Wr + br
            probs = jax.nn.softmax(logits, axis=-1)
            vals, idx = jax.lax.top_k(probs, K)
            cw = (jax.nn.one_hot(idx, E, dtype=x.dtype) * vals[..., None]).sum(axis=1)

            def body(acc, params):
                W1e, b1e, W2e, b2e, cwe = params
                h = jax.nn.relu(xf @ W1e + b1e)
                y = h @ W2e + b2e
                return (acc + cwe[:, None] * y, None)
            out, _ = jax.lax.scan(body, jnp.zeros_like(xf), (W1, b1, W2, b2, cw.T))
            return out.reshape(Bx, Tx, Dx)
        key = jax.random.key(seed)
        k0, k1, k2, k3 = jax.random.split(key, 4)
        s_d = 1.0 / np.sqrt(D)
        s_f = 1.0 / np.sqrt(F)
        return {'x': jax.random.normal(k0, (B, T, D), jnp.float32), 'Wr': jax.random.uniform(k1, (D, E), jnp.float32, -s_d, s_d), 'br': jnp.zeros((E,), jnp.float32), 'W1': jax.random.uniform(k2, (E, D, F), jnp.float32, -s_d, s_d), 'b1': jnp.zeros((E, F), jnp.float32), 'W2': jax.random.uniform(k3, (E, F, D), jnp.float32, -s_f, s_f), 'b2': jnp.zeros((E, D), jnp.float32)}
    _L1_ffn_all = _L1_ffn_setup()
    _L1_ffn_in = {k: v for k, v in _L1_ffn_all.items() if k in ('Wr', 'br', 'W1', 'b1', 'W2', 'b2')}
    del _L1_ffn_all
    return {'x': x, 'src': src, 'dst': dst, 'edge_attr_2': edge_attr_2, 'L0_gnn_Wl': _L0_gnn_in['Wl'], 'L0_gnn_bl': _L0_gnn_in['bl'], 'L0_gnn_Wr': _L0_gnn_in['Wr'], 'L0_gnn_br': _L0_gnn_in['br'], 'L0_gnn_We': _L0_gnn_in['We'], 'L0_gnn_att': _L0_gnn_in['att'], 'L0_gnn_b_out': _L0_gnn_in['b_out'], 'L0_gnn_gamma': _L0_gnn_in['gamma'], 'L0_gnn_beta': _L0_gnn_in['beta'], 'L0_ffn_router_w': _L0_ffn_in['router_w'], 'L0_ffn_w_gate': _L0_ffn_in['w_gate'], 'L0_ffn_w_up': _L0_ffn_in['w_up'], 'L0_ffn_w_down': _L0_ffn_in['w_down'], 'L1_gnn_W1': _L1_gnn_in['W1'], 'L1_gnn_a_src1': _L1_gnn_in['a_src1'], 'L1_gnn_a_dst1': _L1_gnn_in['a_dst1'], 'L1_gnn_b1': _L1_gnn_in['b1'], 'L1_gnn_W2': _L1_gnn_in['W2'], 'L1_gnn_a_src2': _L1_gnn_in['a_src2'], 'L1_gnn_a_dst2': _L1_gnn_in['a_dst2'], 'L1_gnn_b2': _L1_gnn_in['b2'], 'L1_gnn_Wfc': _L1_gnn_in['Wfc'], 'L1_gnn_bfc': _L1_gnn_in['bfc'], 'L1_ffn_Wr': _L1_ffn_in['Wr'], 'L1_ffn_br': _L1_ffn_in['br'], 'L1_ffn_W1': _L1_ffn_in['W1'], 'L1_ffn_b1': _L1_ffn_in['b1'], 'L1_ffn_W2': _L1_ffn_in['W2'], 'L1_ffn_b2': _L1_ffn_in['b2']}

def reference(x, src, dst, edge_attr_2, L0_gnn_Wl, L0_gnn_bl, L0_gnn_Wr, L0_gnn_br, L0_gnn_We, L0_gnn_att, L0_gnn_b_out, L0_gnn_gamma, L0_gnn_beta, L0_ffn_router_w, L0_ffn_w_gate, L0_ffn_w_up, L0_ffn_w_down, L1_gnn_W1, L1_gnn_a_src1, L1_gnn_a_dst1, L1_gnn_b1, L1_gnn_W2, L1_gnn_a_src2, L1_gnn_a_dst2, L1_gnn_b2, L1_gnn_Wfc, L1_gnn_bfc, L1_ffn_Wr, L1_ffn_br, L1_ffn_W1, L1_ffn_b1, L1_ffn_W2, L1_ffn_b2):
    import jax
    import jax.numpy as jnp

    def _L0_gnn_ref(x, edge_attr, Wl, bl, Wr, br, We, att, b_out, gamma, beta, edge_index):
        import jax, jax.numpy as jnp
        import numpy as np
        N, E, D, ED, L = (2048, 32768, 512, 2, 3)
        EPS = 1e-05
        SLOPE = 0.2

        def _segment_softmax(logits, seg, n):
            m = jax.ops.segment_max(logits, seg, num_segments=n)
            m = jnp.where(jnp.isfinite(m), m, 0.0)
            ex = jnp.exp(logits - m[seg])
            den = jax.ops.segment_sum(ex, seg, num_segments=n)
            return ex / (den[seg] + 1e-16)

        def _forward(x, edge_attr, Wl, bl, Wr, br, We, att, b_out, gamma, beta, edge_index):
            n = x.shape[0]
            src, dst = (edge_index[0], edge_index[1])
            ones = jnp.ones((src.shape[0],), x.dtype)
            cnt = jax.ops.segment_sum(ones, dst, num_segments=n)
            mean_ea = jax.ops.segment_sum(edge_attr, dst, num_segments=n) / jnp.maximum(cnt, 1.0)[:, None]
            loop = jnp.arange(n, dtype=edge_index.dtype)
            src2 = jnp.concatenate([src, loop])
            dst2 = jnp.concatenate([dst, loop])
            ea2 = jnp.concatenate([edge_attr, mean_ea], axis=0)
            for k in range(Wl.shape[0]):
                xl = x @ Wl[k] + bl[k]
                xr = x @ Wr[k] + br[k]
                ef = ea2 @ We[k]
                m = jax.nn.leaky_relu(xl[src2] + xr[dst2] + ef, SLOPE)
                logit = m @ att[k]
                alpha = _segment_softmax(logit, dst2, n)
                out = jax.ops.segment_sum(xl[src2] * alpha[:, None], dst2, num_segments=n) + b_out[k]
                h = out + x
                mu = jnp.mean(h, axis=-1, keepdims=True)
                var = jnp.var(h, axis=-1, keepdims=True)
                h = (h - mu) * jax.lax.rsqrt(var + EPS) * gamma[k] + beta[k]
                x = jax.nn.relu(h)
            return x
        return _forward(x, edge_attr, Wl, bl, Wr, br, We, att, b_out, gamma, beta, edge_index)

    def _L0_ffn_ref(x, router_w, w_gate, w_up, w_down):
        import jax, jax.numpy as jnp
        import numpy as np
        B, S, D, H, E, K = (2, 256, 512, 1024, 8, 2)

        def _moe(x, router_w, w_gate, w_up, w_down):
            bsz, seq, d = x.shape
            flat = x.reshape(-1, d)
            logits = flat @ router_w.T
            topk_vals, topk_idx = jax.lax.top_k(logits, K)
            topk_w = jax.nn.softmax(topk_vals, axis=-1)
            s = flat.shape[0]
            dense_w = jnp.zeros((s, E), dtype=flat.dtype).at[jnp.arange(s)[:, None], topk_idx].add(topk_w)
            g = jnp.einsum('sd,edh->esh', flat, w_gate)
            u = jnp.einsum('sd,edh->esh', flat, w_up)
            y = jnp.einsum('esh,ehd->esd', jax.nn.silu(g) * u, w_down)
            out = jnp.einsum('esd,se->sd', y, dense_w)
            return out.reshape(bsz, seq, d)
        return _moe(x, router_w, w_gate, w_up, w_down)

    def _L1_gnn_ref(x, edge_index, W1, a_src1, a_dst1, b1, W2, a_src2, a_dst2, b2, Wfc, bfc):
        import jax, jax.numpy as jnp
        import numpy as np
        N = 1250
        E = 20000
        H = 4
        C = 256
        D_IN = 512
        D_OUT = 512
        NEG_SLOPE = 0.2

        def gat_conv(x, src, dst, W, a_src, a_dst, bias):
            n = x.shape[0]
            h = (x @ W).reshape(n, H, C)
            al_s = jnp.einsum('nhc,hc->nh', h, a_src)
            al_d = jnp.einsum('nhc,hc->nh', h, a_dst)
            e = jax.nn.leaky_relu(al_s[src] + al_d[dst], NEG_SLOPE)
            emax = jax.ops.segment_max(e, dst, num_segments=n)
            w = jnp.exp(e - emax[dst])
            denom = jax.ops.segment_sum(w, dst, num_segments=n)
            alpha = w / denom[dst]
            out = jax.ops.segment_sum(h[src] * alpha[:, :, None], dst, num_segments=n)
            return out.reshape(n, H * C) + bias
        loop = jnp.arange(N, dtype=edge_index.dtype)
        src = jnp.concatenate([edge_index[0], loop])
        dst = jnp.concatenate([edge_index[1], loop])
        h = jax.nn.relu(gat_conv(x, src, dst, W1, a_src1, a_dst1, b1))
        h = jax.nn.relu(gat_conv(h, src, dst, W2, a_src2, a_dst2, b2))
        return h @ Wfc + bfc

    def _L1_ffn_ref(x, Wr, br, W1, b1, W2, b2):
        import jax, jax.numpy as jnp
        import numpy as np
        B, T, D, F, E, K = (8, 1024, 512, 256, 8, 2)

        def _moe_forward(x, Wr, br, W1, b1, W2, b2):
            Bx, Tx, Dx = x.shape
            xf = x.reshape(-1, Dx)
            logits = xf @ Wr + br
            probs = jax.nn.softmax(logits, axis=-1)
            vals, idx = jax.lax.top_k(probs, K)
            cw = (jax.nn.one_hot(idx, E, dtype=x.dtype) * vals[..., None]).sum(axis=1)

            def body(acc, params):
                W1e, b1e, W2e, b2e, cwe = params
                h = jax.nn.relu(xf @ W1e + b1e)
                y = h @ W2e + b2e
                return (acc + cwe[:, None] * y, None)
            out, _ = jax.lax.scan(body, jnp.zeros_like(xf), (W1, b1, W2, b2, cw.T))
            return out.reshape(Bx, Tx, Dx)
        return _moe_forward(x, Wr, br, W1, b1, W2, b2)
    edge_index = jnp.stack([src, dst])
    x = x + _L0_gnn_ref(_layernorm(x, axis=-1), edge_attr_2, L0_gnn_Wl, L0_gnn_bl, L0_gnn_Wr, L0_gnn_br, L0_gnn_We, L0_gnn_att, L0_gnn_b_out, L0_gnn_gamma, L0_gnn_beta, edge_index)
    x = x + _L0_ffn_ref(_layernorm(x, axis=-1)[None], L0_ffn_router_w, L0_ffn_w_gate, L0_ffn_w_up, L0_ffn_w_down)[0]
    x = x + _L1_gnn_ref(_layernorm(x, axis=-1), edge_index, L1_gnn_W1, L1_gnn_a_src1, L1_gnn_a_dst1, L1_gnn_b1, L1_gnn_W2, L1_gnn_a_src2, L1_gnn_a_dst2, L1_gnn_b2, L1_gnn_Wfc, L1_gnn_bfc)
    x = x + _L1_ffn_ref(_layernorm(x, axis=-1)[None], L1_ffn_Wr, L1_ffn_br, L1_ffn_W1, L1_ffn_b1, L1_ffn_W2, L1_ffn_b2)[0]
    return x

_drawn_inputs = setup_inputs


def setup_inputs(seed=0):
    import zlib

    import numpy as np

    out = dict(_drawn_inputs(seed))
    spreads = {'L0_gnn_bl': (0.0, 0.1),
     'L0_gnn_br': (0.0, 0.453),
     'L0_gnn_b_out': (0.0, 0.1),
     'L0_gnn_gamma': (1.0, 0.2),
     'L0_gnn_beta': (0.0, 0.1),
     'L1_gnn_b1': (0.0, 0.1),
     'L1_gnn_b2': (0.0, 0.1),
     'L1_gnn_bfc': (0.0, 0.1),
     'L1_ffn_br': (0.0, 0.531),
     'L1_ffn_b1': (0.0, 0.8),
     'L1_ffn_b2': (0.0, 0.425)}
    factors = {'edge_attr_2': 3.06,
     'L0_gnn_We': 2.795,
     'L1_gnn_a_dst1': 4.414,
     'L1_gnn_a_src2': 4.58,
     'L1_gnn_a_dst2': 8.0}
    for name, (base, spread) in spreads.items():
        noise = np.random.default_rng([zlib.crc32(name.encode()), seed]).standard_normal(out[name].shape)
        drawn = base * np.exp(spread * noise) if base else spread * noise
        out[name] = jnp.asarray(drawn.astype(out[name].dtype))
    for name, factor in factors.items():
        out[name] = (out[name] * factor).astype(out[name].dtype)
    return out
```

```python
import numpy as np

import concourse.bass as bass
from concourse import mybir
from concourse.alu_op_type import AluOpType as ALU
from contextlib import ExitStack, contextmanager

F32, BF16, I32, U32 = mybir.dt.float32, mybir.dt.bfloat16, mybir.dt.int32, mybir.dt.uint32
ACT = mybir.ActivationFunctionType
AX = mybir.AxisListType

P = 128
N, E, D = 1250, 20000, 512
NT = -(-N // P)
LAST = N - (NT - 1) * P
KC = D // P
EP, EK = 125, 160
SUP = 2 * P
NSUP = (E + NT * (SUP - 1)) // SUP
TILES = 2 * NSUP
COLS = TILES + NT
UN = 8
STEPS = TILES // UN
HALVES = 2 * STEPS
XW = D + 4
H, C = 4, 256
HC = H * C
HW = H * (C + 1)
E0, F0 = 8, 1024
E1, F1 = 8, 256
HB0 = F0 // P
CHUNKS = [(0, 512), (512, 512), (1024, NT * P - 1024)]
BIG = 2.0 ** 100
SLOPE = 0.2
EPS = 1e-5
assert TILES % UN == 0 and KC == 4

IDENT, IOTA, TRI, ONES = 0, P, 2 * P, 3 * P
SUPI, GI, XI, BSEL, QSEL = 4 * P, 4 * P + NSUP, 4 * P + NSUP + NT, 4 * P + NSUP + NT + 8, 4 * P + NSUP + NT + 11
CFW = QSEL + 4


def constants():
    cf = np.zeros((P, CFW), np.float32)
    cf[:, IDENT:IDENT + P] = np.eye(P)
    cf[:, IOTA:IOTA + P] = np.arange(P)
    cf[:, TRI:TRI + P] = np.triu(np.ones((P, P)), 1)
    cf[:, ONES:ONES + P] = 1.0
    cf[:, SUPI:SUPI + NSUP] = np.arange(NSUP)
    cf[:, GI:GI + NT] = np.arange(NT)
    cf[:, XI:XI + 8] = np.arange(8)
    row = np.arange(P)
    for b in range(3):
        cf[:, BSEL + b] = (row % 32 < 18) & (row % 32 % 3 == b)
    for q in range(4):
        cf[:, QSEL + q] = row // 32 == q
    cb = np.zeros((P, 4 * P), np.float32)
    cb[:, 0:P] = np.eye(P)
    cb[:, P:2 * P] = np.eye(P) * BIG
    cb[0, 2 * P:3 * P] = -BIG
    cb[:, 3 * P:] = 1.0
    reset = np.ones((EP, NT, EK), np.float32)
    reset[:, :, 0] = 0.0
    return cf, cb, reset.reshape(EP, NT * EK)


class Steps:

    def __init__(self, engine, sem):
        self.engine, self.sem, self.n, self.loop_at, self.per = engine, sem, 0, None, 0

    def step(self, instruction):
        instruction.then_inc(self.sem, 1)
        self.n += 1

    def settle(self):
        at = self.n if self.loop_at is None else self.loop_at * self.per + self.n
        self.engine.wait_ge(self.sem, at)

    @contextmanager
    def loop(self, i, count, per):
        first = self.n
        self.loop_at, self.per = i, per
        yield
        assert self.n == first + per, (self.n - first, per)
        self.loop_at, self.n = None, first + count * per


def build(nc, a, out, stop=99):
    ctx = ExitStack()
    with ctx:
        def sb(name, shape, dtype=F32):
            return ctx.enter_context(nc.sbuf_tensor(name, shape, dtype))

        def sem(name):
            return ctx.enter_context(nc.semaphore(name))

        def dram(name, shape, dtype=F32):
            return nc.dram_tensor(name, shape, dtype).ap()

        slots_d = dram("slots_d", [P * TILES, 4])
        xl_d = [dram(f"xl_d{k}", [NT * P, XW]) for k in range(3)]
        hx_d = [dram(f"hx_d{k}", [NT * P, HW]) for k in range(2)]
        als_d = [dram(f"als_d{k}", [NT * P, H]) for k in range(2)]

        X = sb("X", [P, NT, D])
        RA = sb("RA", [P, NT * (XW + D)])
        RT = sb("RT", [P, 10 * 1280])
        RW = sb("RW", [P, 8192])
        RO = sb("RO", [P, TILES * P], BF16)
        RB = sb("RB", [P, 4 * 512])
        cf = sb("cf", [P, CFW])
        cb = sb("cb", [P, 4 * P], BF16)
        slots = sb("slots", [P, COLS, 4])
        nidx = sb("nidx", [P, NSUP], I32)
        gneg = sb("gneg", [P, NT, NSUP], BF16)
        idxr = sb("idxr", [P, UN], I32)
        st = sb("st", [P, NT, 6])
        mv = sb("mv", [P, NT, 2])
        std = sb("std", [P, NT])
        rstd = sb("rstd", [P, NT])
        sm = sb("sm", [P, 96])
        mm = sb("mm", [P, NT, H])
        PS = ctx.enter_context(nc.psum_tensor("PS", [P, 8 * 512], F32))

        def bank(b, w=512, k=1):
            return PS[:, b * 512:b * 512 + w]

        xT = RT[:, 0:8 * 1280].rearrange("p (c n) -> p c n", c=8)
        xlx = RA[:, 0:NT * XW].rearrange("p (n d) -> p n d", d=XW)
        hin = RA[:, NT * XW:NT * (XW + D)].rearrange("p (n d) -> p n d", d=D)
        hx = RA[:, 0:NT * HW].rearrange("p (n d) -> p n d", d=HW)
        hx4 = RA[:, 0:NT * HW].rearrange("p (n h c) -> p n h c", h=H, c=C + 1)
        hT = RA[:, 0:8 * 1280].rearrange("p (c n) -> p c n", c=8)
        ring0 = RT[:, 0:UN * XW].rearrange("p (t d) -> p t d", d=XW)
        ring1 = RT[:, 0:UN * HW].rearrange("p (t d) -> p t d", d=HW)
        xr3 = RT[:, 5120:12800].bitcast(BF16).rearrange("p (n a d) -> p n a d", n=NT, a=3)
        Oht = RO
        ident, iota, tri, ones = (cf[:, o:o + P] for o in (IDENT, IOTA, TRI, ONES))
        identb, bigid, negbig, onesb = cb[:, 0:P], cb[:, P:2 * P], cb[:, 2 * P:3 * P], cb[:, 3 * P:]
        ROf = RO[:, :].bitcast(F32)
        at = [0]

        def carve(region, n):
            v = region[:, at[0]:at[0] + n]
            at[0] += n
            return v

        GE = NT * EK
        r_dst, r_src = carve(ROf, EK).bitcast(I32), carve(ROf, EK).bitcast(I32)
        r_ea = carve(ROf, 2 * EK)
        r_gi, r_li = carve(ROf, EK).bitcast(I32), carve(ROf, EK).bitcast(I32)
        r_gf, r_pos, r_row = carve(ROf, EK), carve(ROf, EK), carve(ROf, EK)
        r_posi, r_rowi = carve(ROf, EK).bitcast(I32), carve(ROf, EK).bitcast(I32)
        r_reset, r_oh, r_inc, r_t = (carve(ROf, GE) for _ in range(4))
        r_rec = carve(ROf, 4 * EK)
        r_pad = carve(ROf, 4 * TILES)
        r_cmp = carve(ROf, NSUP * NT)
        scr = carve(ROf, 2 * 8 * 4)
        sci = carve(ROf, 2 * 8).bitcast(I32)
        assert at[0] <= TILES * P // 2
        Wl = RW[:, 0:2048].rearrange("p (c d) -> p c d", c=KC)
        Wr = RW[:, 2048:4096].rearrange("p (c d) -> p c d", c=KC)
        zr = RW[:, 0:1024].rearrange("p (b d) -> p b d", b=2)
        tmp880 = RW[:, 0:NT * NSUP].rearrange("p (n s) -> p n s", n=NT)
        wring = RW[:, 0:1024].rearrange("p (t d) -> p t d", t=UN)
        dgr = RW[:, 1024:2048].rearrange("p (b t d) -> p b t d", b=2, t=4)
        tabs = RW[:, 2048:2560]
        Rt, Wt = tabs[:, 0:COLS], tabs[:, 256:256 + COLS]
        parts0, whole0 = RW[:, 1024:1156].bitcast(BF16), RW[:, 1156:1156 + NSUP]
        bout, gamma, beta = (RW[:, 2560 + 512 * k:3072 + 512 * k] for k in range(3))
        eaT = RW[:, 4096:4096 + TILES // 4 * 64].bitcast(BF16)
        wez = RW[:, 6912:7936].bitcast(BF16).rearrange("p (q d) -> p q d", q=4)
        eaTs = RW[:, 7936:8128].bitcast(BF16)
        epf = RW[:, 0:2816]
        ep = epf.bitcast(BF16).rearrange("p (t c) -> p t c", c=32)
        ohr = RW[:, 2816:3456].bitcast(BF16).rearrange("p (b t d) -> p b t d", b=2, t=5)
        easum = RT[:, 0:NSUP * 32].rearrange("p (s c) -> p s c", c=32)
        werow, werem = RW[:, 0:512], RW[:, 512:1024]
        wep = RW[:, 1024:1792].bitcast(BF16).rearrange("p (b d) -> p b d", b=3)
        wsel = RW[:, 1792:2048].bitcast(BF16)
        bl, br, att = (RB[:, 512 * k:512 * k + 512] for k in range(3))
        we0, we1 = bl, br
        xrf, junk, small = bank(4), bank(5), bank(7)
        xr3f = RT[:, 5120:12800].bitcast(BF16)
        Mx = sb("Mx", [P, H, NSUP])
        Lal = sb("Lal", [P, COLS])
        esp = sb("esp", [P, 12, 32], BF16)
        W1 = RW[:, 0:4 * HC].rearrange("p (c d) -> p c d", c=4)
        W2 = RW[:, 0:8 * HC].rearrange("p (c d) -> p c d", c=8)
        Wfc = RW[:, 0:8 * D].rearrange("p (c d) -> p c d", c=8)
        asv, adv = RB[:, 0:HC], RB[:, HC:2 * HC]
        bfc = RT[:, 11264:11264 + D]
        gb = RT[:, 10240:10240 + HC]
        Et = RW[:, 0:COLS * H].rearrange("p (t h) -> p t h", h=H)
        Ew = RW[:, 768:768 + COLS * H].rearrange("p (t h) -> p t h", h=H)
        wring1 = RW[:, 1536:1536 + UN * H * P].rearrange("p (t h d) -> p t h d", t=UN, h=H)
        dgr1 = RW[:, 5632:6656].rearrange("p (b t d) -> p b t d", b=2, t=4)
        parts1, whole1 = RW[:, 5632:6160].bitcast(BF16), RW[:, 6160:6160 + NSUP * H]
        tmp1 = RW[:, 6656:6656 + NT * NSUP].rearrange("p (n s) -> p n s", n=NT)
        asr = sb("asr", [P, UN, H])
        als, ald = sb("als", [P, NT, H]), sb("ald", [P, NT, H])
        wg = RW[:, 0:4096].rearrange("p (c d) -> p c d", c=KC)
        wu = RW[:, 4096:8192].rearrange("p (c d) -> p c d", c=KC)
        wd = RT[:, 5120:9216].rearrange("p (c d) -> p c d", c=HB0)
        sg = RT[:, 9216:10240].rearrange("p (b d) -> p b d", b=2)
        rw = RB[:, 0:KC * 8].rearrange("p (c e) -> p c e", c=KC)
        brr = RB[:, 32:40]
        b1c = RB[:, 40:40 + E1 * 2]
        lg = RB[:, 64:144].rearrange("p (n e) -> p n e", e=8)
        v8 = RB[:, 144:224].rearrange("p (n e) -> p n e", e=8)
        i8 = RB[:, 224:304].bitcast(U32).rearrange("p (n e) -> p n e", e=8)
        i8f = RB[:, 304:384].rearrange("p (n e) -> p n e", e=8)
        dw = RB[:, 384:384 + 208]
        dwv = dw[:, 0:80].rearrange("p (n e) -> p n e", e=8)
        dw2 = RB[:, 600:680].rearrange("p (n e) -> p n e", e=8)
        b2p = RB[:, 1024:1536]
        cwT = RB[:, 1536:1536 + 2 * P].rearrange("p (b t) -> p b t", b=2)
        we1v = [RW[:, 2048 * u:2048 * u + 1024].rearrange("p (c d) -> p c d", c=KC) for u in range(2)]
        we2v = [RW[:, 2048 * u + 1024:2048 * u + 2048].rearrange("p (c d) -> p c d", c=2) for u in range(2)]

        s_const = sem("s_const")
        s_edges = sem("s_edges")
        s_x = sem("s_x")
        s_padded = sem("s_padded")
        s_padst = sem("s_padst")
        s_tot = sem("s_tot")
        s_pref = sem("s_pref")
        s_route = sem("s_route")
        s_sccopy = sem("s_sccopy")
        s_scat = [sem("s_scat0"), sem("s_scat1")]
        s_slots = sem("s_slots")
        s_var = sem("s_var")
        s_std = sem("s_std")
        s_h = sem("s_h")
        s_tp = sem("s_tp")
        s_tpc = sem("s_tpc")
        s_w = sem("s_w")
        s_w2 = sem("s_w2")
        s_proj = sem("s_proj")
        s_ev = sem("s_ev")
        s_rows = sem("s_rows")
        s_tab = sem("s_tab")
        s_oh = sem("s_oh")
        s_bt = sem("s_bt")
        s_btc = sem("s_btc")
        s_esp = sem("s_esp")
        s_est = sem("s_est")
        s_esc = sem("s_esc")
        s_wez = sem("s_wez")
        s_idx = sem("s_idx")
        s_pass = sem("s_pass")
        s_g = [sem(f"s_g{q}") for q in range(4)]
        s_slotA = sem("s_slotA")
        s_apass = sem("s_apass")
        s_nidx = sem("s_nidx")
        s_z = sem("s_z")
        s_zd = sem("s_zd")
        s_st = sem("s_st")
        s_L = sem("s_L")
        s_dg = sem("s_dg")
        s_mx = sem("s_mx")
        s_mr = sem("s_mr")
        s_m3 = sem("s_m3")
        s_md = sem("s_md")
        s_we = sem("s_we")
        s_ex = sem("s_ex")
        s_ai = sem("s_ai")
        s_wb = sem("s_wb")
        s_pb = sem("s_pb")
        s_ac = sem("s_ac")
        s_ad3 = sem("s_ad3")
        s_adp = sem("s_adp")
        s_h2 = sem("s_h2")
        s_fc = sem("s_fc")
        s_fcd = sem("s_fcd")
        s_rt = sem("s_rt")
        s_re = sem("s_re")
        s_rx = sem("s_rx")
        s_rwl = sem("s_rwl")
        s_dw = sem("s_dw")
        s_wgu = sem("s_wgu")
        s_wdn = sem("s_wdn")
        s_gu = sem("s_gu")
        s_sg = sem("s_sg")
        s_ht = sem("s_ht")
        s_y = sem("s_y")
        s_ya = sem("s_ya")
        s_we1 = [sem("s_we10"), sem("s_we11")]
        s_hu = sem("s_hu")
        s_hd = sem("s_hd")
        s_yy = sem("s_yy")
        s_yd = sem("s_yd")
        s_ct = sem("s_ct")
        s_ctc = sem("s_ctc")
        s_cb = sem("s_cb")
        s_cbd = sem("s_cbd")
        s_dve = sem("s_dve")
        s_out = sem("s_out")

        block = ctx.enter_context(nc.Block())

        def finish(sp):
            sp.wait_ge(s_out, 1)
            sp.dma_start(out[0:(NT - 1) * P, :].rearrange("(n p) d -> p n d", p=P), X[:, 0:NT - 1, :]).then_inc(s_out, 16)
            sp.dma_start(out[(NT - 1) * P:N, :], X[0:LAST, NT - 1, :]).then_inc(s_out, 16)
            sp.wait_ge(s_out, 33)

        @block.sync
        def _(sp):
            sp.dma_start(r_dst[0:EP, :], a["dst"].rearrange("(p k) -> p k", k=EK)).then_inc(s_edges, 16)
            sp.dma_start(r_src[0:EP, :], a["src"].rearrange("(p k) -> p k", k=EK)).then_inc(s_edges, 16)
            sp.dma_start(r_ea[0:EP, :], a["edge_attr_2"].rearrange("(p k) c -> p (k c)", k=EK)).then_inc(s_edges, 16)
            sp.dma_start(r_reset[0:EP, :], a["reset"]).then_inc(s_edges, 16)
            sp.dma_start(cf[:, :], a["cf"]).then_inc(s_const, 16)
            sp.dma_start(cb[:, :], a["cb"]).then_inc(s_const, 16)
            sp.dma_start(X[:, 0:NT - 1, :], a["x"][0:(NT - 1) * P, :].rearrange("(n p) d -> p n d", p=P)).then_inc(s_x, 16)
            sp.wait_ge(s_padded, 1)
            sp.dma_start(X[0:LAST, NT - 1, :], a["x"][(NT - 1) * P:N, :]).then_inc(s_x, 16)
            sp.dma_start(slots_d.rearrange("(p t) c -> p (t c)", p=P), r_pad).then_inc(s_padst, 16)
            for k in range(3):
                if k:
                    sp.wait_ge(s_h, NT * k + NT)
                sp.dma_start(Wl, a["L0_gnn_Wl"][k].rearrange("(c p) d -> p c d", p=P)).then_inc(s_w, 16)
                sp.dma_start(Wr, a["L0_gnn_Wr"][k].rearrange("(c p) d -> p c d", p=P)).then_inc(s_w, 16)
                for to, of in ((bl, "L0_gnn_bl"), (br, "L0_gnn_br"), (att, "L0_gnn_att")):
                    sp.dma_start(to, a[of][k].partition_broadcast(P)).then_inc(s_w, 16)
                if k == 0:
                    for h in range(2):
                        sp.wait_ge(s_scat[h], EK // 2 * 16)
                    sp.dma_start(slots[:, 0:TILES, :].rearrange("p t c -> p (t c)"),
                                 slots_d.rearrange("(p t) c -> p (t c)", p=P)).then_inc(s_slots, 16)
                sp.wait_ge(s_rows, NT * (k + 1))
                sp.dma_start(xl_d[k].rearrange("(n p) d -> p n d", p=P), xlx).then_inc(s_tab, 16)
                sp.wait_ge(s_proj, NT * (k + 1))
                if k == 0:
                    sp.wait_ge(s_esp, 1)
                    sp.wait_ge(s_bt, HALVES + 2)
                sp.wait_ge(s_ev, NT * (k + 1))
                for to, c in ((we0, 0), (we1, 1)):
                    sp.dma_start(to, a["L0_gnn_We"][k, c].partition_broadcast(P)).then_inc(s_w2, 16)
                sp.dma_start(werow, a["we_rows"][k]).then_inc(s_w2, 16)
                for to, of in ((bout, "L0_gnn_b_out"), (gamma, "L0_gnn_gamma"), (beta, "L0_gnn_beta")):
                    sp.dma_start(to, a[of][k].partition_broadcast(P)).then_inc(s_w2, 16)
            if stop <= 3:
                return finish(sp)
            sp.wait_ge(s_h, NT * 4)
            sp.dma_start(rw, a["router0"]).then_inc(s_rwl, 16)

            def expert0(e, again):
                if again:
                    sp.wait_ge(s_gu, e * 24)
                sp.dma_start(wg, a["L0_ffn_w_gate"][bass.ds(e, 1)].rearrange("e (c p) d -> p (e c) d", p=P)).then_inc(s_wgu, 16)
                sp.dma_start(wu, a["L0_ffn_w_up"][bass.ds(e, 1)].rearrange("e (c p) d -> p (e c) d", p=P)).then_inc(s_wgu, 16)
                if again:
                    sp.wait_ge(s_y, e * NT)
                sp.dma_start(wd, a["L0_ffn_w_down"][bass.ds(e, 1)].rearrange("e (c p) d -> p (e c) d", p=P)).then_inc(s_wdn, 16)

            expert0(0, False)
            with sp.Fori(1, E0) as e:
                expert0(e, True)
            if stop <= 4:
                return finish(sp)
            for k in range(2):
                if k == 0:
                    sp.wait_ge(s_y, E0 * NT)
                    sp.wait_ge(s_ya, E0 * NT + 2)
                    sp.dma_start(W1, a["L1_gnn_W1"].rearrange("(c p) d -> p c d", p=P)).then_inc(s_w, 16)
                    sp.dma_start(bfc, a["L1_gnn_bfc"].partition_broadcast(P)).then_inc(s_w, 16)
                else:
                    sp.wait_ge(s_h, NT * 6)
                    sp.dma_start(W2, a["L1_gnn_W2"].rearrange("(c p) d -> p c d", p=P)).then_inc(s_w, 16)
                sp.dma_start(asv, a[f"L1_gnn_a_src{k + 1}"].rearrange("h c -> (h c)").partition_broadcast(P)).then_inc(s_w, 16)
                sp.dma_start(adv, a[f"L1_gnn_a_dst{k + 1}"].rearrange("h c -> (h c)").partition_broadcast(P)).then_inc(s_w, 16)
                sp.dma_start(gb, a[f"L1_gnn_b{k + 1}"].partition_broadcast(P)).then_inc(s_w, 16)
                sp.wait_ge(s_rows, NT * (4 + k))
                sp.dma_start(als_d[k].rearrange("(n p) h -> p n h", p=P), als[:, :, :]).then_inc(s_tab, 16)
                sp.dma_start(hx_d[k].rearrange("(n p) d -> p n d", p=P), hx).then_inc(s_tab, 16)
            sp.wait_ge(s_h, NT * 7)
            sp.dma_start(Wfc, a["L1_gnn_Wfc"].rearrange("(c p) d -> p c d", p=P)).then_inc(s_w, 16)
            if stop <= 5:
                return finish(sp)
            sp.wait_ge(s_fcd, NT)
            sp.dma_start(rw, a["router1"]).then_inc(s_rwl, 16)
            sp.dma_start(brr, a["L1_ffn_br"].partition_broadcast(P)).then_inc(s_rwl, 16)
            sp.dma_start(b1c, a["b1_cols"]).then_inc(s_rwl, 16)
            sp.dma_start(b2p, a["b2_rows"]).then_inc(s_rwl, 16)

            def experts1(i, again):
                for u in range(2):
                    if again:
                        sp.wait_ge(s_yy, i * (2 * NT) + u * NT)
                    sp.dma_start(we1v[u], a["L1_ffn_W1"][bass.ds(i * 2 + u, 1)].rearrange("e (c p) d -> p (e c) d", p=P)).then_inc(s_we1[u], 16)
                    sp.dma_start(we2v[u], a["L1_ffn_W2"][bass.ds(i * 2 + u, 1)].rearrange("e (c p) d -> p (e c) d", p=P)).then_inc(s_we1[u], 16)

            experts1(0, False)
            with sp.Fori(1, E1 // 2) as i:
                experts1(i, True)
            finish(sp)

        @block.gpsimd
        def _(pool):
            pool.wait_ge(s_route, 1)
            pool.wait_ge(s_padst, 16)
            def scatter(i, again):
                for h in range(2):
                    if again:
                        pool.wait_ge(s_scat[h], i * 128)
                    pool.sem_inc(s_pass, 1)
                    pool.tensor_copy(sci[0:EP, 8 * h:8 * h + 8], r_rowi[0:EP, bass.ds(i * 16 + 8 * h, 8)]).then_inc(s_sccopy, 1)
                    pool.tensor_copy(scr[0:EP, 32 * h:32 * h + 32], r_rec[0:EP, bass.ds(i * 64 + 32 * h, 32)]).then_inc(s_sccopy, 1)
                    pool.wait_ge(s_sccopy, i * 4 + 2 * h + 2)
                    pool.sem_inc(s_pass, 1)
                    for j in range(8):
                        pool.indirect_dma_start(
                            slots_d, bass.IndirectOffsetOnAxis(ap=sci[0:EP, 8 * h + j:8 * h + j + 1], axis=0),
                            scr[0:EP, 32 * h + 4 * j:32 * h + 4 * j + 4], None).then_inc(s_scat[h], 16)

            scatter(0, False)
            with pool.Fori(1, EK // 16) as i:
                scatter(i, True)
            pool.sem_inc(s_slotA, 4)
            pool.sem_inc(s_pb, 4)

            def gathers(nth, sums, table, ring):
                with pool.Fori(0, STEPS) as i:
                    for q in range(4):
                        pool.wait_ge(s_pb if sums else s_slotA, i * 4 + NSUP * nth + q + 1)
                        pool.sem_inc(s_pass, 1)
                        src = slots[:, bass.ds(i * UN + 2 * q, 2), 0:1].bitcast(I32)
                        pool.tensor_copy(idxr[:, 2 * q:2 * q + 2], src.rearrange("p t c -> p (t c)")).then_inc(s_idx, 1)
                        pool.wait_ge(s_idx, i * 4 + NSUP * (2 * nth + sums) + q + 1)
                        pool.sem_inc(s_pass, 1)
                        for j in (2 * q, 2 * q + 1):
                            pool.indirect_dma_start(ring[:, j, :], None, table,
                                                    bass.IndirectOffsetOnAxis(ap=idxr[:, j:j + 1], axis=0)).then_inc(s_g[q], 16)

            def diagonals(table, ring, at, heads):
                with pool.Fori(0, STEPS) as i:
                    for h in range(2):
                        for hd in range(heads):
                            k = h * heads + hd
                            pool.wait_ge(s_mx, i * (2 * heads) + at + k + 1)
                            pool.sem_inc(s_pass, 1)
                            col = table(i * UN + 4 * h, hd)
                            pool.tensor_tensor(ring[:, k % 2], ident.unsqueeze(1).to_broadcast([P, 4, P]),
                                               col.to_broadcast([P, 4, P]), ALU.mult).then_inc(s_dg, 1)

            pool.sem_inc(s_mx, 2)
            for k in range(3):
                pool.wait_ge(s_tab, 16 * (k + 1))
                pool.wait_ge(s_proj, NT * (k + 1))
                pool.wait_ge(s_slots, 16)
                pool.wait_ge(s_esp, 1)
                gathers(k, 0, xl_d[k], ring0)
                pool.wait_ge(s_L, k + 1)
                diagonals(lambda t, hd: Rt[:, bass.ds(t, 4)].unsqueeze(2), dgr, HALVES * k, 1)
                gathers(k, 1, xl_d[k], ring0)
            if stop <= 4:
                return
            for k in range(2):
                pool.wait_ge(s_tab, 16 * (4 + 2 * k))
                pool.wait_ge(s_tab, 16 * (5 + 2 * k))
                pool.wait_ge(s_proj, NT * (4 + k))
                gathers(3 + k, 0, als_d[k], asr[:, :, :])
                pool.wait_ge(s_L, 4 + k)
                diagonals(lambda t, hd: Et[:, bass.ds(t, 4), hd:hd + 1], dgr1, HALVES * (3 + H * k), H)
                gathers(3 + k, 1, hx_d[k], ring1)

        @block.scalar
        def _(act):
            def root(k):
                act.wait_ge(s_var, k + 1)
                act.activation(std[:, :], mv[:, :, 1], ACT.Sqrt).then_inc(s_std, 1)

            def keep_transposed(g0, parts):
                for g in range(g0, g0 + parts * NT):
                    n, c = (g - g0) // parts, 4 * ((g - g0) % parts)
                    act.wait_ge(s_tp, g + 1)
                    act.copy(xT[:, c:c + 4, n * P:n * P + P],
                             bank(6 + g % 2).rearrange("p (c t) -> p c t", c=4)).then_inc(s_tpc, 1)

            root(0)
            for k in range(3):
                keep_transposed(NT * k, 1)
                if k == 0:
                    with act.Fori(0, STEPS) as i:
                        for h in range(2):
                            act.wait_ge(s_bt, i * 2 + h + 3)
                            act.sem_inc(s_apass, 1)
                            tb = bank(h, 320).bitcast(BF16)
                            act.copy(Oht[:, bass.ds((i * 2 + h) * 512, 512)], tb[:, 0:512])
                            act.copy(eaT[:, bass.ds((i * 2 + h) * P, P)], tb[:, 512:640])
                            act.copy(RT[:, bass.ds((i * 2 + h) * 64, 64)], bank(2 + h, 64)).then_inc(s_btc, 1)
                    act.wait_ge(s_est, 1)
                    act.copy(eaTs, bank(2, 192).bitcast(BF16)).then_inc(s_esc, 1)
                act.wait_ge(s_we, k + 1)
                act.activation(Wt, Wt, ACT.Exp).then_inc(s_ex, 1)
                root(k + 1)
            if stop <= 3:
                return
            root(4)
            keep_transposed(3 * NT, 1)
            act.wait_ge(s_re, 1)
            act.activation(sm[:, 30:40], sm[:, 20:30], ACT.Exp).then_inc(s_rx, 1)
            with act.Fori(0, E0) as e:
                for b in range(24):
                    w = CHUNKS[b // 8][1]
                    act.wait_ge(s_gu, e * 24 + b + 1)
                    act.wait_ge(s_ht, e * 24 + b + 1)
                    act.activation(sg[:, b % 2, 0:w], bank(2 * (b % 2), w), ACT.Silu).then_inc(s_sg, 1)
            if stop <= 4:
                return
            root(5)
            keep_transposed(4 * NT, 1)
            for k in range(2):
                for n in range(NT):
                    act.wait_ge(s_proj, NT * (3 + k) + n + 1)
                    act.copy(hx4[:, n, :, 0:C], PS[:, 1024 * (n % 2):1024 * (n % 2) + HC].rearrange("p (h c) -> p h c", h=H)).then_inc(s_h2, 1)
                act.wait_ge(s_we, 4 + k)
                act.activation(Ew, Ew, ACT.Exp).then_inc(s_ex, 1)
                keep_transposed(5 * NT + 2 * NT * k, 2)
            if stop <= 5:
                return
            root(6)
            keep_transposed(9 * NT, 1)
            act.wait_ge(s_re, 2)
            act.activation(lg, lg, ACT.Exp).then_inc(s_rx, 1)

        @block.tensor
        def _(pe):
            mmul = nc.tensor.matmul

            def hin_block(n, c):
                return hin[:, n, c * P:c * P + P]

            def hx_block(n, c):
                return hx4[:, n, c // 2, c % 2 * P:c % 2 * P + P]

            def transposed(g0, parts, q, src):
                for g in range(g0, g0 + parts * NT):
                    n, c = (g - g0) // parts, 4 * ((g - g0) % parts)
                    pe.wait_ge(s_h, NT * q + n + 1)
                    if g >= 2:
                        pe.wait_ge(s_tpc, g - 1)
                    for j in range(4):
                        last = nc.tensor.transpose(bank(6 + g % 2)[:, j * P:j * P + P],
                                                   src(n, c + j), ident)
                    last.then_inc(s_tp, 1)

            def at_edges(parts, heads, stride, done):
                with pe.Fori(0, STEPS) as i:
                    for q in range(4):
                        for j in range(2):
                            t = i * UN + 2 * q + j
                            last = mmul(PS[:, bass.ds(t * stride, 3 * heads)], Oht[:, bass.ds(t * P, P)],
                                        parts[:, bass.ds((i * 4 + q) * (3 * heads), 3 * heads)], start=True, stop=True)
                    last.then_inc(done, 1)

            def masked(at, ring, heads):
                with pe.Fori(0, STEPS) as i:
                    for h in range(2):
                        for hd in range(heads):
                            k = h * heads + hd
                            pe.wait_ge(s_mr, i * (2 * heads) + at + k + 1)
                            b = bank(4 + k % 2)
                            mmul(b, bigid, Oht[:, bass.ds((i * 2 + h) * 512, 512)], start=True, stop=False)
                            mmul(b, negbig, onesb.unsqueeze(1).to_broadcast([P, 4, P]), start=False, stop=False)
                            pe.wait_ge(s_dg, i * (2 * heads) + at + k + 1)
                            mmul(b, ones, ring[:, k % 2].rearrange("p t d -> p (t d)"), start=False, stop=True).then_inc(s_mx, 1)

            pe.wait_ge(s_const, 32)
            pe.wait_ge(s_tot, 1)
            mmul(bank(0, NT), tri[0:EP, 0:P], sm[0:EP, 0:NT], start=True, stop=True)
            mmul(bank(1, NT), ones[0:EP, :], sm[0:EP, 0:NT], start=True, stop=True).then_inc(s_pref, 1)
            pe.wait_ge(s_route, 1)
            pe.wait_ge(s_nidx, 1)
            pe.sem_inc(s_mr, 2)
            pe.sem_inc(s_ac, 2)
            for k in range(3):
                transposed(NT * k, 1, k, hin_block)
                pe.wait_ge(s_w, 16 * 5 * (k + 1))
                for n in range(NT):
                    pe.wait_ge(s_tpc, NT * k + n + 1)
                    if n >= 2:
                        pe.wait_ge(s_ev, NT * k + n - 1)
                    for side, w in enumerate((Wl, Wr)):
                        for c in range(KC):
                            last = mmul(bank(2 * (n % 2) + side), xT[:, c, n * P:n * P + P], w[:, c, :],
                                        start=(c == 0), stop=(c == KC - 1))
                    last.then_inc(s_proj, 1)
                if k == 0:
                    pe.wait_ge(s_ev, NT)
                    pe.sem_inc(s_btc, 2)
                    pe.sem_inc(s_bt, 2)
                    with pe.Fori(0, STEPS) as i:
                        for h in range(2):
                            pe.wait_ge(s_oh, i * 2 + h + 1)
                            pe.wait_ge(s_btc, i * 2 + h + 1)
                            tb = bank(h, 320).bitcast(BF16)
                            for j in range(5):
                                nc.tensor.transpose(tb[:, j * P:j * P + P], ohr[:, h, j, :], identb)
                            for q in range(2):
                                for j in range(2):
                                    t = i * UN + 4 * h + 2 * q + j
                                    last = mmul(bank(2 + h)[:, 32 * q:32 * q + 32], ohr[:, h, 2 * q + j, :],
                                                ep[:, bass.ds(t, 1), :].rearrange("p t c -> p (t c)"),
                                                start=(j == 0), stop=(j == 1))
                            last.then_inc(s_bt, 1)
                    pe.wait_ge(s_btc, HALVES + 2)
                    pe.wait_ge(s_esp, 1)
                    for j in range(3):
                        last = nc.tensor.transpose(bank(2, 192).bitcast(BF16)[:, j * P:j * P + P],
                                                   esp[:, 4 * j:4 * j + 4, :].rearrange("p t c -> p (t c)"), identb)
                    last.then_inc(s_est, 1)
                    pe.wait_ge(s_esc, 1)
                pe.wait_ge(s_wez, k + 1)
                pe.wait_ge(s_ev, NT * (k + 1))
                for n in range(NT):
                    if n >= 4:
                        pe.wait_ge(s_zd, COLS * k + n - 3)
                    for b in range(3):
                        mmul(bank(n % 4), identb, xr3[:, n, b, :], start=(b == 0), stop=False)
                    mmul(bank(n % 4), eaTs[:, (n // 4) * P:(n // 4) * P + P], wez[:, n % 4, :],
                         start=False, stop=True).then_inc(s_z, 1)
                pe.wait_ge(s_zd, COLS * k + NT)
                with pe.Fori(0, STEPS) as i:
                    for h in range(2):
                        for q in range(2):
                            n = pe.value_load(nidx[0:1, bass.ds(i * 4 + 2 * h + q, 1)], min_val=0, max_val=NT - 1)
                            for j in range(2):
                                u = 4 * h + 2 * q + j
                                pe.wait_ge(s_zd, i * UN + COLS * k + NT + u - 3)
                                for b in range(3):
                                    mmul(bank(u % 4), Oht[:, bass.ds((i * UN + u) * P, P)],
                                         xr3f[:, bass.ds(n * (3 * D) + b * D, D)], start=(b == 0), stop=False)
                                mmul(bank(u % 4), eaT[:, bass.ds((i * 2 + h) * P, P)], wez[:, u % 4, :],
                                     start=False, stop=True).then_inc(s_z, 1)
                masked(HALVES * k, dgr, 1)
                pe.wait_ge(s_m3, k + 1)
                at_edges(parts0, 1, 4, s_md)
                pe.wait_ge(s_zd, COLS * (k + 1))
                with pe.Fori(0, STEPS) as i:
                    for h in range(2):
                        pe.wait_ge(s_wb, i * 2 + (HALVES + 2) * k + h + 1)
                        for q in range(2):
                            pe.wait_ge(s_g[2 * h + q], i * 32 + 32 * (STEPS * (2 * k + 1) + 1))
                            pe.wait_ge(s_ac, i * 4 + 2 * HALVES * k + 2 * h + q + 1)
                            for j in range(2):
                                u = 4 * h + 2 * q + j
                                mmul(bank(2 * q), wring[:, u, :], ring0[:, u, 0:D], start=(j == 0), stop=(j == 1))
                                last = mmul(bank(2 * q + 1, 2), wring[:, u, :], ring0[:, u, D:D + 2],
                                            start=(j == 0), stop=(j == 1))
                            last.then_inc(s_pb, 1)
            if stop <= 3:
                return
            transposed(3 * NT, 1, 3, hin_block)

            def router(q):
                for n in range(NT):
                    pe.wait_ge(s_tpc, q + n + 1)
                    for c in range(KC):
                        last = mmul(bank(4)[:, 8 * n:8 * n + 8], xT[:, c, n * P:n * P + P], rw[:, c, :],
                                    start=(c == 0), stop=(c == KC - 1))
                last.then_inc(s_rt, 1)

            pe.wait_ge(s_rwl, 16)
            router(3 * NT)
            pe.wait_ge(s_dw, 1)
            pe.sem_inc(s_ht, 2)
            pe.sem_inc(s_ya, 2)
            with pe.Fori(0, E0) as e:
                pe.wait_ge(s_wgu, e * 32 + 32)
                for b in range(24):
                    t0, w = CHUNKS[b // 8]
                    hb = b % 8
                    pe.wait_ge(s_ht, e * 24 + b + 1)
                    for side, wt in enumerate((wg, wu)):
                        for c in range(KC):
                            last = mmul(bank(2 * (b % 2) + side, w), wt[:, c, hb * P:hb * P + P], xT[:, c, t0:t0 + w],
                                        start=(c == 0), stop=(c == KC - 1))
                    last.then_inc(s_gu, 1)
                pe.wait_ge(s_ht, e * 24 + 26)
                pe.wait_ge(s_wdn, e * 16 + 16)
                for n in range(NT):
                    pe.wait_ge(s_ya, e * NT + n + 1)
                    for hb in range(HB0):
                        last = mmul(bank(4 + n % 2), hT[:, hb, n * P:n * P + P], wd[:, hb, :],
                                    start=(hb == 0), stop=(hb == HB0 - 1))
                    last.then_inc(s_y, 1)
            if stop <= 4:
                return
            transposed(4 * NT, 1, 4, hin_block)
            for k in range(2):
                pe.wait_ge(s_w, 16 * (15 + 5 + 4 * k))
                pe.wait_ge(s_tpc, 5 * NT + 2 * NT * k)
                for n in range(NT):
                    if n >= 2:
                        pe.wait_ge(s_h2, NT * k + n - 1)
                    w, kc = (W1, 4) if k == 0 else (W2, 8)
                    for side in range(2):
                        for c in range(kc):
                            last = mmul(bank(2 * (n % 2) + side), xT[:, c, n * P:n * P + P], w[:, c, 512 * side:512 * side + 512],
                                        start=(c == 0), stop=(c == kc - 1))
                    last.then_inc(s_proj, 1)
                pe.wait_ge(s_h2, NT * (k + 1))
                pe.wait_ge(s_ad3, k + 1)
                at_edges(parts1, H, 16, s_adp)
                pe.wait_ge(s_L, 4 + k)
                masked(HALVES * (3 + H * k), dgr1, H)
                pe.wait_ge(s_m3, 4 + k)
                at_edges(parts1, H, 16, s_md)
                pe.wait_ge(s_we, 4 + k)
                with pe.Fori(0, STEPS) as i:
                    for h in range(2):
                        pe.wait_ge(s_wb, i * 2 + (HALVES + 2) * (3 + k) + h + 1)
                        for q in range(2):
                            pe.wait_ge(s_g[2 * h + q], i * 32 + 32 * (STEPS * (7 + 2 * k) + 1))
                            pe.wait_ge(s_ac, i * 4 + 2 * HALVES * (3 + k) + 2 * h + q + 1)
                            for hd in range(H):
                                for j in range(2):
                                    u = 4 * h + 2 * q + j
                                    last = mmul(bank(4 * q + hd, C + 1), wring1[:, u, hd, :],
                                                ring1[:, u, (C + 1) * hd:(C + 1) * hd + C + 1], start=(j == 0), stop=(j == 1))
                            last.then_inc(s_pb, 1)
                transposed(5 * NT + 2 * NT * k, 2, 5 + k, hx_block)
            pe.wait_ge(s_w, 16 * (15 + 10))
            for n in range(NT):
                pe.wait_ge(s_tpc, 7 * NT + 2 * n + 2)
                if n >= 2:
                    pe.wait_ge(s_fcd, n - 1)
                for c in range(8):
                    last = mmul(bank(n % 2), xT[:, c, n * P:n * P + P], Wfc[:, c, :], start=(c == 0), stop=(c == 7))
                last.then_inc(s_fc, 1)
            if stop <= 5:
                return
            transposed(9 * NT, 1, 7, hin_block)
            pe.wait_ge(s_rwl, 16 * 5)
            router(9 * NT)
            pe.wait_ge(s_dw, 2)
            for n in range(NT):
                if n >= 2:
                    pe.wait_ge(s_ctc, n - 1)
                nc.tensor.transpose(bank(6 + n % 2)[:, 0:P], dw[:, 8 * n:8 * n + P], ident).then_inc(s_ct, 1)
                pe.wait_ge(s_ctc, n + 1)
                if n >= 2:
                    pe.wait_ge(s_cbd, n - 1)
                mmul(bank(4 + n % 2), cwT[:, n % 2, :], b2p, start=True, stop=True).then_inc(s_cb, 1)
            pe.wait_ge(s_cbd, NT)
            pe.sem_inc(s_hd, 2)
            pe.sem_inc(s_yd, 2)
            pe.sem_inc(s_yy, NT)
            with pe.Fori(0, E1 // 2) as i:
                for u in range(2):
                    pe.wait_ge(s_we1[u], i * 32 + 32)
                    for b in range(6):
                        t0, w = CHUNKS[b // 2]
                        pe.wait_ge(s_hd, i * 12 + 6 * u + b + 1)
                        for c in range(KC):
                            last = mmul(bank(b % 2, w), we1v[u][:, c, (b % 2) * P:(b % 2) * P + P], xT[:, c, t0:t0 + w],
                                        start=(c == 0), stop=(c == KC - 1))
                        last.then_inc(s_hu, 1)
                    pe.wait_ge(s_hd, i * 12 + 6 * u + 8)
                    for n in range(NT):
                        pe.wait_ge(s_yd, i * (2 * NT) + NT * u + n + 1)
                        for c in range(2):
                            last = mmul(bank(4 + n % 2), hT[:, c, n * P:n * P + P], we2v[u][:, c, :],
                                        start=(c == 0), stop=(c == 1))
                        last.then_inc(s_yy, 1)

        @block.vector
        def _(dve):
            v = nc.vector
            S = Steps(dve, s_dve)
            do, settle = S.step, S.settle

            def norm_stats(src):
                for n in range(NT):
                    do(v.bn_stats(st[:, n, :], src[:, n, :]))
                settle()
                for n in range(NT):
                    do(v.bn_aggr(mv[:, n, :], st[:, n, :]))
                settle()
                v.tensor_scalar(mv[:, :, 1], mv[:, :, 1], EPS, None, ALU.add).then_inc(s_var, 1)

            def root_back(k):
                dve.wait_ge(s_std, k + 1)
                do(v.reciprocal(rstd[:, :], std[:, :]))
                settle()

            def layer_norm(k):
                norm_stats(X)
                root_back(k)
                for n in range(NT):
                    v.tensor_scalar(hin[:, n, :], X[:, n, :], mv[:, n, 0:1], rstd[:, n:n + 1],
                                    ALU.subtract, ALU.mult).then_inc(s_h, 1)

            def split(dst3, src, rest):
                do(v.tensor_copy(dst3[0], src))
                settle()
                do(v.tensor_tensor(rest, src, dst3[0], ALU.subtract))
                settle()
                do(v.tensor_copy(dst3[1], rest))
                settle()
                do(v.tensor_tensor(dst3[2], rest, dst3[1], ALU.subtract))
                settle()

            do(v.memset(sm[:, :], 0.0))
            do(v.memset(r_pad, 0.0))
            do(v.memset(X[96:P, NT - 1, :], 0.0))
            settle()
            v.memset(r_pad.rearrange("p (t c) -> p t c", c=4)[:, :, 1], -1.0).then_inc(s_padded, 1)
            do(v.memset(slots[:, TILES:COLS, :], -1.0))
            dve.wait_ge(s_const, 32)
            dve.wait_ge(s_edges, 64)
            rows = slice(0, EP)
            do(v.tensor_scalar(r_gi[rows], r_dst[rows], 7, None, ALU.arith_shift_right))
            do(v.tensor_scalar(r_li[rows], r_dst[rows], 127, None, ALU.bitwise_and))
            settle()
            do(v.tensor_copy(r_gf[rows], r_gi[rows]))
            rec = r_rec.rearrange("p (k c) -> p k c", c=4)
            do(v.tensor_copy(rec[rows, :, 1], r_li[rows]))
            do(v.tensor_copy(rec[rows, :, 0].bitcast(I32), r_src[rows]))
            do(v.tensor_copy(rec[rows, :, 2:4], r_ea[rows].rearrange("p (k c) -> p k c", c=2)))
            settle()
            oh = r_oh.rearrange("p (g k) -> p g k", g=NT)
            inc = r_inc.rearrange("p (g k) -> p g k", g=NT)
            rt = r_t.rearrange("p (g k) -> p g k", g=NT)
            do(v.tensor_tensor(oh[rows], r_gf[rows].unsqueeze(1).to_broadcast([EP, NT, EK]),
                               cf[rows, GI:GI + NT].unsqueeze(2).to_broadcast([EP, NT, EK]), ALU.is_equal))
            settle()
            do(v.tensor_tensor_scan(r_inc[rows], r_reset[rows], r_oh[rows], 0.0, ALU.mult, ALU.add))
            settle()
            v.tensor_copy(sm[rows, 0:NT], inc[rows, :, EK - 1]).then_inc(s_tot, 1)
            dve.wait_ge(s_pref, 1)
            smi = sm[:, 10:20].bitcast(I32)
            do(v.tensor_scalar(smi, bank(1, NT), float(SUP - 1), None, ALU.add))
            do(v.tensor_copy(sm[:, 50:60], bank(0, NT)))
            settle()
            do(v.tensor_scalar(smi, smi, 8, None, ALU.arith_shift_right))
            settle()
            do(v.tensor_copy(sm[:, 20:30], smi))
            settle()
            do(v.tensor_tensor_scan(sm[:, 30:40], cf[:, ONES:ONES + NT], sm[:, 20:30], 0.0, ALU.mult, ALU.add))
            settle()
            do(v.tensor_tensor(sm[:, 40:50], sm[:, 30:40], sm[:, 20:30], ALU.subtract))
            settle()
            do(v.scalar_tensor_tensor(sm[:, 60:70], sm[:, 40:50], float(SUP), sm[:, 50:60], ALU.mult, ALU.add))
            settle()
            do(v.tensor_tensor(rt[rows], inc[rows], sm[rows, 60:70].unsqueeze(2).to_broadcast([EP, NT, EK]), ALU.add))
            settle()
            do(v.tensor_tensor(rt[rows], rt[rows], oh[rows], ALU.mult))
            settle()
            do(v.tensor_reduce(r_pos[rows], r_t.rearrange("p (g k) -> p k g", g=NT)[rows], AX.X, ALU.add))
            settle()
            do(v.tensor_scalar(r_posi[rows], r_pos[rows], -1.0, None, ALU.add))
            settle()
            do(v.tensor_scalar(r_gi[rows], r_posi[rows], 7, None, ALU.arith_shift_right))
            do(v.tensor_scalar(r_li[rows], r_posi[rows], 127, None, ALU.bitwise_and))
            settle()
            v.scalar_tensor_tensor(r_rowi[rows], r_li[rows], float(TILES), r_gi[rows], ALU.mult, ALU.add).then_inc(s_route, 1)
            cmp = r_cmp.rearrange("p (s g) -> p s g", g=NT)
            do(v.tensor_tensor(cmp, cf[:, SUPI:SUPI + NSUP].unsqueeze(2).to_broadcast([P, NSUP, NT]),
                               sm[:, 30:40].unsqueeze(1).to_broadcast([P, NSUP, NT]), ALU.is_ge))
            settle()
            nf = small[:, 0:NSUP]
            do(v.tensor_reduce(nf, cmp, AX.X, ALU.add))
            settle()
            do(v.tensor_scalar(nf, nf, float(NT - 1), None, ALU.min))
            settle()
            do(v.tensor_copy(nidx[:, :], nf))
            do(v.tensor_tensor(gneg[:, :, :], nf.unsqueeze(1).to_broadcast([P, NT, NSUP]),
                               cf[:, GI:GI + NT].unsqueeze(2).to_broadcast([P, NT, NSUP]), ALU.not_equal))
            settle()
            v.tensor_scalar(gneg[:, :, :], gneg[:, :, :], -BIG, None, ALU.mult).then_inc(s_nidx, 1)

            dve.wait_ge(s_x, 32)
            layer_norm(0)

            def ring_logits(k):
                for n in range(NT):
                    dve.wait_ge(s_z, COLS * k + n + 1)
                    if n >= 2:
                        dve.wait_ge(s_st, COLS * k + n - 1)
                    v.tensor_tensor(zr[:, n % 2, :], bank(n % 4), xlx[:, n, 0:D], ALU.add).then_inc(s_zd, 1)
                    dve.wait_ge(s_zd, COLS * k + n + 1)
                    v.scalar_tensor_tensor(zr[:, n % 2, :], zr[:, n % 2, :], 0.0, att, ALU.max, ALU.mult,
                                           accum_out=Rt[:, TILES + n:TILES + n + 1]).then_inc(s_st, 1)
                dve.wait_ge(s_st, COLS * k + NT)
                with dve.Fori(0, STEPS) as i:
                    for h in range(2):
                        done = i * UN + COLS * k + NT + 4 * h
                        for pair in range(2):
                            dve.wait_ge(s_g[2 * h + pair], i * 32 + 32 * (STEPS * 2 * k + 1))
                            for j in (2 * pair, 2 * pair + 1):
                                u = 4 * h + j
                                dve.wait_ge(s_z, done + j + 1)
                                dve.wait_ge(s_st, done + j - 1)
                                v.tensor_tensor(zr[:, j % 2, :], bank(u % 4), ring0[:, u, 0:D], ALU.add).then_inc(s_zd, 1)
                            for j in (2 * pair, 2 * pair + 1):
                                dve.wait_ge(s_zd, done + j + 1)
                                v.scalar_tensor_tensor(zr[:, j % 2, :], zr[:, j % 2, :], 0.0, att, ALU.max, ALU.mult,
                                                       accum_out=Rt[:, bass.ds(i * UN + 4 * h + j, 1)]).then_inc(s_st, 1)
                            u = 4 * h + 2 * pair
                            v.tensor_copy(Lal[:, bass.ds(i * UN + u, 2)], ring0[:, u:u + 2, D]).then_inc(s_slotA, 1)

            def maxima(at, heads):
                with dve.Fori(0, STEPS) as i:
                    for h in range(2):
                        for hd in range(heads):
                            kk = h * heads + hd
                            dve.wait_ge(s_mx, i * (2 * heads) + at + kk + 3)
                            v.tensor_reduce(Mx[:, hd, bass.ds(i * 4 + 2 * h, 2)],
                                            bank(4 + kk % 2).rearrange("p (s t) -> p s t", s=2), AX.X, ALU.max).then_inc(s_mr, 1)

            def to_supers(tmp, values, parts, whole, heads, done):
                w = whole.rearrange("p (s h) -> p s h", h=heads)
                for hd in range(heads):
                    do(v.tensor_tensor(tmp, values[:, :, hd:hd + 1].to_broadcast([P, NT, NSUP]), gneg[:, :, :], ALU.add))
                    settle()
                    do(v.tensor_reduce(w[:, :, hd], tmp.rearrange("p n s -> p s n"), AX.X, ALU.max))
                    settle()
                of = parts.rearrange("p (s h b) -> p s h b", h=heads, b=3)
                split([of[:, :, :, b] for b in range(3)], w, w)
                v.tensor_copy(sm[:, 0:1], sm[:, 1:2]).then_inc(done, 1)

            def at_edge(heads, stride):
                tiles = PS[:, 0:TILES * stride].rearrange("p (t w) -> p t w", w=stride)[:, :, 0:3 * heads]
                return tiles.rearrange("p t (h b) -> p t h b", b=3)

            def node_maxima(tmp, parts, whole, own, heads):
                for hd in range(heads):
                    do(v.tensor_tensor(tmp, Mx[:, hd, :].unsqueeze(1).to_broadcast([P, NT, NSUP]), gneg[:, :, :], ALU.add))
                    settle()
                    do(v.tensor_reduce(mm[:, :, hd], tmp, AX.X, ALU.max))
                    settle()
                do(v.tensor_tensor(mm[:, :, 0:heads], mm[:, :, 0:heads], own, ALU.max))
                settle()
                to_supers(tmp, mm, parts, whole, heads, s_m3)

            for k in range(3):
                dve.wait_ge(s_w, 16 * 5 * (k + 1))
                do(v.memset(xlx[:, :, D:XW], 1.0))
                settle()
                for n in range(NT):
                    dve.wait_ge(s_proj, NT * k + n + 1)
                    p = 2 * (n % 2)
                    do(v.tensor_tensor(xlx[:, n, 0:D], bank(p), bl, ALU.add))
                    v.tensor_tensor(xrf, bank(p + 1), br, ALU.add).then_inc(s_ev, 1)
                    settle()
                    dve.wait_ge(s_ev, NT * k + n + 1)
                    v.scalar_tensor_tensor(junk, xlx[:, n, 0:D], SLOPE, att, ALU.mult, ALU.mult,
                                           accum_out=xlx[:, n, D:D + 1]).then_inc(s_rows, 1)
                    split([xr3[:, n, b, :] for b in range(3)], xrf, xrf)
                if k == 0:
                    dve.wait_ge(s_slots, 16)
                    dve.wait_ge(s_proj, NT)
                    do(v.memset(ep, 0.0))
                    settle()
                    do(v.memset(ep[:, :, 18], 1.0))
                    attr_parts(v, do, settle, ep, slots[:, 0:TILES, :], Lal[:, 0:TILES], TILES)
                    settle()
                    with dve.Fori(0, STEPS) as i:
                        for h in range(2):
                            dve.wait_ge(s_bt, i * 2 + h + 1)
                            v.tensor_tensor(ohr[:, h, 0:4, :], iota.unsqueeze(1).to_broadcast([P, 4, P]),
                                            slots[:, bass.ds(i * UN + 4 * h, 4), 1:2].to_broadcast([P, 4, P]), ALU.is_equal)
                            v.tensor_copy(ohr[:, h, 4, :], epf.bitcast(BF16)[:, bass.ds((i * 2 + h) * P, P)]).then_inc(s_oh, 1)
                    dve.wait_ge(s_btc, HALVES + 2)
                    for c in range(2):
                        whole = easum[:, :, 9 * c]
                        for b in (3, 6):
                            do(v.tensor_tensor(whole, whole, easum[:, :, 9 * c + b], ALU.add))
                            settle()
                    for c, to in ((18, sm[:, 70:80]), (0, slots[:, TILES:COLS, 2]), (9, slots[:, TILES:COLS, 3])):
                        do(v.scalar_tensor_tensor(tmp880, gneg[:, :, :], 0.0, easum[:, :, c].unsqueeze(1).to_broadcast([P, NT, NSUP]),
                                                  ALU.is_equal, ALU.mult))
                        settle()
                        do(v.tensor_reduce(to, tmp880, AX.X, ALU.add))
                        settle()
                    do(v.tensor_scalar(sm[:, 70:80], sm[:, 70:80], 1.0, None, ALU.max))
                    settle()
                    do(v.reciprocal(sm[:, 80:90], sm[:, 70:80]))
                    settle()
                    for c in range(2):
                        own = slots[:, TILES:COLS, 2 + c]
                        do(v.tensor_tensor(own, own, sm[:, 80:90], ALU.mult))
                    settle()
                    do(v.memset(esp[:, :, :], 0.0))
                    settle()
                    attr_parts(v, do, settle, esp[:, 0:NT, :], slots[:, TILES:COLS, :], Lal[:, 0:NT], NT)
                    v.tensor_copy(sm[:, 0:1], sm[:, 1:2]).then_inc(s_esp, 1)
                dve.wait_ge(s_w2, 96 * (k + 1))
                split([wep[:, b, :] for b in range(3)], werow, werem)
                do(v.tensor_scalar(werem, wep[:, 0, :], cf[:, BSEL:BSEL + 1], None, ALU.mult))
                settle()
                do(v.scalar_tensor_tensor(werem, wep[:, 1, :], cf[:, BSEL + 1:BSEL + 2], werem, ALU.mult, ALU.add))
                settle()
                do(v.scalar_tensor_tensor(wsel, wep[:, 2, :], cf[:, BSEL + 2:BSEL + 3], werem, ALU.mult, ALU.add))
                settle()
                for q in range(4):
                    do(v.tensor_scalar(wez[:, q, :], wsel, cf[:, QSEL + q:QSEL + q + 1], None, ALU.mult))
                for c, w in enumerate((we0, we1)):
                    do(v.scalar_tensor_tensor(junk, w, SLOPE, att, ALU.mult, ALU.mult, accum_out=sm[:, 92 + c:93 + c]))
                    settle()
                v.tensor_copy(Lal[:, TILES:COLS], xlx[:, :, D]).then_inc(s_wez, 1)
                dve.wait_ge(s_wez, k + 1)
                ring_logits(k)
                dve.wait_ge(s_st, COLS * (k + 1))
                dve.wait_ge(s_slotA, NSUP * (k + 1) + 4)
                do(v.scalar_tensor_tensor(Rt, Rt, 1.0 - SLOPE, Lal[:, :], ALU.mult, ALU.add))
                settle()
                do(v.scalar_tensor_tensor(Rt, slots[:, :, 2], sm[:, 92:93], Rt, ALU.mult, ALU.add))
                settle()
                v.scalar_tensor_tensor(Rt, slots[:, :, 3], sm[:, 93:94], Rt, ALU.mult, ALU.add).then_inc(s_L, 1)
                maxima(HALVES * k, 1)
                dve.wait_ge(s_mr, HALVES * (k + 1) + 2)
                dve.wait_ge(s_L, k + 1)
                node_maxima(tmp880, parts0, whole0, Rt[:, TILES:COLS].unsqueeze(2), 1)
                do(v.tensor_tensor(Wt[:, TILES:COLS], Rt[:, TILES:COLS], mm[:, :, 0], ALU.subtract))
                dve.wait_ge(s_md, STEPS * (k + 1))
                do(v.tensor_reduce(Wt[:, 0:TILES].unsqueeze(2), at_edge(1, 4), AX.X, ALU.add))
                settle()
                do(v.tensor_tensor(Wt[:, 0:TILES], Rt[:, 0:TILES], Wt[:, 0:TILES], ALU.subtract))
                settle()
                v.tensor_scalar(Wt, Wt, 0.0, None, ALU.min).then_inc(s_we, 1)
                dve.wait_ge(s_ex, k + 1)
                dve.wait_ge(s_tab, 16 * (k + 1))
                for n in range(NT):
                    do(v.tensor_scalar(xlx[:, n, 0:D + 2], xlx[:, n, 0:D + 2], Wt[:, TILES + n:TILES + n + 1], None, ALU.mult))
                settle()
                base = (HALVES + 2) * k

                def weigh(t, h):
                    for j in range(4):
                        last = v.tensor_scalar(wring[:, 4 * h + j, :], iota, slots[:, bass.ds(t + j, 1), 1:2].rearrange("p t c -> p (t c)"),
                                               Wt[:, bass.ds(t + j, 1)], ALU.is_equal, ALU.mult)
                    last.then_inc(s_wb, 1)

                for h in range(2):
                    weigh(4 * h, h)
                with dve.Fori(0, STEPS) as i:
                    for h in range(2):
                        for q in range(2):
                            s = 2 * h + q
                            n = dve.value_load(nidx[0:1, bass.ds(i * 4 + s, 1)], min_val=0, max_val=NT - 1)
                            sums = RA[:, bass.ds(n * XW, D + 2)]
                            dve.wait_ge(s_pb, i * 4 + 2 * HALVES * k + s + 5)
                            dve.wait_ge(s_ac, i * 4 + 2 * HALVES * k + s + 2)
                            v.tensor_tensor(sums, sums, PS[:, 1024 * q:1024 * q + D + 2], ALU.add).then_inc(s_ac, 1)
                        weigh(i * UN + UN + 4 * h, h)
                dve.wait_ge(s_ac, 2 * HALVES * (k + 1) + 2)
                do(v.tensor_scalar(sm[:, 0:NT], xlx[:, :, D + 1], 1e-16, None, ALU.add))
                settle()
                do(v.reciprocal(sm[:, 10:20], sm[:, 0:NT]))
                settle()
                for n in range(NT):
                    do(v.scalar_tensor_tensor(hin[:, n, :], xlx[:, n, 0:D], sm[:, 10 + n:11 + n], hin[:, n, :], ALU.mult, ALU.add))
                settle()
                for n in range(NT):
                    do(v.tensor_tensor(hin[:, n, :], hin[:, n, :], bout, ALU.add))
                settle()
                norm_stats(hin)
                root_back(k + 1)
                for n in range(NT):
                    do(v.scalar_tensor_tensor(hin[:, n, :], hin[:, n, :], mv[:, n, 0:1], gamma, ALU.subtract, ALU.mult))
                settle()
                for n in range(NT):
                    do(v.scalar_tensor_tensor(hin[:, n, :], hin[:, n, :], rstd[:, n:n + 1], beta, ALU.mult, ALU.add))
                settle()
                if k < 2:
                    for n in range(NT):
                        v.tensor_scalar(hin[:, n, :], hin[:, n, :], 0.0, None, ALU.max).then_inc(s_h, 1)
                else:
                    for n in range(NT):
                        do(v.scalar_tensor_tensor(X[:, n, :], hin[:, n, :], 0.0, X[:, n, :], ALU.max, ALU.add))
                    settle()
            if stop <= 3:
                v.tensor_copy(sm[:, 0:1], sm[:, 1:2]).then_inc(s_out, 1)
                return
            layer_norm(4)

            def two_best(count):
                for n in range(NT):
                    do(v.max(v8[:, n, :], lg[:, n, :]))
                settle()
                for n in range(NT):
                    do(v.max_index(i8[:, n, :], v8[:, n, :], lg[:, n, :]))
                settle()
                do(v.tensor_copy(i8f, i8))
                settle()

            def place(first, second):
                eight = cf[:, XI:XI + 8].unsqueeze(1).to_broadcast([P, NT, 8])
                for to, c, val in ((dwv, 0, first), (dw2, 1, second)):
                    do(v.tensor_tensor(to, eight, i8f[:, :, c:c + 1].to_broadcast([P, NT, 8]), ALU.is_equal))
                    settle()
                    do(v.tensor_tensor(to, to, val.to_broadcast([P, NT, 8]), ALU.mult))
                    settle()
                v.tensor_tensor(dwv, dwv, dw2, ALU.add).then_inc(s_dw, 1)

            dve.wait_ge(s_rt, 1)
            do(v.tensor_copy(lg, bank(4, 80).rearrange("p (n e) -> p n e", e=8)))
            settle()
            two_best(0)
            v.tensor_tensor(sm[:, 20:30], v8[:, :, 1], v8[:, :, 0], ALU.subtract).then_inc(s_re, 1)
            dve.wait_ge(s_rx, 1)
            do(v.tensor_scalar(sm[:, 40:50], sm[:, 30:40], 1.0, None, ALU.add))
            settle()
            do(v.reciprocal(sm[:, 50:60], sm[:, 40:50]))
            settle()
            do(v.tensor_tensor(sm[:, 60:70], sm[:, 50:60], sm[:, 30:40], ALU.mult))
            settle()
            place(sm[:, 50:60].unsqueeze(2), sm[:, 60:70].unsqueeze(2))
            dve.wait_ge(s_dw, 1)
            with dve.Fori(0, E0) as e:
                for b in range(24):
                    t0, w = CHUNKS[b // 8]
                    dve.wait_ge(s_sg, e * 24 + b + 1)
                    v.tensor_tensor(hT[:, b % 8, t0:t0 + w], sg[:, b % 2, 0:w], bank(2 * (b % 2) + 1, w), ALU.mult).then_inc(s_ht, 1)
                for n in range(NT):
                    dve.wait_ge(s_y, e * NT + n + 1)
                    v.scalar_tensor_tensor(X[:, n, :], bank(4 + n % 2), dw[:, bass.ds(e + 8 * n, 1)], X[:, n, :],
                                           ALU.mult, ALU.add).then_inc(s_ya, 1)
            dve.wait_ge(s_ya, E0 * NT + 2)
            if stop <= 4:
                v.tensor_copy(sm[:, 0:1], sm[:, 1:2]).then_inc(s_out, 1)
                return
            layer_norm(5)
            for k in range(2):
                dve.wait_ge(s_w, 16 * (15 + 5 + 4 * k))
                for n in range(NT):
                    dve.wait_ge(s_h2, NT * k + n + 1)
                    if n:
                        dve.wait_ge(s_rows, NT * (3 + k) + n)
                    v.memset(hx4[:, n, :, C:C + 1], 1.0)
                    for hd in range(H):
                        for side, (vec, to) in enumerate(((asv, als), (adv, ald))):
                            last = v.scalar_tensor_tensor(PS[:, 2048 + C * (2 * hd + side):2048 + C * (2 * hd + side + 1)], hx4[:, n, hd, 0:C], 1.0, vec[:, C * hd:C * hd + C],
                                                          ALU.mult, ALU.mult, accum_out=to[:, n, hd:hd + 1])
                    last.then_inc(s_rows, 1)
                dve.wait_ge(s_rows, NT * (4 + k))
                do(v.tensor_tensor(Et[:, TILES:COLS, :], als[:, :, :], ald[:, :, :], ALU.add))
                to_supers(tmp1, ald, parts1, whole1, H, s_ad3)
                with dve.Fori(0, STEPS) as i:
                    for q in range(4):
                        dve.wait_ge(s_g[q], i * 32 + 32 * (STEPS * (6 + 2 * k) + 1))
                        v.tensor_scalar(Et[:, bass.ds(i * UN + 2 * q, 2), :], asr[:, 2 * q:2 * q + 2, :], 0.0, None, ALU.add).then_inc(s_slotA, 1)
                dve.wait_ge(s_slotA, NSUP * (4 + k) + 4)
                dve.wait_ge(s_adp, STEPS * (k + 1))
                do(v.tensor_reduce(Ew[:, 0:TILES, :], at_edge(H, 16), AX.X, ALU.add))
                settle()
                do(v.tensor_tensor(Et[:, 0:TILES, :], Et[:, 0:TILES, :], Ew[:, 0:TILES, :], ALU.add))
                settle()
                dve.wait_ge(s_ad3, k + 1)
                v.scalar_tensor_tensor(Et, Et, SLOPE, Et, ALU.mult, ALU.max).then_inc(s_L, 1)
                maxima(HALVES * (3 + H * k), H)
                dve.wait_ge(s_mr, HALVES * (3 + H * (k + 1)) + 2)
                dve.wait_ge(s_L, 4 + k)
                node_maxima(tmp1, parts1, whole1, Et[:, TILES:COLS, :], H)
                do(v.tensor_tensor(Ew[:, TILES:COLS, :], Et[:, TILES:COLS, :], mm[:, :, :], ALU.subtract))
                dve.wait_ge(s_md, STEPS * (4 + k))
                do(v.tensor_reduce(Ew[:, 0:TILES, :], at_edge(H, 16), AX.X, ALU.add))
                settle()
                do(v.tensor_tensor(Ew[:, 0:TILES, :], Et[:, 0:TILES, :], Ew[:, 0:TILES, :], ALU.subtract))
                settle()
                v.tensor_scalar(Ew, Ew, 0.0, None, ALU.min).then_inc(s_we, 1)
                dve.wait_ge(s_ex, 4 + k)
                dve.wait_ge(s_tab, 16 * (5 + 2 * k))
                for n in range(NT):
                    for hd in range(H):
                        do(v.tensor_scalar(hx4[:, n, hd, :], hx4[:, n, hd, :],
                                           Ew[:, TILES + n, hd:hd + 1], None, ALU.mult))
                settle()

                def weigh1(t, h):
                    for j in range(4):
                        for hd in range(H):
                            last = v.tensor_scalar(wring1[:, 4 * h + j, hd, :], iota,
                                                   slots[:, bass.ds(t + j, 1), 1:2].rearrange("p t c -> p (t c)"),
                                                   Ew[:, bass.ds(t + j, 1), hd:hd + 1].rearrange("p t c -> p (t c)"), ALU.is_equal, ALU.mult)
                    last.then_inc(s_wb, 1)

                for h in range(2):
                    weigh1(4 * h, h)
                with dve.Fori(0, STEPS) as i:
                    for h in range(2):
                        for q in range(2):
                            s = 2 * h + q
                            n = dve.value_load(nidx[0:1, bass.ds(i * 4 + s, 1)], min_val=0, max_val=NT - 1)
                            sums = RA[:, bass.ds(n * HW, HW)].rearrange("p (h c) -> p h c", h=H)
                            dve.wait_ge(s_pb, i * 4 + 2 * HALVES * (3 + k) + s + 5)
                            dve.wait_ge(s_ac, i * 4 + 2 * HALVES * (3 + k) + s + 2)
                            v.tensor_tensor(sums, sums, PS[:, 2048 * q:2048 * q + 2048].rearrange("p (h c) -> p h c", h=H)[:, :, 0:C + 1],
                                            ALU.add).then_inc(s_ac, 1)
                        weigh1(i * UN + UN + 4 * h, h)
                dve.wait_ge(s_ac, 2 * HALVES * (4 + k) + 2)
                do(v.reciprocal(mm[:, :, :], hx4[:, :, :, C]))
                settle()
                for n in range(NT):
                    for hd in range(H):
                        do(v.scalar_tensor_tensor(hx4[:, n, hd, 0:C], hx4[:, n, hd, 0:C], mm[:, n, hd:hd + 1],
                                                  gb[:, C * hd:C * hd + C], ALU.mult, ALU.add))
                settle()
                for n in range(NT):
                    v.tensor_scalar(hx4[:, n, :, 0:C], hx4[:, n, :, 0:C], 0.0, None, ALU.max).then_inc(s_h, 1)
            for n in range(NT):
                dve.wait_ge(s_fc, n + 1)
                do(v.tensor_tensor(X[:, n, :], X[:, n, :], bfc, ALU.add))
                settle()
                v.tensor_tensor(X[:, n, :], X[:, n, :], bank(n % 2), ALU.add).then_inc(s_fcd, 1)
            dve.wait_ge(s_fcd, NT)
            if stop <= 5:
                v.tensor_copy(sm[:, 0:1], sm[:, 1:2]).then_inc(s_out, 1)
                return
            layer_norm(6)
            do(v.memset(dw, 0.0))
            dve.wait_ge(s_rwl, 16 * 5)
            dve.wait_ge(s_rt, 2)
            do(v.tensor_tensor(lg, bank(4, 80).rearrange("p (n e) -> p n e", e=8), brr.unsqueeze(1).to_broadcast([P, NT, 8]), ALU.add))
            settle()
            do(v.tensor_reduce(sm[:, 0:NT], lg, AX.X, ALU.max))
            settle()
            v.tensor_tensor(lg, lg, sm[:, 0:NT].unsqueeze(2).to_broadcast([P, NT, 8]), ALU.subtract).then_inc(s_re, 1)
            dve.wait_ge(s_rx, 2)
            do(v.tensor_reduce(sm[:, 10:20], lg, AX.X, ALU.add))
            settle()
            do(v.reciprocal(sm[:, 20:30], sm[:, 10:20]))
            settle()
            do(v.tensor_tensor(lg, lg, sm[:, 20:30].unsqueeze(2).to_broadcast([P, NT, 8]), ALU.mult))
            settle()
            two_best(1)
            place(v8[:, :, 0:1], v8[:, :, 1:2])
            dve.wait_ge(s_dw, 2)
            for n in range(NT):
                dve.wait_ge(s_ct, n + 1)
                v.tensor_copy(cwT[:, n % 2, :], bank(6 + n % 2, P)).then_inc(s_ctc, 1)
                dve.wait_ge(s_cb, n + 1)
                v.tensor_tensor(X[:, n, :], X[:, n, :], bank(4 + n % 2), ALU.add).then_inc(s_cbd, 1)
            dve.wait_ge(s_cbd, NT)
            with dve.Fori(0, E1 // 2) as i:
                for u in range(2):
                    for b in range(6):
                        t0, w = CHUNKS[b // 2]
                        dve.wait_ge(s_hu, i * 12 + 6 * u + b + 1)
                        v.tensor_scalar(hT[:, b % 2, t0:t0 + w], bank(b % 2, w), b1c[:, bass.ds(i * 4 + 2 * u + b % 2, 1)], 0.0,
                                        ALU.add, ALU.max).then_inc(s_hd, 1)
                    for n in range(NT):
                        dve.wait_ge(s_yy, i * (2 * NT) + NT * u + n + 1 + NT)
                        v.scalar_tensor_tensor(X[:, n, :], bank(4 + n % 2), dw[:, bass.ds(i * 2 + (u + 8 * n), 1)], X[:, n, :],
                                               ALU.mult, ALU.add).then_inc(s_yd, 1)
            dve.wait_ge(s_yd, E1 * NT + 2)
            v.tensor_copy(sm[:, 0:1], sm[:, 1:2]).then_inc(s_out, 1)


def attr_parts(v, do, settle, to, slots, rest, n):
    for c in range(2):
        src = slots[:, :, 2 + c]
        for a in range(3):
            cols = [to[:, :, c * 9 + a * 3 + b] for b in range(3)]
            for col in cols:
                do(v.tensor_copy(col, src))
            settle()
            if a < 2:
                do(v.tensor_tensor(rest, src, cols[0], ALU.subtract))
                settle()
                src = rest


_SHAPED = ("x", "src", "dst", "edge_attr_2", "L0_gnn_Wl", "L0_gnn_bl", "L0_gnn_Wr", "L0_gnn_br", "L0_gnn_We", "L0_gnn_att",
           "L0_gnn_b_out", "L0_gnn_gamma", "L0_gnn_beta", "L0_ffn_w_gate", "L0_ffn_w_up", "L0_ffn_w_down", "L1_gnn_W1",
           "L1_gnn_a_src1", "L1_gnn_a_dst1", "L1_gnn_b1", "L1_gnn_W2", "L1_gnn_a_src2", "L1_gnn_a_dst2", "L1_gnn_b2",
           "L1_gnn_Wfc", "L1_gnn_bfc", "L1_ffn_br", "L1_ffn_W1", "L1_ffn_W2")


def kernel(**inputs):
    import ml_dtypes
    import concourse.bacc as bacc
    from concourse.bass_utils import run_bass_kernel_spmd

    arrays = {k: np.ascontiguousarray(inputs[k]) for k in _SHAPED}
    cf, cb, reset = constants()
    arrays["cf"], arrays["cb"], arrays["reset"] = cf, cb.astype(ml_dtypes.bfloat16), reset
    We = np.asarray(inputs["L0_gnn_We"])
    rows = np.zeros((3, P, D), np.float32)
    for q in range(4):
        for c in range(2):
            rows[:, 32 * q + 9 * c:32 * q + 9 * c + 9] = We[:, c:c + 1]
    arrays["we_rows"] = rows
    inner = lambda w: np.ascontiguousarray(w.reshape(KC, P, 8).transpose(1, 0, 2).reshape(P, KC * 8))
    arrays["router0"] = inner(np.asarray(inputs["L0_ffn_router_w"]).T)
    arrays["router1"] = inner(np.asarray(inputs["L1_ffn_Wr"]))
    b1 = np.asarray(inputs["L1_ffn_b1"])
    arrays["b1_cols"] = np.ascontiguousarray(b1.reshape(E1 * 2, P).T)
    b2 = np.zeros((P, D), np.float32)
    b2[0:E1] = inputs["L1_ffn_b2"]
    arrays["b2_rows"] = b2

    nc = bacc.Bacc("TRN2", target_bir_lowering=False, num_devices=1)
    a = {k: nc.dram_tensor(f"in_{k}", v.shape, mybir.dt.from_np(v.dtype), kind="ExternalInput").ap() for k, v in arrays.items()}
    out = nc.dram_tensor("out", (N, D), F32, kind="ExternalOutput").ap()
    build(nc, a, out)
    r = run_bass_kernel_spmd(nc, [{f"in_{k}": v for k, v in arrays.items()}], core_ids=[0])
    return r.results[0]["out"]
```

```python
import numpy as np

import concourse.bass as bass
from concourse import mybir
from concourse.alu_op_type import AluOpType as ALU
from contextlib import ExitStack, contextmanager

F32, BF16, I32, U32 = mybir.dt.float32, mybir.dt.bfloat16, mybir.dt.int32, mybir.dt.uint32
ACT = mybir.ActivationFunctionType
AX = mybir.AxisListType

P = 128
N, E, D = 1250, 20000, 512
NT = -(-N // P)
LAST = N - (NT - 1) * P
KC = D // P
EP, EK = 125, 160
SUP = 2 * P
NSUP = (E + NT * (SUP - 1)) // SUP
TILES = 2 * NSUP
COLS = TILES + NT
UN = 8
STEPS = TILES // UN
HALVES = 2 * STEPS
XW = D + 4
H, C = 4, 256
HC = H * C
HW = H * (C + 1)
E0, F0 = 8, 1024
E1, F1 = 8, 256
HB0 = F0 // P
SUPS0 = (2 * NT * P + E0 * (SUP - 1)) // SUP
PICKS = 2 * NT
CHUNKS = [(0, 512), (512, 512), (1024, NT * P - 1024)]
BIG = 2.0 ** 100
SLOPE = 0.2
EPS = 1e-5
assert TILES % UN == 0 and KC == 4

AT_ADP, AT_MAX0, AT_MAX1 = 7 * 512, 6 * 512, 7 * 512

IDENT, IOTA, TRI, ONES = 0, P, 2 * P, 3 * P
SUPI, GI, XI, BSEL, QSEL = 4 * P, 4 * P + NSUP, 4 * P + NSUP + NT, 4 * P + NSUP + NT + 8, 4 * P + NSUP + NT + 11
TOK = QSEL + 4
CFW = TOK + NT
SEL = 4 * P
CBW = SEL + UN * H


def constants():
    cf = np.zeros((P, CFW), np.float32)
    cf[:, IDENT:IDENT + P] = np.eye(P)
    cf[:, IOTA:IOTA + P] = np.arange(P)
    cf[:, TRI:TRI + P] = np.triu(np.ones((P, P)), 1)
    cf[:, ONES:ONES + P] = 1.0
    cf[:, SUPI:SUPI + NSUP] = np.arange(NSUP)
    cf[:, GI:GI + NT] = np.arange(NT)
    cf[:, XI:XI + 8] = np.arange(8)
    row = np.arange(P)
    for b in range(3):
        cf[:, BSEL + b] = (row % 32 < 18) & (row % 32 % 3 == b)
    for q in range(4):
        cf[:, QSEL + q] = row // 32 == q
    cf[:, TOK:TOK + NT] = row[:, None] + P * np.arange(NT)
    cb = np.zeros((P, CBW), np.float32)
    cb[:, 0:P] = np.eye(P)
    cb[:, P:2 * P] = np.eye(P) * BIG
    cb[0, 2 * P:3 * P] = -BIG
    cb[:, 3 * P:4 * P] = 1.0
    for b in range(3):
        cb[b * UN * H + np.arange(UN * H), SEL + np.arange(UN * H)] = 1.0
    reset = np.ones((EP, NT, EK), np.float32)
    reset[:, :, 0] = 0.0
    return cf, cb, reset.reshape(EP, NT * EK)


class Steps:

    def __init__(self, engine, sem):
        self.engine, self.sem, self.n, self.loop_at, self.per = engine, sem, 0, None, 0

    def step(self, instruction):
        instruction.then_inc(self.sem, 1)
        self.n += 1

    def settle(self):
        at = self.n if self.loop_at is None else self.loop_at * self.per + self.n
        self.engine.wait_ge(self.sem, at)

    @contextmanager
    def loop(self, i, count, per):
        first = self.n
        self.loop_at, self.per = i, per
        yield
        assert self.n == first + per, (self.n - first, per)
        self.loop_at, self.n = None, first + count * per


def build(nc, a, out, stop=99):
    ctx = ExitStack()
    with ctx:
        def sb(name, shape, dtype=F32):
            return ctx.enter_context(nc.sbuf_tensor(name, shape, dtype))

        def sem(name):
            return ctx.enter_context(nc.semaphore(name))

        def dram(name, shape, dtype=F32):
            return nc.dram_tensor(name, shape, dtype).ap()

        slots_d = dram("slots_d", [P * TILES, 4])
        xl_d = [dram(f"xl_d{k}", [NT * P, XW]) for k in range(3)]
        hx_d = [dram(f"hx_d{k}", [NT * P, HW]) for k in range(2)]
        als_d = [dram(f"als_d{k}", [NT * P, H]) for k in range(2)]

        h_d = dram("h_d", [NT * P, D])
        tok_d = dram("tok_d", [P * 2 * SUPS0, 1], I32)
        y_d = dram("y_d", [SUPS0 * SUP, D])

        X = sb("X", [P, NT, D])
        RA = sb("RA", [P, NT * (XW + D)])
        RT = sb("RT", [P, 10 * 1280])
        RW = sb("RW", [P, 8192])
        RO = sb("RO", [P, TILES * P], BF16)
        RB = sb("RB", [P, 4 * 512])
        cf = sb("cf", [P, CFW])
        cb = sb("cb", [P, CBW], BF16)
        slots = sb("slots", [P, COLS, 4])
        nidx = sb("nidx", [P, NSUP], I32)
        gneg = sb("gneg", [P, NT, NSUP], BF16)
        idxr = sb("idxr", [P, UN], I32)
        st = sb("st", [P, NT, 6])
        mv = sb("mv", [P, NT, 2])
        std = sb("std", [P, NT])
        rstd = sb("rstd", [P, NT])
        sm = sb("sm", [P, 96])
        mm = sb("mm", [P, NT, H])
        PS = ctx.enter_context(nc.psum_tensor("PS", [P, 8 * 512], F32))

        def bank(b, w=512, k=1):
            return PS[:, b * 512:b * 512 + w]

        xT = RT[:, 0:8 * 1280].rearrange("p (c n) -> p c n", c=8)
        xlx = RA[:, 0:NT * XW].rearrange("p (n d) -> p n d", d=XW)
        hin = RA[:, NT * XW:NT * (XW + D)].rearrange("p (n d) -> p n d", d=D)
        hx = RA[:, 0:NT * HW].rearrange("p (n d) -> p n d", d=HW)
        hx4 = RA[:, 0:NT * HW].rearrange("p (n h c) -> p n h c", h=H, c=C + 1)
        hT = RA[:, 0:8 * 1280].rearrange("p (c n) -> p c n", c=8)
        ring0 = RT[:, 0:UN * XW].rearrange("p (t d) -> p t d", d=XW)
        ring1 = RT[:, 0:UN * HW].rearrange("p (t d) -> p t d", d=HW)
        xr3 = RT[:, 5120:12800].bitcast(BF16).rearrange("p (n a d) -> p n a d", n=NT, a=3)
        Oht = RO
        ident, iota, tri, ones = (cf[:, o:o + P] for o in (IDENT, IOTA, TRI, ONES))
        identb, bigid, negbig, onesb = cb[:, 0:P], cb[:, P:2 * P], cb[:, 2 * P:3 * P], cb[:, 3 * P:4 * P]
        ROf = RO[:, :].bitcast(F32)
        at = [0]

        def carve(region, n):
            v = region[:, at[0]:at[0] + n]
            at[0] += n
            return v

        GE = NT * EK
        r_dst, r_src = carve(ROf, EK).bitcast(I32), carve(ROf, EK).bitcast(I32)
        r_ea = carve(ROf, 2 * EK)
        r_gi, r_li = carve(ROf, EK).bitcast(I32), carve(ROf, EK).bitcast(I32)
        r_gf, r_pos, r_row = carve(ROf, EK), carve(ROf, EK), carve(ROf, EK)
        r_posi, r_rowi = carve(ROf, EK).bitcast(I32), carve(ROf, EK).bitcast(I32)
        r_reset, r_oh, r_inc, r_t = (carve(ROf, GE) for _ in range(4))
        r_rec = carve(ROf, 4 * EK)
        r_pad = carve(ROf, 4 * TILES)
        r_cmp = carve(ROf, NSUP * NT)
        scr = carve(ROf, 2 * 8 * 4)
        sci = carve(ROf, 2 * 8).bitcast(I32)
        assert at[0] <= TILES * P // 2
        Wl = RW[:, 0:2048].rearrange("p (c d) -> p c d", c=KC)
        Wr = RW[:, 2048:4096].rearrange("p (c d) -> p c d", c=KC)
        zr = RW[:, 0:1024].rearrange("p (b d) -> p b d", b=2)
        tmp880 = RW[:, 0:NT * NSUP].rearrange("p (n s) -> p n s", n=NT)
        wring = RW[:, 0:1024].rearrange("p (t d) -> p t d", t=UN)
        dgr = RW[:, 1024:2048].rearrange("p (b t d) -> p b t d", b=2, t=4)
        tabs = RW[:, 2048:2560]
        Rt, Wt = tabs[:, 0:COLS], tabs[:, 256:256 + COLS]
        parts0, whole0 = RW[:, 1024:1156].bitcast(BF16), RW[:, 1156:1156 + NSUP]
        bout, gamma, beta = (RW[:, 2560 + 512 * k:3072 + 512 * k] for k in range(3))
        eaT = RW[:, 4096:4096 + TILES // 4 * 64].bitcast(BF16)
        wez = RW[:, 6912:7936].bitcast(BF16).rearrange("p (q d) -> p q d", q=4)
        eaTs = RW[:, 7936:8128].bitcast(BF16)
        epf = RW[:, 0:2816]
        ep = epf.bitcast(BF16).rearrange("p (t c) -> p t c", c=32)
        ohr = RW[:, 2816:3456].bitcast(BF16).rearrange("p (b t d) -> p b t d", b=2, t=5)
        easum = RT[:, 0:NSUP * 32].rearrange("p (s c) -> p s c", c=32)
        werow, werem = RW[:, 0:512], RW[:, 512:1024]
        wep = RW[:, 1024:1792].bitcast(BF16).rearrange("p (b d) -> p b d", b=3)
        wsel = RW[:, 1792:2048].bitcast(BF16)
        bl, br, att = (RB[:, 512 * k:512 * k + 512] for k in range(3))
        we0, we1 = bl, br
        xrf, junk, small = bank(4), bank(5), bank(7)
        xr3f = RT[:, 5120:12800].bitcast(BF16)
        Mx = sb("Mx", [P, H, NSUP])
        Lal = sb("Lal", [P, COLS])
        esp = sb("esp", [P, 12, 32], BF16)
        W1 = RW[:, 0:4 * HC].rearrange("p (c d) -> p c d", c=4)
        W2 = RW[:, 0:8 * HC].rearrange("p (c d) -> p c d", c=8)
        Wfc = RW[:, 0:8 * D].rearrange("p (c d) -> p c d", c=8)
        asv, adv = RB[:, 0:HC], RB[:, HC:2 * HC]
        bfc = RT[:, 11264:11264 + D]
        gb = RT[:, 10240:10240 + HC]
        Et = RW[:, 0:COLS * H].rearrange("p (t h) -> p t h", h=H)
        Ew = RW[:, 768:768 + COLS * H].rearrange("p (t h) -> p t h", h=H)
        wring1 = RW[:, 1536:1536 + UN * H * P].rearrange("p (t h d) -> p t h d", t=UN, h=H)
        lp = RW[:, 6512:6560].bitcast(BF16)
        lpT = RW[:, 6560:6624].bitcast(BF16)
        lrest = RW[:, 6624:6624 + UN * H]
        parts1, whole1 = RW[:, 5632:6160].bitcast(BF16), RW[:, 6160:6160 + NSUP * H]
        tmp1 = RW[:, 6656:6656 + NT * NSUP].rearrange("p (n s) -> p n s", n=NT)
        asr = sb("asr", [P, UN, H])
        als, ald = sb("als", [P, NT, H]), sb("ald", [P, NT, H])
        wg = [r[:, 0:4096].rearrange("p (c d) -> p c d", c=KC) for r in (RW, RA)]
        wu = [r[:, 4096:8192].rearrange("p (c d) -> p c d", c=KC) for r in (RW, RA)]
        wd = [RT[:, 4096 * u:4096 * u + 4096].rearrange("p (c d) -> p c d", c=HB0) for u in range(2)]
        xg = RT[:, 8192:10240].rearrange("p (t d) -> p t d", d=D)
        xgT = RT[:, 10240:12288].rearrange("p (u c t) -> p u c t", u=2, c=KC)
        sg = RT[:, 12288:12800].rearrange("p (b d) -> p b d", b=2)
        hidden = RA[:, 8192:10240].rearrange("p (c t) -> p c t", c=HB0)
        yst = RB[:, 1024:2048].rearrange("p (t d) -> p t d", t=2)
        yg = RA[:, 0:PICKS * D].rearrange("p (k d) -> p k d", d=D)
        picks = RB[:, 384:384 + PICKS]
        place0 = RB[:, 404:404 + PICKS].bitcast(I32)
        row0 = RB[:, 424:424 + PICKS].bitcast(I32)
        pos0 = RB[:, 444:444 + PICKS]
        hi0 = RB[:, 464:464 + PICKS].bitcast(I32)
        lo0 = RB[:, 484:484 + PICKS].bitcast(I32)
        tokid = RB[:, 504:504 + NT].bitcast(I32)
        eidx = RB[:, 520:520 + SUPS0].bitcast(I32)
        tokens = RB[:, 560:560 + 2 * SUPS0].bitcast(I32)
        zeros = RB[:, 600:600 + 2 * SUPS0].bitcast(I32)
        p_oh, p_inc, p_t, p_reset = (RT[:, 8192 + 160 * j:8352 + 160 * j] for j in range(4))
        p_cmp = RT[:, 8832:8832 + SUPS0 * E0]
        rw = RB[:, 0:KC * 8].rearrange("p (c e) -> p c e", c=KC)
        brr = RB[:, 32:40]
        b1c = RB[:, 40:40 + E1 * 2]
        lg = RB[:, 64:144].rearrange("p (n e) -> p n e", e=8)
        v8 = RB[:, 144:224].rearrange("p (n e) -> p n e", e=8)
        i8 = RB[:, 224:304].bitcast(U32).rearrange("p (n e) -> p n e", e=8)
        i8f = RB[:, 304:384].rearrange("p (n e) -> p n e", e=8)
        dw = RB[:, 384:384 + 208]
        dwv = dw[:, 0:80].rearrange("p (n e) -> p n e", e=8)
        dw2 = RB[:, 600:680].rearrange("p (n e) -> p n e", e=8)
        b2p = RB[:, 1024:1536]
        cwT = RB[:, 1536:1536 + 2 * P].rearrange("p (b t) -> p b t", b=2)
        we1v = [RW[:, 2048 * u:2048 * u + 1024].rearrange("p (c d) -> p c d", c=KC) for u in range(2)]
        we2v = [RW[:, 2048 * u + 1024:2048 * u + 2048].rearrange("p (c d) -> p c d", c=2) for u in range(2)]

        s_const = sem("s_const")
        s_edges = sem("s_edges")
        s_x = sem("s_x")
        s_padded = sem("s_padded")
        s_padst = sem("s_padst")
        s_tot = sem("s_tot")
        s_pref = sem("s_pref")
        s_route = sem("s_route")
        s_sccopy = sem("s_sccopy")
        s_scat = [sem("s_scat0"), sem("s_scat1")]
        s_slots = sem("s_slots")
        s_var = sem("s_var")
        s_std = sem("s_std")
        s_h = sem("s_h")
        s_tp = sem("s_tp")
        s_tpc = sem("s_tpc")
        s_w = sem("s_w")
        s_w2 = sem("s_w2")
        s_proj = sem("s_proj")
        s_ev = sem("s_ev")
        s_rows = sem("s_rows")
        s_tab = sem("s_tab")
        s_oh = sem("s_oh")
        s_bt = sem("s_bt")
        s_btc = sem("s_btc")
        s_esp = sem("s_esp")
        s_est = sem("s_est")
        s_esc = sem("s_esc")
        s_wez = sem("s_wez")
        s_idx = sem("s_idx")
        s_pass = sem("s_pass")
        s_g = [sem(f"s_g{q}") for q in range(4)]
        s_slotA = sem("s_slotA")
        s_apass = sem("s_apass")
        s_nidx = sem("s_nidx")
        s_z = sem("s_z")
        s_zd = sem("s_zd")
        s_st = sem("s_st")
        s_L = sem("s_L")
        s_dg = sem("s_dg")
        s_mx = sem("s_mx")
        s_mr = sem("s_mr")
        s_m3 = sem("s_m3")
        s_md = sem("s_md")
        s_we = sem("s_we")
        s_ex = sem("s_ex")
        s_ai = sem("s_ai")
        s_wb = sem("s_wb")
        s_pb = sem("s_pb")
        s_ac = sem("s_ac")
        s_ad3 = sem("s_ad3")
        s_adp = sem("s_adp")
        s_h2 = sem("s_h2")
        s_lp = sem("s_lp")
        s_lt = sem("s_lt")
        s_ltc = sem("s_ltc")
        s_fc = sem("s_fc")
        s_fcd = sem("s_fcd")
        s_rt = sem("s_rt")
        s_re = sem("s_re")
        s_rx = sem("s_rx")
        s_rwl = sem("s_rwl")
        s_dw = sem("s_dw")
        s_hd_d = sem("s_hd_d")
        s_exp = sem("s_exp")
        s_ps = sem("s_ps")
        s_tok = sem("s_tok")
        s_xg = [sem("s_xg0"), sem("s_xg1")]
        s_xt = sem("s_xt")
        s_xc = sem("s_xc")
        s_yst = sem("s_yst")
        s_yg = sem("s_yg")
        s_wgu = [sem("s_wgu0"), sem("s_wgu1")]
        s_wdn = [sem("s_wdn0"), sem("s_wdn1")]
        s_gu = sem("s_gu")
        s_sg = sem("s_sg")
        s_ht = sem("s_ht")
        s_y = sem("s_y")
        s_ya = sem("s_ya")
        s_we1 = [sem("s_we10"), sem("s_we11")]
        s_hu = sem("s_hu")
        s_hd = sem("s_hd")
        s_yy = sem("s_yy")
        s_yd = sem("s_yd")
        s_ct = sem("s_ct")
        s_ctc = sem("s_ctc")
        s_cb = sem("s_cb")
        s_cbd = sem("s_cbd")
        s_dve = sem("s_dve")
        s_out = sem("s_out")

        block = ctx.enter_context(nc.Block())

        def finish(sp):
            sp.wait_ge(s_out, 1)
            sp.dma_start(out[0:(NT - 1) * P, :].rearrange("(n p) d -> p n d", p=P), X[:, 0:NT - 1, :]).then_inc(s_out, 16)
            sp.dma_start(out[(NT - 1) * P:N, :], X[0:LAST, NT - 1, :]).then_inc(s_out, 16)
            sp.wait_ge(s_out, 33)

        @block.sync
        def _(sp):
            sp.dma_start(r_dst[0:EP, :], a["dst"].rearrange("(p k) -> p k", k=EK)).then_inc(s_edges, 16)
            sp.dma_start(r_src[0:EP, :], a["src"].rearrange("(p k) -> p k", k=EK)).then_inc(s_edges, 16)
            sp.dma_start(r_ea[0:EP, :], a["edge_attr_2"].rearrange("(p k) c -> p (k c)", k=EK)).then_inc(s_edges, 16)
            sp.dma_start(r_reset[0:EP, :], a["reset"]).then_inc(s_edges, 16)
            sp.dma_start(cf[:, :], a["cf"]).then_inc(s_const, 16)
            sp.dma_start(cb[:, :], a["cb"]).then_inc(s_const, 16)
            sp.dma_start(X[:, 0:NT - 1, :], a["x"][0:(NT - 1) * P, :].rearrange("(n p) d -> p n d", p=P)).then_inc(s_x, 16)
            sp.wait_ge(s_padded, 1)
            sp.dma_start(X[0:LAST, NT - 1, :], a["x"][(NT - 1) * P:N, :]).then_inc(s_x, 16)
            sp.dma_start(slots_d.rearrange("(p t) c -> p (t c)", p=P), r_pad).then_inc(s_padst, 16)
            for k in range(3):
                if k:
                    sp.wait_ge(s_h, NT * k + NT)
                sp.dma_start(Wl, a["L0_gnn_Wl"][k].rearrange("(c p) d -> p c d", p=P)).then_inc(s_w, 16)
                sp.dma_start(Wr, a["L0_gnn_Wr"][k].rearrange("(c p) d -> p c d", p=P)).then_inc(s_w, 16)
                for to, of in ((bl, "L0_gnn_bl"), (br, "L0_gnn_br"), (att, "L0_gnn_att")):
                    sp.dma_start(to, a[of][k].partition_broadcast(P)).then_inc(s_w, 16)
                if k == 0:
                    for h in range(2):
                        sp.wait_ge(s_scat[h], EK // 2 * 16)
                    sp.dma_start(slots[:, 0:TILES, :].rearrange("p t c -> p (t c)"),
                                 slots_d.rearrange("(p t) c -> p (t c)", p=P)).then_inc(s_slots, 16)
                sp.wait_ge(s_rows, NT * (k + 1))
                sp.dma_start(xl_d[k].rearrange("(n p) d -> p n d", p=P), xlx).then_inc(s_tab, 16)
                sp.wait_ge(s_proj, NT * (k + 1))
                if k == 0:
                    sp.wait_ge(s_esp, 1)
                    sp.wait_ge(s_bt, HALVES + 2)
                sp.wait_ge(s_ev, NT * (k + 1))
                for to, c in ((we0, 0), (we1, 1)):
                    sp.dma_start(to, a["L0_gnn_We"][k, c].partition_broadcast(P)).then_inc(s_w2, 16)
                sp.dma_start(werow, a["we_rows"][k]).then_inc(s_w2, 16)
                for to, of in ((bout, "L0_gnn_b_out"), (gamma, "L0_gnn_gamma"), (beta, "L0_gnn_beta")):
                    sp.dma_start(to, a[of][k].partition_broadcast(P)).then_inc(s_w2, 16)
            if stop <= 3:
                return finish(sp)
            sp.wait_ge(s_h, NT * 4)
            sp.dma_start(rw, a["router0"]).then_inc(s_rwl, 16)
            sp.dma_start(h_d.rearrange("(n p) d -> p n d", p=P), hin).then_inc(s_hd_d, 16)
            sp.wait_ge(s_dw, 1)
            sp.dma_start(tok_d.rearrange("(p t) c -> p (t c)", p=P), zeros).then_inc(s_hd_d, 16)
            sp.sem_inc(s_yst, 16)
            sp.wait_ge(s_exp, 1)
            sp.wait_ge(s_rt, 1)
            sp.wait_ge(s_hd_d, 32)

            def load_gate_up(t, u):
                e = sp.value_load(eidx[0:1, bass.ds(t, 1)], min_val=0, max_val=E0 - 1)
                sp.dma_start(wg[u], a["L0_ffn_w_gate"][bass.ds(e, 1)].rearrange("e (c p) d -> p (e c) d", p=P)).then_inc(s_wgu[u], 16)
                sp.dma_start(wu[u], a["L0_ffn_w_up"][bass.ds(e, 1)].rearrange("e (c p) d -> p (e c) d", p=P)).then_inc(s_wgu[u], 16)
                return e

            def load_down(e, u):
                sp.dma_start(wd[u], a["L0_ffn_w_down"][bass.ds(e, 1)].rearrange("e (c p) d -> p (e c) d", p=P)).then_inc(s_wdn[u], 16)

            def super_tile0(t, u, more):
                if more:
                    sp.wait_ge(s_gu, t * HB0 + HB0)
                    e = load_gate_up(t + 2, u)
                    sp.wait_ge(s_y, t * 2 + 4)
                    load_down(e, u)
                sp.wait_ge(s_ya, t * 2 + 4)
                sp.dma_start(y_d[bass.ds(t * SUP, SUP), :].rearrange("(j p) d -> p j d", p=P), yst).then_inc(s_yst, 16)

            load_down(load_gate_up(0, 0), 0)
            sp.wait_ge(s_ps, 16 * PICKS)
            sp.dma_start(tokens, tok_d.rearrange("(p t) c -> p (t c)", p=P)).then_inc(s_tok, 16)
            load_down(load_gate_up(1, 1), 1)
            with sp.Fori(0, (SUPS0 - 3) // 2) as i:
                for u in range(2):
                    super_tile0(i * 2 + u, u, True)
            for t in range(SUPS0 - 3, SUPS0):
                super_tile0(t, t % 2, t + 2 < SUPS0)
            if stop <= 4:
                return finish(sp)
            for k in range(2):
                if k == 0:
                    sp.wait_ge(s_y, 2 * SUPS0 + 2)
                    sp.dma_start(W1, a["L1_gnn_W1"].rearrange("(c p) d -> p c d", p=P)).then_inc(s_w, 16)
                    sp.dma_start(bfc, a["L1_gnn_bfc"].partition_broadcast(P)).then_inc(s_w, 16)
                else:
                    sp.wait_ge(s_h, NT * 6)
                    sp.dma_start(W2, a["L1_gnn_W2"].rearrange("(c p) d -> p c d", p=P)).then_inc(s_w, 16)
                sp.wait_ge(s_h, NT * 5)
                sp.dma_start(asv, a[f"L1_gnn_a_src{k + 1}"].rearrange("h c -> (h c)").partition_broadcast(P)).then_inc(s_w, 16)
                sp.dma_start(adv, a[f"L1_gnn_a_dst{k + 1}"].rearrange("h c -> (h c)").partition_broadcast(P)).then_inc(s_w, 16)
                sp.dma_start(gb, a[f"L1_gnn_b{k + 1}"].partition_broadcast(P)).then_inc(s_w, 16)
                sp.wait_ge(s_rows, NT * (4 + k))
                sp.dma_start(als_d[k].rearrange("(n p) h -> p n h", p=P), als[:, :, :]).then_inc(s_tab, 16)
                sp.dma_start(hx_d[k].rearrange("(n p) d -> p n d", p=P), hx).then_inc(s_tab, 16)
            sp.wait_ge(s_h, NT * 7)
            sp.dma_start(Wfc, a["L1_gnn_Wfc"].rearrange("(c p) d -> p c d", p=P)).then_inc(s_w, 16)
            if stop <= 5:
                return finish(sp)
            sp.wait_ge(s_fcd, NT)
            sp.dma_start(rw, a["router1"]).then_inc(s_rwl, 16)
            sp.dma_start(brr, a["L1_ffn_br"].partition_broadcast(P)).then_inc(s_rwl, 16)
            sp.dma_start(b1c, a["b1_cols"]).then_inc(s_rwl, 16)
            sp.dma_start(b2p, a["b2_rows"]).then_inc(s_rwl, 16)

            def experts1(i, again):
                for u in range(2):
                    if again:
                        sp.wait_ge(s_yy, i * (2 * NT) + u * NT)
                    sp.dma_start(we1v[u], a["L1_ffn_W1"][bass.ds(i * 2 + u, 1)].rearrange("e (c p) d -> p (e c) d", p=P)).then_inc(s_we1[u], 16)
                    sp.dma_start(we2v[u], a["L1_ffn_W2"][bass.ds(i * 2 + u, 1)].rearrange("e (c p) d -> p (e c) d", p=P)).then_inc(s_we1[u], 16)

            experts1(0, False)
            with sp.Fori(1, E1 // 2) as i:
                experts1(i, True)
            finish(sp)

        @block.gpsimd
        def _(pool):
            pool.wait_ge(s_route, 1)
            pool.wait_ge(s_padst, 16)
            def scatter(i, again):
                for h in range(2):
                    if again:
                        pool.wait_ge(s_scat[h], i * 128)
                    pool.sem_inc(s_pass, 1)
                    pool.tensor_copy(sci[0:EP, 8 * h:8 * h + 8], r_rowi[0:EP, bass.ds(i * 16 + 8 * h, 8)]).then_inc(s_sccopy, 1)
                    pool.tensor_copy(scr[0:EP, 32 * h:32 * h + 32], r_rec[0:EP, bass.ds(i * 64 + 32 * h, 32)]).then_inc(s_sccopy, 1)
                    pool.wait_ge(s_sccopy, i * 4 + 2 * h + 2)
                    pool.sem_inc(s_pass, 1)
                    for j in range(8):
                        pool.indirect_dma_start(
                            slots_d, bass.IndirectOffsetOnAxis(ap=sci[0:EP, 8 * h + j:8 * h + j + 1], axis=0),
                            scr[0:EP, 32 * h + 4 * j:32 * h + 4 * j + 4], None).then_inc(s_scat[h], 16)

            scatter(0, False)
            with pool.Fori(1, EK // 16) as i:
                scatter(i, True)
            pool.sem_inc(s_slotA, 4)
            pool.sem_inc(s_pb, 4)

            def gathers(nth, sums, table, ring):
                with pool.Fori(0, STEPS) as i:
                    for q in range(4):
                        pool.wait_ge(s_pb if sums else s_slotA, i * 4 + NSUP * nth + q + 1)
                        pool.sem_inc(s_pass, 1)
                        src = slots[:, bass.ds(i * UN + 2 * q, 2), 0:1].bitcast(I32)
                        pool.tensor_copy(idxr[:, 2 * q:2 * q + 2], src.rearrange("p t c -> p (t c)")).then_inc(s_idx, 1)
                        pool.wait_ge(s_idx, i * 4 + NSUP * (2 * nth + sums) + SUPS0 * (nth > 2) + q + 1)
                        pool.sem_inc(s_pass, 1)
                        for j in (2 * q, 2 * q + 1):
                            pool.indirect_dma_start(ring[:, j, :], None, table,
                                                    bass.IndirectOffsetOnAxis(ap=idxr[:, j:j + 1], axis=0)).then_inc(s_g[q], 16)

            def diagonals(at):
                with pool.Fori(0, STEPS) as i:
                    for h in range(2):
                        pool.wait_ge(s_mx, i * 2 + at + h + 1)
                        pool.sem_inc(s_pass, 1)
                        pool.tensor_tensor(dgr[:, h], ident.unsqueeze(1).to_broadcast([P, 4, P]),
                                           Rt[:, bass.ds(i * UN + 4 * h, 4)].unsqueeze(2).to_broadcast([P, 4, P]),
                                           ALU.mult).then_inc(s_dg, 1)

            pool.sem_inc(s_mx, 2)
            for k in range(3):
                pool.wait_ge(s_tab, 16 * (k + 1))
                pool.wait_ge(s_proj, NT * (k + 1))
                pool.wait_ge(s_slots, 16)
                pool.wait_ge(s_esp, 1)
                gathers(k, 0, xl_d[k], ring0)
                pool.wait_ge(s_L, k + 1)
                diagonals(HALVES * k)
                gathers(k, 1, xl_d[k], ring0)
            if stop <= 3:
                return
            pool.wait_ge(s_exp, 1)
            pool.wait_ge(s_hd_d, 32)
            for k in range(PICKS):
                pool.indirect_dma_start(tok_d, bass.IndirectOffsetOnAxis(ap=row0[:, k:k + 1], axis=0),
                                        tokid[:, k % NT:k % NT + 1], None).then_inc(s_ps, 16)
            pool.wait_ge(s_tok, 16)

            def tokens_of(t, u):
                pool.wait_ge(s_xt, t + 1)
                pool.sem_inc(s_pass, 1)
                pool.tensor_copy(idxr[:, 2 * u:2 * u + 2], tokens[:, bass.ds(t * 2, 2)]).then_inc(s_idx, 1)
                pool.wait_ge(s_idx, t + 6 * NSUP + 1)
                pool.sem_inc(s_pass, 1)
                for j in (2 * u, 2 * u + 1):
                    pool.indirect_dma_start(xg[:, j, :], None, h_d,
                                            bass.IndirectOffsetOnAxis(ap=idxr[:, j:j + 1], axis=0)).then_inc(s_xg[u], 16)

            with pool.Fori(0, SUPS0 // 2) as i:
                for u in range(2):
                    tokens_of(i * 2 + u, u)
            tokens_of(SUPS0 - 1, 0)
            pool.wait_ge(s_yst, 16 * (SUPS0 + 1))
            for k in range(PICKS):
                pool.indirect_dma_start(yg[:, k, :], None, y_d,
                                        bass.IndirectOffsetOnAxis(ap=place0[:, k:k + 1], axis=0)).then_inc(s_yg, 16)
            if stop <= 4:
                return
            for k in range(2):
                pool.wait_ge(s_tab, 16 * (4 + 2 * k))
                pool.wait_ge(s_tab, 16 * (5 + 2 * k))
                pool.wait_ge(s_proj, NT * (4 + k))
                gathers(3 + k, 0, als_d[k], asr[:, :, :])
                pool.wait_ge(s_slotA, NSUP * (4 + k) + 4)
                gathers(3 + k, 1, hx_d[k], ring1)

        @block.scalar
        def _(act):
            def root(k):
                act.wait_ge(s_var, k + 1)
                act.activation(std[:, :], mv[:, :, 1], ACT.Sqrt).then_inc(s_std, 1)

            def keep_transposed(g0, parts):
                for g in range(g0, g0 + parts * NT):
                    n, c = (g - g0) // parts, 4 * ((g - g0) % parts)
                    act.wait_ge(s_tp, g + 1)
                    act.copy(xT[:, c:c + 4, n * P:n * P + P],
                             bank(6 + g % 2).rearrange("p (c t) -> p c t", c=4)).then_inc(s_tpc, 1)

            def weights(nth, w):
                act.wait_ge(s_we, (STEPS + 1) * nth + 1)
                act.activation(w[:, TILES:COLS, :], w[:, TILES:COLS, :], ACT.Exp).then_inc(s_ex, 1)
                with act.Fori(0, STEPS) as i:
                    act.wait_ge(s_we, i + (STEPS + 1) * nth + 2)
                    act.activation(w[:, bass.ds(i * UN, UN), :], w[:, bass.ds(i * UN, UN), :], ACT.Exp).then_inc(s_ex, 1)

            root(0)
            for k in range(3):
                keep_transposed(NT * k, 1)
                if k == 0:
                    with act.Fori(0, STEPS) as i:
                        for h in range(2):
                            act.wait_ge(s_bt, i * 2 + h + 3)
                            act.sem_inc(s_apass, 1)
                            tb = bank(h, 320).bitcast(BF16)
                            act.copy(Oht[:, bass.ds((i * 2 + h) * 512, 512)], tb[:, 0:512])
                            act.copy(eaT[:, bass.ds((i * 2 + h) * P, P)], tb[:, 512:640])
                            act.copy(RT[:, bass.ds((i * 2 + h) * 64, 64)], bank(2 + h, 64)).then_inc(s_btc, 1)
                    act.wait_ge(s_est, 1)
                    act.copy(eaTs, bank(2, 192).bitcast(BF16)).then_inc(s_esc, 1)
                weights(k, Wt.unsqueeze(2))
                root(k + 1)
            if stop <= 3:
                return
            root(4)
            keep_transposed(3 * NT, 1)
            act.wait_ge(s_re, 1)
            act.activation(sm[:, 30:40], sm[:, 20:30], ACT.Exp).then_inc(s_rx, 1)

            def keep_tokens(t, u):
                act.wait_ge(s_xt, t + 3)
                for j in range(2):
                    act.copy(xgT[:, u, :, j * P:j * P + P], bank(6 + j).rearrange("p (c t) -> p c t", c=KC)).then_inc(s_xc, 1)

            def gates(t):
                for b in range(HB0):
                    act.wait_ge(s_gu, t * HB0 + b + 1)
                    act.wait_ge(s_ht, t * HB0 + b + 1)
                    act.activation(sg[:, b % 2, :], bank(2 * (b % 2), SUP), ACT.Silu).then_inc(s_sg, 1)

            keep_tokens(0, 0)
            with act.Fori(0, SUPS0 // 2) as i:
                for u in range(2):
                    gates(i * 2 + u)
                    keep_tokens(i * 2 + (u + 1), 1 - u)
            gates(SUPS0 - 1)
            if stop <= 4:
                return
            root(5)
            keep_transposed(4 * NT, 1)
            for k in range(2):
                for n in range(NT):
                    act.wait_ge(s_proj, NT * (3 + k) + n + 1)
                    act.copy(hx4[:, n, :, 0:C], PS[:, 1024 * (n % 2):1024 * (n % 2) + HC].rearrange("p (h c) -> p h c", h=H)).then_inc(s_h2, 1)
                with act.Fori(0, STEPS) as i:
                    act.wait_ge(s_lt, i + STEPS * k + 1)
                    act.copy(lpT[0:3 * UN * H, :], bank(6, 64).bitcast(BF16)[0:3 * UN * H, :]).then_inc(s_ltc, 1)
                weights(3 + k, Ew)
                keep_transposed(5 * NT + 2 * NT * k, 2)
            if stop <= 5:
                return
            root(6)
            keep_transposed(9 * NT, 1)
            act.wait_ge(s_re, 2)
            act.activation(lg, lg, ACT.Exp).then_inc(s_rx, 1)

        @block.tensor
        def _(pe):
            mmul = nc.tensor.matmul

            def hin_block(n, c):
                return hin[:, n, c * P:c * P + P]

            def hx_block(n, c):
                return hx4[:, n, c // 2, c % 2 * P:c % 2 * P + P]

            def transposed(g0, parts, q, src):
                for g in range(g0, g0 + parts * NT):
                    n, c = (g - g0) // parts, 4 * ((g - g0) % parts)
                    pe.wait_ge(s_h, NT * q + n + 1)
                    if g >= 2:
                        pe.wait_ge(s_tpc, g - 1)
                    for j in range(4):
                        last = nc.tensor.transpose(bank(6 + g % 2)[:, j * P:j * P + P],
                                                   src(n, c + j), ident)
                    last.then_inc(s_tp, 1)

            def at_edges(i, parts, heads, to, done):
                w = 3 * heads
                for u in range(UN):
                    last = mmul(PS[:, to + u * w:to + u * w + w], Oht[:, bass.ds((i * UN + u) * P, P)],
                                parts[:, bass.ds((i * 4 + u // 2) * w, w)], start=True, stop=True)
                last.then_inc(done, 1)

            def maxima_at(i, nth, parts, heads, to):
                pe.wait_ge(s_we, i + (STEPS + 1) * nth + 1)
                at_edges(i, parts, heads, to, s_md)

            def mask(b, i, h):
                mmul(b, bigid, Oht[:, bass.ds((i * 2 + h) * 512, 512)], start=True, stop=False)
                mmul(b, negbig, onesb.unsqueeze(1).to_broadcast([P, 4, P]), start=False, stop=False)

            def masked_heads(k):
                rows = 3 * UN * H

                def step(i, more):
                    pe.wait_ge(s_lp, i + STEPS * k + 1)
                    nc.tensor.transpose(bank(6, 64).bitcast(BF16)[0:rows, :], lp[:, 0:rows], identb).then_inc(s_lt, 1)
                    if more:
                        at_edges(i + 1, parts1, H, AT_ADP, s_adp)
                    for h in range(2):
                        for hd in range(H):
                            m = h * H + hd
                            pe.wait_ge(s_mr, i * (2 * H) + HALVES * (3 + H * k) + m + 1)
                            b = bank(4 + m % 2)
                            mask(b, i, h)
                            if m == 0:
                                pe.wait_ge(s_ltc, i + STEPS * k + 1)
                            for j in range(4):
                                c = SEL + (4 * h + j) * H + hd
                                last = mmul(b[:, j * P:j * P + P], cb[0:rows, c:c + 1].to_broadcast([rows, P]), lpT[0:rows, :],
                                            start=False, stop=(j == 3))
                            last.then_inc(s_mx, 1)

                at_edges(0, parts1, H, AT_ADP, s_adp)
                with pe.Fori(0, STEPS - 1) as i:
                    step(i, True)
                step(STEPS - 1, False)

            def masked(at):
                with pe.Fori(0, STEPS) as i:
                    for h in range(2):
                        pe.wait_ge(s_mr, i * 2 + at + h + 1)
                        b = bank(4 + h)
                        mask(b, i, h)
                        pe.wait_ge(s_dg, i * 2 + at + h + 1)
                        mmul(b, ones, dgr[:, h].rearrange("p t d -> p (t d)"), start=False, stop=True).then_inc(s_mx, 1)

            pe.wait_ge(s_const, 32)
            pe.wait_ge(s_tot, 1)
            mmul(bank(0, NT), tri[0:EP, 0:P], sm[0:EP, 0:NT], start=True, stop=True)
            mmul(bank(1, NT), ones[0:EP, :], sm[0:EP, 0:NT], start=True, stop=True).then_inc(s_pref, 1)
            pe.wait_ge(s_route, 1)
            pe.wait_ge(s_nidx, 1)
            pe.sem_inc(s_mr, 2)
            pe.sem_inc(s_ac, 2)
            for k in range(3):
                transposed(NT * k, 1, k, hin_block)
                pe.wait_ge(s_w, 16 * 5 * (k + 1))
                for n in range(NT):
                    pe.wait_ge(s_tpc, NT * k + n + 1)
                    if n >= 2:
                        pe.wait_ge(s_ev, NT * k + n - 1)
                    for side, w in enumerate((Wl, Wr)):
                        for c in range(KC):
                            last = mmul(bank(2 * (n % 2) + side), xT[:, c, n * P:n * P + P], w[:, c, :],
                                        start=(c == 0), stop=(c == KC - 1))
                    last.then_inc(s_proj, 1)
                if k == 0:
                    pe.wait_ge(s_ev, NT)
                    pe.sem_inc(s_btc, 2)
                    pe.sem_inc(s_bt, 2)
                    with pe.Fori(0, STEPS) as i:
                        for h in range(2):
                            pe.wait_ge(s_oh, i * 2 + h + 1)
                            pe.wait_ge(s_btc, i * 2 + h + 1)
                            tb = bank(h, 320).bitcast(BF16)
                            for j in range(5):
                                nc.tensor.transpose(tb[:, j * P:j * P + P], ohr[:, h, j, :], identb)
                            for q in range(2):
                                for j in range(2):
                                    t = i * UN + 4 * h + 2 * q + j
                                    last = mmul(bank(2 + h)[:, 32 * q:32 * q + 32], ohr[:, h, 2 * q + j, :],
                                                ep[:, bass.ds(t, 1), :].rearrange("p t c -> p (t c)"),
                                                start=(j == 0), stop=(j == 1))
                            last.then_inc(s_bt, 1)
                    pe.wait_ge(s_btc, HALVES + 2)
                    pe.wait_ge(s_esp, 1)
                    for j in range(3):
                        last = nc.tensor.transpose(bank(2, 192).bitcast(BF16)[:, j * P:j * P + P],
                                                   esp[:, 4 * j:4 * j + 4, :].rearrange("p t c -> p (t c)"), identb)
                    last.then_inc(s_est, 1)
                    pe.wait_ge(s_esc, 1)
                pe.wait_ge(s_wez, k + 1)
                pe.wait_ge(s_ev, NT * (k + 1))
                for n in range(NT):
                    if n >= 4:
                        pe.wait_ge(s_zd, COLS * k + n - 3)
                    for b in range(3):
                        mmul(bank(n % 4), identb, xr3[:, n, b, :], start=(b == 0), stop=False)
                    mmul(bank(n % 4), eaTs[:, (n // 4) * P:(n // 4) * P + P], wez[:, n % 4, :],
                         start=False, stop=True).then_inc(s_z, 1)
                pe.wait_ge(s_zd, COLS * k + NT)
                with pe.Fori(0, STEPS) as i:
                    for h in range(2):
                        for q in range(2):
                            n = pe.value_load(nidx[0:1, bass.ds(i * 4 + 2 * h + q, 1)], min_val=0, max_val=NT - 1)
                            for j in range(2):
                                u = 4 * h + 2 * q + j
                                pe.wait_ge(s_zd, i * UN + COLS * k + NT + u - 3)
                                for b in range(3):
                                    mmul(bank(u % 4), Oht[:, bass.ds((i * UN + u) * P, P)],
                                         xr3f[:, bass.ds(n * (3 * D) + b * D, D)], start=(b == 0), stop=False)
                                mmul(bank(u % 4), eaT[:, bass.ds((i * 2 + h) * P, P)], wez[:, u % 4, :],
                                     start=False, stop=True).then_inc(s_z, 1)
                masked(HALVES * k)
                pe.wait_ge(s_m3, k + 1)
                pe.wait_ge(s_zd, COLS * (k + 1))
                maxima_at(0, k, parts0, 1, AT_MAX0)

                def sums(i, more):
                    if more:
                        maxima_at(i + 1, k, parts0, 1, AT_MAX0)
                    for h in range(2):
                        pe.wait_ge(s_wb, i * 2 + HALVES * k + h + 1)
                        for q in range(2):
                            pe.wait_ge(s_g[2 * h + q], i * 32 + 32 * (STEPS * (2 * k + 1) + 1))
                            pe.wait_ge(s_ac, i * 4 + 2 * HALVES * k + 2 * h + q + 1)
                            for j in range(2):
                                u = 4 * h + 2 * q + j
                                mmul(bank(2 * q), wring[:, u, :], ring0[:, u, 0:D], start=(j == 0), stop=(j == 1))
                                last = mmul(bank(2 * q + 1, 2), wring[:, u, :], ring0[:, u, D:D + 2],
                                            start=(j == 0), stop=(j == 1))
                            last.then_inc(s_pb, 1)

                with pe.Fori(0, STEPS - 1) as i:
                    sums(i, True)
                sums(STEPS - 1, False)
            if stop <= 3:
                return
            transposed(3 * NT, 1, 3, hin_block)

            def router(q):
                for n in range(NT):
                    pe.wait_ge(s_tpc, q + n + 1)
                    for c in range(KC):
                        last = mmul(bank(4)[:, 8 * n:8 * n + 8], xT[:, c, n * P:n * P + P], rw[:, c, :],
                                    start=(c == 0), stop=(c == KC - 1))
                last.then_inc(s_rt, 1)

            pe.wait_ge(s_rwl, 16)
            router(3 * NT)
            pe.wait_ge(s_tot, 2)
            mmul(bank(0, E0), tri, sm[:, 0:E0], start=True, stop=True)
            mmul(bank(1, E0), ones, sm[:, 0:E0], start=True, stop=True).then_inc(s_pref, 1)
            pe.wait_ge(s_exp, 1)
            pe.sem_inc(s_ht, 2)
            pe.sem_inc(s_ya, 2)
            pe.sem_inc(s_xt, 2)
            pe.sem_inc(s_y, 2)

            def transpose_tokens(t, u, fill):
                pe.wait_ge(s_xg[u], fill * 32)
                for j in range(2):
                    for c in range(KC):
                        last = nc.tensor.transpose(bank(6 + j)[:, c * P:c * P + P], xg[:, 2 * u + j, c * P:c * P + P], ident)
                last.then_inc(s_xt, 1)

            def expert(t, u, fill, more):
                pe.wait_ge(s_xc, t * 2 + 2)
                pe.wait_ge(s_wgu[u], fill * 32)
                for b in range(HB0):
                    pe.wait_ge(s_ht, t * HB0 + b + 1)
                    for side, wt in enumerate((wg[u], wu[u])):
                        for c in range(KC):
                            last = mmul(bank(2 * (b % 2) + side, SUP), wt[:, c, b * P:b * P + P], xgT[:, u, c, :],
                                        start=(c == 0), stop=(c == KC - 1))
                    last.then_inc(s_gu, 1)
                if more:
                    transpose_tokens(t + 1, 1 - u, fill + u)
                pe.wait_ge(s_ht, t * HB0 + HB0 + 2)
                pe.wait_ge(s_wdn[u], fill * 16)
                for j in range(2):
                    pe.wait_ge(s_ya, t * 2 + j + 1)
                    for hb in range(HB0):
                        last = mmul(bank(4 + j), hidden[:, hb, j * P:j * P + P], wd[u][:, hb, :],
                                    start=(hb == 0), stop=(hb == HB0 - 1))
                    last.then_inc(s_y, 1)

            transpose_tokens(0, 0, 1)
            with pe.Fori(0, SUPS0 // 2) as i:
                for u in range(2):
                    expert(i * 2 + u, u, i + 1, True)
            expert(SUPS0 - 1, 0, SUPS0 // 2 + 1, False)
            if stop <= 4:
                return
            transposed(4 * NT, 1, 4, hin_block)
            for k in range(2):
                pe.wait_ge(s_w, 16 * (15 + 5 + 4 * k))
                pe.wait_ge(s_tpc, 5 * NT + 2 * NT * k)
                for n in range(NT):
                    if n >= 2:
                        pe.wait_ge(s_h2, NT * k + n - 1)
                    w, kc = (W1, 4) if k == 0 else (W2, 8)
                    for side in range(2):
                        for c in range(kc):
                            last = mmul(bank(2 * (n % 2) + side), xT[:, c, n * P:n * P + P], w[:, c, 512 * side:512 * side + 512],
                                        start=(c == 0), stop=(c == kc - 1))
                    last.then_inc(s_proj, 1)
                pe.wait_ge(s_h2, NT * (k + 1))
                pe.wait_ge(s_ad3, k + 1)
                masked_heads(k)
                pe.wait_ge(s_m3, 4 + k)
                maxima_at(0, 3 + k, parts1, H, AT_MAX1)

                def head_sums(i, more):
                    for h in range(2):
                        pe.wait_ge(s_wb, i * 2 + HALVES * (3 + k) + h + 1)
                        for q in range(2):
                            pe.wait_ge(s_g[2 * h + q], i * 32 + 32 * (STEPS * (7 + 2 * k) + 1))
                            pe.wait_ge(s_ac, i * 4 + 2 * HALVES * (3 + k) + 2 * h + q + 1)
                            ahead = more and h == 0 and q == 1
                            if ahead:
                                maxima_at(i + 1, 3 + k, parts1, H, AT_MAX1)
                            for hd in range(H):
                                if ahead and hd == H - 1:
                                    pe.wait_ge(s_we, i + (STEPS + 1) * (3 + k) + 3)
                                for j in range(2):
                                    u = 4 * h + 2 * q + j
                                    last = mmul(bank(4 * q + hd, C + 1), wring1[:, u, hd, :],
                                                ring1[:, u, (C + 1) * hd:(C + 1) * hd + C + 1], start=(j == 0), stop=(j == 1))
                            last.then_inc(s_pb, 1)

                with pe.Fori(0, STEPS - 1) as i:
                    head_sums(i, True)
                head_sums(STEPS - 1, False)
                transposed(5 * NT + 2 * NT * k, 2, 5 + k, hx_block)
            pe.wait_ge(s_w, 16 * (15 + 10))
            for n in range(NT):
                pe.wait_ge(s_tpc, 7 * NT + 2 * n + 2)
                if n >= 2:
                    pe.wait_ge(s_fcd, n - 1)
                for c in range(8):
                    last = mmul(bank(n % 2), xT[:, c, n * P:n * P + P], Wfc[:, c, :], start=(c == 0), stop=(c == 7))
                last.then_inc(s_fc, 1)
            if stop <= 5:
                return
            transposed(9 * NT, 1, 7, hin_block)
            pe.wait_ge(s_rwl, 16 * 5)
            router(9 * NT)
            pe.wait_ge(s_dw, 2)
            for n in range(NT):
                if n >= 2:
                    pe.wait_ge(s_ctc, n - 1)
                nc.tensor.transpose(bank(6 + n % 2)[:, 0:P], dw[:, 8 * n:8 * n + P], ident).then_inc(s_ct, 1)
                pe.wait_ge(s_ctc, n + 1)
                if n >= 2:
                    pe.wait_ge(s_cbd, n - 1)
                mmul(bank(4 + n % 2), cwT[:, n % 2, :], b2p, start=True, stop=True).then_inc(s_cb, 1)
            pe.wait_ge(s_cbd, NT)
            pe.sem_inc(s_hd, 2)
            pe.sem_inc(s_yd, 2)
            pe.sem_inc(s_yy, NT)
            with pe.Fori(0, E1 // 2) as i:
                for u in range(2):
                    pe.wait_ge(s_we1[u], i * 32 + 32)
                    for b in range(6):
                        t0, w = CHUNKS[b // 2]
                        pe.wait_ge(s_hd, i * 12 + 6 * u + b + 1)
                        for c in range(KC):
                            last = mmul(bank(b % 2, w), we1v[u][:, c, (b % 2) * P:(b % 2) * P + P], xT[:, c, t0:t0 + w],
                                        start=(c == 0), stop=(c == KC - 1))
                        last.then_inc(s_hu, 1)
                    pe.wait_ge(s_hd, i * 12 + 6 * u + 8)
                    for n in range(NT):
                        pe.wait_ge(s_yd, i * (2 * NT) + NT * u + n + 1)
                        for c in range(2):
                            last = mmul(bank(4 + n % 2), hT[:, c, n * P:n * P + P], we2v[u][:, c, :],
                                        start=(c == 0), stop=(c == 1))
                        last.then_inc(s_yy, 1)

        @block.vector
        def _(dve):
            v = nc.vector
            S = Steps(dve, s_dve)
            do, settle = S.step, S.settle

            def norm_stats(src):
                for n in range(NT):
                    do(v.bn_stats(st[:, n, :], src[:, n, :]))
                settle()
                for n in range(NT):
                    do(v.bn_aggr(mv[:, n, :], st[:, n, :]))
                settle()
                v.tensor_scalar(mv[:, :, 1], mv[:, :, 1], EPS, None, ALU.add).then_inc(s_var, 1)

            def root_back(k):
                dve.wait_ge(s_std, k + 1)
                do(v.reciprocal(rstd[:, :], std[:, :]))
                settle()

            def layer_norm(k):
                norm_stats(X)
                root_back(k)
                for n in range(NT):
                    v.tensor_scalar(hin[:, n, :], X[:, n, :], mv[:, n, 0:1], rstd[:, n:n + 1],
                                    ALU.subtract, ALU.mult).then_inc(s_h, 1)

            def split(dst3, src, rest):
                do(v.tensor_copy(dst3[0], src))
                settle()
                do(v.tensor_tensor(rest, src, dst3[0], ALU.subtract))
                settle()
                do(v.tensor_copy(dst3[1], rest))
                settle()
                do(v.tensor_tensor(dst3[2], rest, dst3[1], ALU.subtract))
                settle()

            do(v.memset(sm[:, :], 0.0))
            do(v.memset(r_pad, 0.0))
            do(v.memset(X[96:P, NT - 1, :], 0.0))
            settle()
            v.memset(r_pad.rearrange("p (t c) -> p t c", c=4)[:, :, 1], -1.0).then_inc(s_padded, 1)
            do(v.memset(slots[:, TILES:COLS, :], -1.0))
            dve.wait_ge(s_const, 32)
            dve.wait_ge(s_edges, 64)
            rows = slice(0, EP)
            do(v.tensor_scalar(r_gi[rows], r_dst[rows], 7, None, ALU.arith_shift_right))
            do(v.tensor_scalar(r_li[rows], r_dst[rows], 127, None, ALU.bitwise_and))
            settle()
            do(v.tensor_copy(r_gf[rows], r_gi[rows]))
            rec = r_rec.rearrange("p (k c) -> p k c", c=4)
            do(v.tensor_copy(rec[rows, :, 1], r_li[rows]))
            do(v.tensor_copy(rec[rows, :, 0].bitcast(I32), r_src[rows]))
            do(v.tensor_copy(rec[rows, :, 2:4], r_ea[rows].rearrange("p (k c) -> p k c", c=2)))
            settle()
            oh = r_oh.rearrange("p (g k) -> p g k", g=NT)
            inc = r_inc.rearrange("p (g k) -> p g k", g=NT)
            rt = r_t.rearrange("p (g k) -> p g k", g=NT)
            do(v.tensor_tensor(oh[rows], r_gf[rows].unsqueeze(1).to_broadcast([EP, NT, EK]),
                               cf[rows, GI:GI + NT].unsqueeze(2).to_broadcast([EP, NT, EK]), ALU.is_equal))
            settle()
            do(v.tensor_tensor_scan(r_inc[rows], r_reset[rows], r_oh[rows], 0.0, ALU.mult, ALU.add))
            settle()
            v.tensor_copy(sm[rows, 0:NT], inc[rows, :, EK - 1]).then_inc(s_tot, 1)
            dve.wait_ge(s_pref, 1)
            smi = sm[:, 10:20].bitcast(I32)
            do(v.tensor_scalar(smi, bank(1, NT), float(SUP - 1), None, ALU.add))
            do(v.tensor_copy(sm[:, 50:60], bank(0, NT)))
            settle()
            do(v.tensor_scalar(smi, smi, 8, None, ALU.arith_shift_right))
            settle()
            do(v.tensor_copy(sm[:, 20:30], smi))
            settle()
            do(v.tensor_tensor_scan(sm[:, 30:40], cf[:, ONES:ONES + NT], sm[:, 20:30], 0.0, ALU.mult, ALU.add))
            settle()
            do(v.tensor_tensor(sm[:, 40:50], sm[:, 30:40], sm[:, 20:30], ALU.subtract))
            settle()
            do(v.scalar_tensor_tensor(sm[:, 60:70], sm[:, 40:50], float(SUP), sm[:, 50:60], ALU.mult, ALU.add))
            settle()
            do(v.tensor_tensor(rt[rows], inc[rows], sm[rows, 60:70].unsqueeze(2).to_broadcast([EP, NT, EK]), ALU.add))
            settle()
            do(v.tensor_tensor(rt[rows], rt[rows], oh[rows], ALU.mult))
            settle()
            do(v.tensor_reduce(r_pos[rows], r_t.rearrange("p (g k) -> p k g", g=NT)[rows], AX.X, ALU.add))
            settle()
            do(v.tensor_scalar(r_posi[rows], r_pos[rows], -1.0, None, ALU.add))
            settle()
            do(v.tensor_scalar(r_gi[rows], r_posi[rows], 7, None, ALU.arith_shift_right))
            do(v.tensor_scalar(r_li[rows], r_posi[rows], 127, None, ALU.bitwise_and))
            settle()
            v.scalar_tensor_tensor(r_rowi[rows], r_li[rows], float(TILES), r_gi[rows], ALU.mult, ALU.add).then_inc(s_route, 1)
            cmp = r_cmp.rearrange("p (s g) -> p s g", g=NT)
            do(v.tensor_tensor(cmp, cf[:, SUPI:SUPI + NSUP].unsqueeze(2).to_broadcast([P, NSUP, NT]),
                               sm[:, 30:40].unsqueeze(1).to_broadcast([P, NSUP, NT]), ALU.is_ge))
            settle()
            nf = small[:, 0:NSUP]
            do(v.tensor_reduce(nf, cmp, AX.X, ALU.add))
            settle()
            do(v.tensor_scalar(nf, nf, float(NT - 1), None, ALU.min))
            settle()
            do(v.tensor_copy(nidx[:, :], nf))
            do(v.tensor_tensor(gneg[:, :, :], nf.unsqueeze(1).to_broadcast([P, NT, NSUP]),
                               cf[:, GI:GI + NT].unsqueeze(2).to_broadcast([P, NT, NSUP]), ALU.not_equal))
            settle()
            v.tensor_scalar(gneg[:, :, :], gneg[:, :, :], -BIG, None, ALU.mult).then_inc(s_nidx, 1)

            dve.wait_ge(s_x, 32)
            layer_norm(0)

            def ring_logits(k):
                for n in range(NT):
                    dve.wait_ge(s_z, COLS * k + n + 1)
                    if n >= 2:
                        dve.wait_ge(s_st, COLS * k + n - 1)
                    v.tensor_tensor(zr[:, n % 2, :], bank(n % 4), xlx[:, n, 0:D], ALU.add).then_inc(s_zd, 1)
                    dve.wait_ge(s_zd, COLS * k + n + 1)
                    v.scalar_tensor_tensor(zr[:, n % 2, :], zr[:, n % 2, :], 0.0, att, ALU.max, ALU.mult,
                                           accum_out=Rt[:, TILES + n:TILES + n + 1]).then_inc(s_st, 1)
                dve.wait_ge(s_st, COLS * k + NT)
                with dve.Fori(0, STEPS) as i:
                    for h in range(2):
                        done = i * UN + COLS * k + NT + 4 * h
                        for pair in range(2):
                            dve.wait_ge(s_g[2 * h + pair], i * 32 + 32 * (STEPS * 2 * k + 1))
                            for j in (2 * pair, 2 * pair + 1):
                                u = 4 * h + j
                                dve.wait_ge(s_z, done + j + 1)
                                dve.wait_ge(s_st, done + j - 1)
                                v.tensor_tensor(zr[:, j % 2, :], bank(u % 4), ring0[:, u, 0:D], ALU.add).then_inc(s_zd, 1)
                            for j in (2 * pair, 2 * pair + 1):
                                dve.wait_ge(s_zd, done + j + 1)
                                v.scalar_tensor_tensor(zr[:, j % 2, :], zr[:, j % 2, :], 0.0, att, ALU.max, ALU.mult,
                                                       accum_out=Rt[:, bass.ds(i * UN + 4 * h + j, 1)]).then_inc(s_st, 1)
                            u = 4 * h + 2 * pair
                            v.tensor_copy(Lal[:, bass.ds(i * UN + u, 2)], ring0[:, u:u + 2, D]).then_inc(s_slotA, 1)

            def maxima(i, at, heads):
                for h in range(2):
                    for hd in range(heads):
                        kk = h * heads + hd
                        dve.wait_ge(s_mx, i * (2 * heads) + at + kk + 3)
                        v.tensor_reduce(Mx[:, hd, bass.ds(i * 4 + 2 * h, 2)],
                                        bank(4 + kk % 2).rearrange("p (s t) -> p s t", s=2), AX.X, ALU.max).then_inc(s_mr, 1)

            def to_supers(tmp, values, parts, whole, heads, done):
                w = whole.rearrange("p (s h) -> p s h", h=heads)
                for hd in range(heads):
                    do(v.tensor_tensor(tmp, values[:, :, hd:hd + 1].to_broadcast([P, NT, NSUP]), gneg[:, :, :], ALU.add))
                    settle()
                    do(v.tensor_reduce(w[:, :, hd], tmp.rearrange("p n s -> p s n"), AX.X, ALU.max))
                    settle()
                of = parts.rearrange("p (s h b) -> p s h b", h=heads, b=3)
                split([of[:, :, :, b] for b in range(3)], w, w)
                v.tensor_copy(sm[:, 0:1], sm[:, 1:2]).then_inc(done, 1)

            def at_edge(to, heads):
                return PS[:, to:to + UN * 3 * heads].rearrange("p (t h b) -> p t h b", h=heads, b=3)

            def exponents(i, nth, to, logits, w):
                at = bass.ds(i * UN, UN)
                dve.wait_ge(s_md, i + STEPS * nth + 1)
                do(v.tensor_reduce(w[:, at, :], at_edge(to, w.shape[2]), AX.X, ALU.add))
                settle()
                do(v.tensor_tensor(w[:, at, :], logits[:, at, :], w[:, at, :], ALU.subtract))
                settle()
                v.tensor_scalar(w[:, at, :], w[:, at, :], 0.0, None, ALU.min).then_inc(s_we, 1)

            def node_maxima(tmp, parts, whole, own, heads):
                for hd in range(heads):
                    do(v.tensor_tensor(tmp, Mx[:, hd, :].unsqueeze(1).to_broadcast([P, NT, NSUP]), gneg[:, :, :], ALU.add))
                    settle()
                    do(v.tensor_reduce(mm[:, :, hd], tmp, AX.X, ALU.max))
                    settle()
                do(v.tensor_tensor(mm[:, :, 0:heads], mm[:, :, 0:heads], own, ALU.max))
                settle()
                to_supers(tmp, mm, parts, whole, heads, s_m3)

            for k in range(3):
                dve.wait_ge(s_w, 16 * 5 * (k + 1))
                do(v.memset(xlx[:, :, D:XW], 1.0))
                settle()
                for n in range(NT):
                    dve.wait_ge(s_proj, NT * k + n + 1)
                    p = 2 * (n % 2)
                    do(v.tensor_tensor(xlx[:, n, 0:D], bank(p), bl, ALU.add))
                    v.tensor_tensor(xrf, bank(p + 1), br, ALU.add).then_inc(s_ev, 1)
                    settle()
                    dve.wait_ge(s_ev, NT * k + n + 1)
                    v.scalar_tensor_tensor(junk, xlx[:, n, 0:D], SLOPE, att, ALU.mult, ALU.mult,
                                           accum_out=xlx[:, n, D:D + 1]).then_inc(s_rows, 1)
                    split([xr3[:, n, b, :] for b in range(3)], xrf, xrf)
                if k == 0:
                    dve.wait_ge(s_slots, 16)
                    dve.wait_ge(s_proj, NT)
                    do(v.memset(ep, 0.0))
                    settle()
                    do(v.memset(ep[:, :, 18], 1.0))
                    attr_parts(v, do, settle, ep, slots[:, 0:TILES, :], Lal[:, 0:TILES], TILES)
                    settle()
                    with dve.Fori(0, STEPS) as i:
                        for h in range(2):
                            dve.wait_ge(s_bt, i * 2 + h + 1)
                            v.tensor_tensor(ohr[:, h, 0:4, :], iota.unsqueeze(1).to_broadcast([P, 4, P]),
                                            slots[:, bass.ds(i * UN + 4 * h, 4), 1:2].to_broadcast([P, 4, P]), ALU.is_equal)
                            v.tensor_copy(ohr[:, h, 4, :], epf.bitcast(BF16)[:, bass.ds((i * 2 + h) * P, P)]).then_inc(s_oh, 1)
                    dve.wait_ge(s_btc, HALVES + 2)
                    for c in range(2):
                        whole = easum[:, :, 9 * c]
                        for b in (3, 6):
                            do(v.tensor_tensor(whole, whole, easum[:, :, 9 * c + b], ALU.add))
                            settle()
                    for c, to in ((18, sm[:, 70:80]), (0, slots[:, TILES:COLS, 2]), (9, slots[:, TILES:COLS, 3])):
                        do(v.scalar_tensor_tensor(tmp880, gneg[:, :, :], 0.0, easum[:, :, c].unsqueeze(1).to_broadcast([P, NT, NSUP]),
                                                  ALU.is_equal, ALU.mult))
                        settle()
                        do(v.tensor_reduce(to, tmp880, AX.X, ALU.add))
                        settle()
                    do(v.tensor_scalar(sm[:, 70:80], sm[:, 70:80], 1.0, None, ALU.max))
                    settle()
                    do(v.reciprocal(sm[:, 80:90], sm[:, 70:80]))
                    settle()
                    for c in range(2):
                        own = slots[:, TILES:COLS, 2 + c]
                        do(v.tensor_tensor(own, own, sm[:, 80:90], ALU.mult))
                    settle()
                    do(v.memset(esp[:, :, :], 0.0))
                    settle()
                    attr_parts(v, do, settle, esp[:, 0:NT, :], slots[:, TILES:COLS, :], Lal[:, 0:NT], NT)
                    v.tensor_copy(sm[:, 0:1], sm[:, 1:2]).then_inc(s_esp, 1)
                dve.wait_ge(s_w2, 96 * (k + 1))
                split([wep[:, b, :] for b in range(3)], werow, werem)
                do(v.tensor_scalar(werem, wep[:, 0, :], cf[:, BSEL:BSEL + 1], None, ALU.mult))
                settle()
                do(v.scalar_tensor_tensor(werem, wep[:, 1, :], cf[:, BSEL + 1:BSEL + 2], werem, ALU.mult, ALU.add))
                settle()
                do(v.scalar_tensor_tensor(wsel, wep[:, 2, :], cf[:, BSEL + 2:BSEL + 3], werem, ALU.mult, ALU.add))
                settle()
                for q in range(4):
                    do(v.tensor_scalar(wez[:, q, :], wsel, cf[:, QSEL + q:QSEL + q + 1], None, ALU.mult))
                for c, w in enumerate((we0, we1)):
                    do(v.scalar_tensor_tensor(junk, w, SLOPE, att, ALU.mult, ALU.mult, accum_out=sm[:, 92 + c:93 + c]))
                    settle()
                v.tensor_copy(Lal[:, TILES:COLS], xlx[:, :, D]).then_inc(s_wez, 1)
                dve.wait_ge(s_wez, k + 1)
                ring_logits(k)
                dve.wait_ge(s_st, COLS * (k + 1))
                dve.wait_ge(s_slotA, NSUP * (k + 1) + 4)
                do(v.scalar_tensor_tensor(Rt, Rt, 1.0 - SLOPE, Lal[:, :], ALU.mult, ALU.add))
                settle()
                do(v.scalar_tensor_tensor(Rt, slots[:, :, 2], sm[:, 92:93], Rt, ALU.mult, ALU.add))
                settle()
                v.scalar_tensor_tensor(Rt, slots[:, :, 3], sm[:, 93:94], Rt, ALU.mult, ALU.add).then_inc(s_L, 1)
                with dve.Fori(0, STEPS) as i:
                    maxima(i, HALVES * k, 1)
                dve.wait_ge(s_mr, HALVES * (k + 1) + 2)
                dve.wait_ge(s_L, k + 1)
                node_maxima(tmp880, parts0, whole0, Rt[:, TILES:COLS].unsqueeze(2), 1)
                v.tensor_tensor(Wt[:, TILES:COLS], Rt[:, TILES:COLS], mm[:, :, 0], ALU.subtract).then_inc(s_we, 1)
                R3, W3 = Rt.unsqueeze(2), Wt.unsqueeze(2)
                exponents(0, k, AT_MAX0, R3, W3)
                dve.wait_ge(s_ex, (STEPS + 1) * k + 1)
                dve.wait_ge(s_tab, 16 * (k + 1))
                for n in range(NT):
                    do(v.tensor_scalar(xlx[:, n, 0:D + 2], xlx[:, n, 0:D + 2], Wt[:, TILES + n:TILES + n + 1], None, ALU.mult))
                settle()

                def weigh(i, h):
                    t = i * UN + 4 * h
                    dve.wait_ge(s_ex, i + (STEPS + 1) * k + 2)
                    for j in range(4):
                        last = v.tensor_scalar(wring[:, 4 * h + j, :], iota, slots[:, bass.ds(t + j, 1), 1:2].rearrange("p t c -> p (t c)"),
                                               Wt[:, bass.ds(t + j, 1)], ALU.is_equal, ALU.mult)
                    last.then_inc(s_wb, 1)

                for h in range(2):
                    weigh(0, h)

                def add_sums(i, more):
                    if more:
                        exponents(i + 1, k, AT_MAX0, R3, W3)
                    for h in range(2):
                        for q in range(2):
                            s = 2 * h + q
                            n = dve.value_load(nidx[0:1, bass.ds(i * 4 + s, 1)], min_val=0, max_val=NT - 1)
                            sums = RA[:, bass.ds(n * XW, D + 2)]
                            dve.wait_ge(s_pb, i * 4 + 2 * HALVES * k + s + 5)
                            dve.wait_ge(s_ac, i * 4 + 2 * HALVES * k + s + 2)
                            v.tensor_tensor(sums, sums, PS[:, 1024 * q:1024 * q + D + 2], ALU.add).then_inc(s_ac, 1)
                        if more:
                            weigh(i + 1, h)

                with dve.Fori(0, STEPS - 1) as i, S.loop(i, STEPS - 1, 2):
                    add_sums(i, True)
                add_sums(STEPS - 1, False)
                dve.wait_ge(s_ac, 2 * HALVES * (k + 1) + 2)
                do(v.tensor_scalar(sm[:, 0:NT], xlx[:, :, D + 1], 1e-16, None, ALU.add))
                settle()
                do(v.reciprocal(sm[:, 10:20], sm[:, 0:NT]))
                settle()
                for n in range(NT):
                    do(v.scalar_tensor_tensor(hin[:, n, :], xlx[:, n, 0:D], sm[:, 10 + n:11 + n], hin[:, n, :], ALU.mult, ALU.add))
                settle()
                for n in range(NT):
                    do(v.tensor_tensor(hin[:, n, :], hin[:, n, :], bout, ALU.add))
                settle()
                norm_stats(hin)
                root_back(k + 1)
                for n in range(NT):
                    do(v.scalar_tensor_tensor(hin[:, n, :], hin[:, n, :], mv[:, n, 0:1], gamma, ALU.subtract, ALU.mult))
                settle()
                for n in range(NT):
                    do(v.scalar_tensor_tensor(hin[:, n, :], hin[:, n, :], rstd[:, n:n + 1], beta, ALU.mult, ALU.add))
                settle()
                if k < 2:
                    for n in range(NT):
                        v.tensor_scalar(hin[:, n, :], hin[:, n, :], 0.0, None, ALU.max).then_inc(s_h, 1)
                else:
                    for n in range(NT):
                        do(v.scalar_tensor_tensor(X[:, n, :], hin[:, n, :], 0.0, X[:, n, :], ALU.max, ALU.add))
                    settle()
            if stop <= 3:
                v.tensor_copy(sm[:, 0:1], sm[:, 1:2]).then_inc(s_out, 1)
                return
            layer_norm(4)

            def two_best(count):
                for n in range(NT):
                    do(v.max(v8[:, n, :], lg[:, n, :]))
                settle()
                for n in range(NT):
                    do(v.max_index(i8[:, n, :], v8[:, n, :], lg[:, n, :]))
                settle()
                do(v.tensor_copy(i8f, i8))
                settle()

            def place(first, second):
                eight = cf[:, XI:XI + 8].unsqueeze(1).to_broadcast([P, NT, 8])
                for to, c, val in ((dwv, 0, first), (dw2, 1, second)):
                    do(v.tensor_tensor(to, eight, i8f[:, :, c:c + 1].to_broadcast([P, NT, 8]), ALU.is_equal))
                    settle()
                    do(v.tensor_tensor(to, to, val.to_broadcast([P, NT, 8]), ALU.mult))
                    settle()
                v.tensor_tensor(dwv, dwv, dw2, ALU.add).then_inc(s_dw, 1)

            dve.wait_ge(s_rt, 1)
            do(v.tensor_copy(lg, bank(4, 80).rearrange("p (n e) -> p n e", e=8)))
            settle()
            two_best(0)
            v.tensor_tensor(sm[:, 20:30], v8[:, :, 1], v8[:, :, 0], ALU.subtract).then_inc(s_re, 1)
            dve.wait_ge(s_rx, 1)
            do(v.tensor_scalar(sm[:, 40:50], sm[:, 30:40], 1.0, None, ALU.add))
            settle()
            do(v.reciprocal(sm[:, 50:60], sm[:, 40:50]))
            settle()
            do(v.tensor_tensor(sm[:, 60:70], sm[:, 50:60], sm[:, 30:40], ALU.mult))
            settle()
            do(v.memset(p_reset, 1.0))
            do(v.tensor_copy(tokid, cf[:, TOK:TOK + NT]))
            for c in range(2):
                do(v.tensor_copy(picks[:, c * NT:c * NT + NT], i8f[:, :, c]))
            v.memset(zeros, 0).then_inc(s_dw, 1)
            settle()
            by = lambda r: r.rearrange("p (e k) -> p e k", e=E0)
            do(v.memset(by(p_reset)[:, :, 0:1], 0.0))
            do(v.tensor_tensor(by(p_oh), picks.unsqueeze(1).to_broadcast([P, E0, PICKS]),
                               cf[:, XI:XI + E0].unsqueeze(2).to_broadcast([P, E0, PICKS]), ALU.is_equal))
            settle()
            do(v.tensor_tensor_scan(p_inc, p_reset, p_oh, 0.0, ALU.mult, ALU.add))
            settle()
            v.tensor_copy(sm[:, 0:E0], by(p_inc)[:, :, PICKS - 1]).then_inc(s_tot, 1)
            dve.wait_ge(s_pref, 2)
            padded = sm[:, 10:18].bitcast(I32)
            do(v.tensor_scalar(padded, bank(1, E0), float(SUP - 1), None, ALU.add))
            settle()
            do(v.tensor_scalar(padded, padded, 8, None, ALU.arith_shift_right))
            settle()
            do(v.tensor_copy(sm[:, 20:28], padded))
            settle()
            do(v.tensor_tensor_scan(sm[:, 30:38], cf[:, ONES:ONES + E0], sm[:, 20:28], 0.0, ALU.mult, ALU.add))
            settle()
            do(v.tensor_tensor(sm[:, 40:48], sm[:, 30:38], sm[:, 20:28], ALU.subtract))
            settle()
            do(v.scalar_tensor_tensor(sm[:, 0:E0], sm[:, 40:48], float(SUP), bank(0, E0), ALU.mult, ALU.add))
            settle()
            do(v.tensor_tensor(by(p_t), by(p_inc), sm[:, 0:E0].unsqueeze(2).to_broadcast([P, E0, PICKS]), ALU.add))
            settle()
            do(v.tensor_tensor(p_t, p_t, p_oh, ALU.mult))
            settle()
            do(v.tensor_reduce(pos0, p_t.rearrange("p (e k) -> p k e", e=E0), AX.X, ALU.add))
            settle()
            do(v.tensor_scalar(place0, pos0, -1.0, None, ALU.add))
            settle()
            do(v.tensor_scalar(hi0, place0, 7, None, ALU.arith_shift_right))
            do(v.tensor_scalar(lo0, place0, 127, None, ALU.bitwise_and))
            settle()
            do(v.scalar_tensor_tensor(row0, lo0, float(2 * SUPS0), hi0, ALU.mult, ALU.add))
            se = p_cmp.rearrange("p (s e) -> p s e", e=E0)
            do(v.tensor_tensor(se, cf[:, SUPI:SUPI + SUPS0].unsqueeze(2).to_broadcast([P, SUPS0, E0]),
                               sm[:, 30:38].unsqueeze(1).to_broadcast([P, SUPS0, E0]), ALU.is_ge))
            settle()
            do(v.tensor_reduce(p_oh[:, 0:SUPS0], se, AX.X, ALU.add))
            settle()
            v.tensor_scalar(eidx, p_oh[:, 0:SUPS0], float(E0 - 1), None, ALU.min).then_inc(s_exp, 1)

            def hidden_and_out(t):
                for b in range(HB0):
                    dve.wait_ge(s_sg, t * HB0 + b + 1)
                    if b == 0:
                        dve.wait_ge(s_y, t * 2 + 2)
                    v.tensor_tensor(hidden[:, b, :], sg[:, b % 2, :], bank(2 * (b % 2) + 1, SUP), ALU.mult).then_inc(s_ht, 1)
                dve.wait_ge(s_yst, t * 16 + 16)
                for j in range(2):
                    dve.wait_ge(s_y, t * 2 + j + 3)
                    v.tensor_copy(yst[:, j, :], bank(4 + j)).then_inc(s_ya, 1)

            with dve.Fori(0, SUPS0 // 2) as i:
                for u in range(2):
                    hidden_and_out(i * 2 + u)
            hidden_and_out(SUPS0 - 1)
            dve.wait_ge(s_yg, 16 * PICKS)
            for c in range(2):
                for n in range(NT):
                    do(v.scalar_tensor_tensor(X[:, n, :], yg[:, c * NT + n, :], sm[:, 50 + 10 * c + n:51 + 10 * c + n], X[:, n, :],
                                              ALU.mult, ALU.add))
                settle()
            if stop <= 4:
                v.tensor_copy(sm[:, 0:1], sm[:, 1:2]).then_inc(s_out, 1)
                return
            layer_norm(5)
            for k in range(2):
                dve.wait_ge(s_w, 16 * (15 + 5 + 4 * k))
                for n in range(NT):
                    dve.wait_ge(s_h2, NT * k + n + 1)
                    if n:
                        dve.wait_ge(s_rows, NT * (3 + k) + n)
                    v.memset(hx4[:, n, :, C:C + 1], 1.0)
                    for hd in range(H):
                        for side, (vec, to) in enumerate(((asv, als), (adv, ald))):
                            last = v.scalar_tensor_tensor(PS[:, 2048 + C * (2 * hd + side):2048 + C * (2 * hd + side + 1)], hx4[:, n, hd, 0:C], 1.0, vec[:, C * hd:C * hd + C],
                                                          ALU.mult, ALU.mult, accum_out=to[:, n, hd:hd + 1])
                    last.then_inc(s_rows, 1)
                dve.wait_ge(s_rows, NT * (4 + k))
                do(v.tensor_tensor(Et[:, TILES:COLS, :], als[:, :, :], ald[:, :, :], ALU.add))
                to_supers(tmp1, ald, parts1, whole1, H, s_ad3)
                own = Et[:, TILES:COLS, :]
                do(v.scalar_tensor_tensor(own, own, SLOPE, own, ALU.mult, ALU.max))
                parts = [lp[:, b * UN * H:(b + 1) * UN * H].rearrange("p (t h) -> p t h", h=H) for b in range(3)]
                rest = lrest.rearrange("p (t h) -> p t h", h=H)
                with dve.Fori(0, STEPS) as i, S.loop(i, STEPS, 5):
                    dve.wait_ge(s_adp, i + STEPS * k + 1)
                    do(v.tensor_reduce(Et[:, bass.ds(i * UN, UN), :], at_edge(AT_ADP, H), AX.X, ALU.add))
                    settle()
                    for q in range(4):
                        dve.wait_ge(s_g[q], i * 32 + 32 * (STEPS * (6 + 2 * k) + 1))
                        at = bass.ds(i * UN + 2 * q, 2)
                        v.tensor_tensor(Et[:, at, :], asr[:, 2 * q:2 * q + 2, :], Et[:, at, :], ALU.add).then_inc(s_slotA, 1)
                    dve.wait_ge(s_slotA, i * 4 + NSUP * (3 + k) + 8)
                    e8 = Et[:, bass.ds(i * UN, UN), :]
                    do(v.scalar_tensor_tensor(e8, e8, SLOPE, e8, ALU.mult, ALU.max))
                    settle()
                    do(v.tensor_scalar(parts[0], e8, 1.0, None, ALU.mult))
                    settle()
                    do(v.tensor_tensor(rest, e8, parts[0], ALU.subtract))
                    settle()
                    do(v.tensor_copy(parts[1], rest))
                    settle()
                    v.tensor_tensor(parts[2], rest, parts[1], ALU.subtract).then_inc(s_lp, 1)
                    maxima(i, HALVES * (3 + H * k), H)
                dve.wait_ge(s_lp, STEPS * (k + 1))
                dve.wait_ge(s_mr, HALVES * (3 + H * (k + 1)) + 2)
                node_maxima(tmp1, parts1, whole1, Et[:, TILES:COLS, :], H)
                v.tensor_tensor(Ew[:, TILES:COLS, :], Et[:, TILES:COLS, :], mm[:, :, :], ALU.subtract).then_inc(s_we, 1)
                exponents(0, 3 + k, AT_MAX1, Et, Ew)
                dve.wait_ge(s_ex, (STEPS + 1) * (3 + k) + 1)
                dve.wait_ge(s_tab, 16 * (5 + 2 * k))
                for n in range(NT):
                    for hd in range(H):
                        do(v.tensor_scalar(hx4[:, n, hd, :], hx4[:, n, hd, :],
                                           Ew[:, TILES + n, hd:hd + 1], None, ALU.mult))
                settle()

                def weigh1(i, h):
                    t = i * UN + 4 * h
                    dve.wait_ge(s_ex, i + (STEPS + 1) * (3 + k) + 2)
                    for j in range(4):
                        for hd in range(H):
                            last = v.tensor_scalar(wring1[:, 4 * h + j, hd, :], iota,
                                                   slots[:, bass.ds(t + j, 1), 1:2].rearrange("p t c -> p (t c)"),
                                                   Ew[:, bass.ds(t + j, 1), hd:hd + 1].rearrange("p t c -> p (t c)"), ALU.is_equal, ALU.mult)
                    last.then_inc(s_wb, 1)

                for h in range(2):
                    weigh1(0, h)

                def add_head_sums(i, more):
                    for h in range(2):
                        for q in range(2):
                            if more and h == 0 and q == 1:
                                exponents(i + 1, 3 + k, AT_MAX1, Et, Ew)
                            s = 2 * h + q
                            n = dve.value_load(nidx[0:1, bass.ds(i * 4 + s, 1)], min_val=0, max_val=NT - 1)
                            sums = RA[:, bass.ds(n * HW, HW)].rearrange("p (h c) -> p h c", h=H)
                            dve.wait_ge(s_pb, i * 4 + 2 * HALVES * (3 + k) + s + 5)
                            dve.wait_ge(s_ac, i * 4 + 2 * HALVES * (3 + k) + s + 2)
                            v.tensor_tensor(sums, sums, PS[:, 2048 * q:2048 * q + 2048].rearrange("p (h c) -> p h c", h=H)[:, :, 0:C + 1],
                                            ALU.add).then_inc(s_ac, 1)
                        if more:
                            weigh1(i + 1, h)

                with dve.Fori(0, STEPS - 1) as i, S.loop(i, STEPS - 1, 2):
                    add_head_sums(i, True)
                add_head_sums(STEPS - 1, False)
                dve.wait_ge(s_ac, 2 * HALVES * (4 + k) + 2)
                do(v.reciprocal(mm[:, :, :], hx4[:, :, :, C]))
                settle()
                for n in range(NT):
                    for hd in range(H):
                        do(v.scalar_tensor_tensor(hx4[:, n, hd, 0:C], hx4[:, n, hd, 0:C], mm[:, n, hd:hd + 1],
                                                  gb[:, C * hd:C * hd + C], ALU.mult, ALU.add))
                settle()
                for n in range(NT):
                    v.tensor_scalar(hx4[:, n, :, 0:C], hx4[:, n, :, 0:C], 0.0, None, ALU.max).then_inc(s_h, 1)
            for n in range(NT):
                dve.wait_ge(s_fc, n + 1)
                do(v.tensor_tensor(X[:, n, :], X[:, n, :], bfc, ALU.add))
                settle()
                v.tensor_tensor(X[:, n, :], X[:, n, :], bank(n % 2), ALU.add).then_inc(s_fcd, 1)
            dve.wait_ge(s_fcd, NT)
            if stop <= 5:
                v.tensor_copy(sm[:, 0:1], sm[:, 1:2]).then_inc(s_out, 1)
                return
            layer_norm(6)
            do(v.memset(dw, 0.0))
            dve.wait_ge(s_rwl, 16 * 5)
            dve.wait_ge(s_rt, 2)
            do(v.tensor_tensor(lg, bank(4, 80).rearrange("p (n e) -> p n e", e=8), brr.unsqueeze(1).to_broadcast([P, NT, 8]), ALU.add))
            settle()
            do(v.tensor_reduce(sm[:, 0:NT], lg, AX.X, ALU.max))
            settle()
            v.tensor_tensor(lg, lg, sm[:, 0:NT].unsqueeze(2).to_broadcast([P, NT, 8]), ALU.subtract).then_inc(s_re, 1)
            dve.wait_ge(s_rx, 2)
            do(v.tensor_reduce(sm[:, 10:20], lg, AX.X, ALU.add))
            settle()
            do(v.reciprocal(sm[:, 20:30], sm[:, 10:20]))
            settle()
            do(v.tensor_tensor(lg, lg, sm[:, 20:30].unsqueeze(2).to_broadcast([P, NT, 8]), ALU.mult))
            settle()
            two_best(1)
            place(v8[:, :, 0:1], v8[:, :, 1:2])
            dve.wait_ge(s_dw, 2)
            for n in range(NT):
                dve.wait_ge(s_ct, n + 1)
                v.tensor_copy(cwT[:, n % 2, :], bank(6 + n % 2, P)).then_inc(s_ctc, 1)
                dve.wait_ge(s_cb, n + 1)
                v.tensor_tensor(X[:, n, :], X[:, n, :], bank(4 + n % 2), ALU.add).then_inc(s_cbd, 1)
            dve.wait_ge(s_cbd, NT)
            with dve.Fori(0, E1 // 2) as i:
                for u in range(2):
                    for b in range(6):
                        t0, w = CHUNKS[b // 2]
                        dve.wait_ge(s_hu, i * 12 + 6 * u + b + 1)
                        v.tensor_scalar(hT[:, b % 2, t0:t0 + w], bank(b % 2, w), b1c[:, bass.ds(i * 4 + 2 * u + b % 2, 1)], 0.0,
                                        ALU.add, ALU.max).then_inc(s_hd, 1)
                    for n in range(NT):
                        dve.wait_ge(s_yy, i * (2 * NT) + NT * u + n + 1 + NT)
                        v.scalar_tensor_tensor(X[:, n, :], bank(4 + n % 2), dw[:, bass.ds(i * 2 + (u + 8 * n), 1)], X[:, n, :],
                                               ALU.mult, ALU.add).then_inc(s_yd, 1)
            dve.wait_ge(s_yd, E1 * NT + 2)
            v.tensor_copy(sm[:, 0:1], sm[:, 1:2]).then_inc(s_out, 1)


def attr_parts(v, do, settle, to, slots, rest, n):
    for c in range(2):
        src = slots[:, :, 2 + c]
        for a in range(3):
            cols = [to[:, :, c * 9 + a * 3 + b] for b in range(3)]
            for col in cols:
                do(v.tensor_copy(col, src))
            settle()
            if a < 2:
                do(v.tensor_tensor(rest, src, cols[0], ALU.subtract))
                settle()
                src = rest


_SHAPED = ("x", "src", "dst", "edge_attr_2", "L0_gnn_Wl", "L0_gnn_bl", "L0_gnn_Wr", "L0_gnn_br", "L0_gnn_We", "L0_gnn_att",
           "L0_gnn_b_out", "L0_gnn_gamma", "L0_gnn_beta", "L0_ffn_w_gate", "L0_ffn_w_up", "L0_ffn_w_down", "L1_gnn_W1",
           "L1_gnn_a_src1", "L1_gnn_a_dst1", "L1_gnn_b1", "L1_gnn_W2", "L1_gnn_a_src2", "L1_gnn_a_dst2", "L1_gnn_b2",
           "L1_gnn_Wfc", "L1_gnn_bfc", "L1_ffn_br", "L1_ffn_W1", "L1_ffn_W2")


def kernel(**inputs):
    import ml_dtypes
    import concourse.bacc as bacc
    from concourse.bass_utils import run_bass_kernel_spmd

    arrays = {k: np.ascontiguousarray(inputs[k]) for k in _SHAPED}
    cf, cb, reset = constants()
    arrays["cf"], arrays["cb"], arrays["reset"] = cf, cb.astype(ml_dtypes.bfloat16), reset
    We = np.asarray(inputs["L0_gnn_We"])
    rows = np.zeros((3, P, D), np.float32)
    for q in range(4):
        for c in range(2):
            rows[:, 32 * q + 9 * c:32 * q + 9 * c + 9] = We[:, c:c + 1]
    arrays["we_rows"] = rows
    inner = lambda w: np.ascontiguousarray(w.reshape(KC, P, 8).transpose(1, 0, 2).reshape(P, KC * 8))
    arrays["router0"] = inner(np.asarray(inputs["L0_ffn_router_w"]).T)
    arrays["router1"] = inner(np.asarray(inputs["L1_ffn_Wr"]))
    b1 = np.asarray(inputs["L1_ffn_b1"])
    arrays["b1_cols"] = np.ascontiguousarray(b1.reshape(E1 * 2, P).T)
    b2 = np.zeros((P, D), np.float32)
    b2[0:E1] = inputs["L1_ffn_b2"]
    arrays["b2_rows"] = b2

    nc = bacc.Bacc("TRN2", target_bir_lowering=False, num_devices=1)
    a = {k: nc.dram_tensor(f"in_{k}", v.shape, mybir.dt.from_np(v.dtype), kind="ExternalInput").ap() for k, v in arrays.items()}
    out = nc.dram_tensor("out", (N, D), F32, kind="ExternalOutput").ap()
    build(nc, a, out)
    r = run_bass_kernel_spmd(nc, [{f"in_{k}": v for k, v in arrays.items()}], core_ids=[0])
    return r.results[0]["out"]
```

```python
import numpy as np

import concourse.bass as bass
from concourse import mybir
from concourse.alu_op_type import AluOpType as ALU
from contextlib import ExitStack, contextmanager

F32, BF16, I32, U32 = mybir.dt.float32, mybir.dt.bfloat16, mybir.dt.int32, mybir.dt.uint32
ACT = mybir.ActivationFunctionType
AX = mybir.AxisListType

P = 128
N, E, D = 1250, 20000, 512
NT = -(-N // P)
LAST = N - (NT - 1) * P
KC = D // P
EP, EK = 125, 160
SUP = 2 * P
NSUP = (E + NT * (SUP - 1)) // SUP
TILES = 2 * NSUP
COLS = TILES + NT
UN = 8
STEPS = TILES // UN
GT = 16
GROUPS = TILES // GT
HALVES = 2 * STEPS
XW = D + 4
H, C = 4, 256
HC = H * C
HW = H * (C + 1)
E0, F0 = 8, 1024
E1, F1 = 8, 256
HB0 = F0 // P
SUPS0 = (2 * NT * P + E0 * (SUP - 1)) // SUP
PICKS = 2 * NT
CHUNKS = [(0, 512), (512, 512), (1024, NT * P - 1024)]
BIG = 2.0 ** 100
SLOPE = 0.2
EPS = 1e-5
ADDS = NT + TILES * 3 // 4
assert TILES % UN == 0 and KC == 4

AT_ADP, AT_MAX0, AT_MAX1 = 7 * 512, 6 * 512, 7 * 512

IDENT, IOTA, TRI, ONES = 0, P, 2 * P, 3 * P
SUPI, GI, XI, BSEL, QSEL = 4 * P, 4 * P + NSUP, 4 * P + NSUP + NT, 4 * P + NSUP + NT + 8, 4 * P + NSUP + NT + 11
TOK = QSEL + 4
CFW = TOK + NT
SEL = 4 * P
SEL0 = SEL + UN * H
CBW = SEL0 + GT


def constants():
    cf = np.zeros((P, CFW), np.float32)
    cf[:, IDENT:IDENT + P] = np.eye(P)
    cf[:, IOTA:IOTA + P] = np.arange(P)
    cf[:, TRI:TRI + P] = np.triu(np.ones((P, P)), 1)
    cf[:, ONES:ONES + P] = 1.0
    cf[:, SUPI:SUPI + NSUP] = np.arange(NSUP)
    cf[:, GI:GI + NT] = np.arange(NT)
    cf[:, XI:XI + 8] = np.arange(8)
    row = np.arange(P)
    for b in range(3):
        cf[:, BSEL + b] = (row % 32 < 18) & (row % 32 % 3 == b)
    for q in range(4):
        cf[:, QSEL + q] = row // 32 == q
    cf[:, TOK:TOK + NT] = row[:, None] + P * np.arange(NT)
    cb = np.zeros((P, CBW), np.float32)
    cb[:, 0:P] = np.eye(P)
    cb[:, P:2 * P] = np.eye(P) * BIG
    cb[0, 2 * P:3 * P] = -BIG
    cb[:, 3 * P:4 * P] = 1.0
    for b in range(3):
        cb[b * UN * H + np.arange(UN * H), SEL + np.arange(UN * H)] = 1.0
        cb[b * GT + np.arange(GT), SEL0 + np.arange(GT)] = 1.0
    reset = np.ones((EP, NT, EK), np.float32)
    reset[:, :, 0] = 0.0
    return cf, cb, reset.reshape(EP, NT * EK)


class Steps:

    def __init__(self, engine, sem):
        self.engine, self.sem, self.n, self.loop_at, self.per = engine, sem, 0, None, 0

    def step(self, instruction):
        instruction.then_inc(self.sem, 1)
        self.n += 1

    def settle(self):
        at = self.n if self.loop_at is None else self.loop_at * self.per + self.n
        self.engine.wait_ge(self.sem, at)

    def all_but(self, last):
        self.engine.wait_ge(self.sem, self.n - last)

    @contextmanager
    def loop(self, i, count, per):
        first = self.n
        self.loop_at, self.per = i, per
        yield
        assert self.n == first + per, (self.n - first, per)
        self.loop_at, self.n = None, first + count * per


def build(nc, a, out):
    ctx = ExitStack()
    with ctx:
        def sb(name, shape, dtype=F32):
            return ctx.enter_context(nc.sbuf_tensor(name, shape, dtype))

        def sem(name):
            return ctx.enter_context(nc.semaphore(name))

        def dram(name, shape, dtype=F32):
            return nc.dram_tensor(name, shape, dtype).ap()

        slots_d = dram("slots_d", [P * TILES, 4])
        xl_d = [dram(f"xl_d{k}", [NT * P, XW]) for k in range(3)]
        hx_d = [dram(f"hx_d{k}", [NT * P, HW]) for k in range(2)]
        als_d = [dram(f"als_d{k}", [NT * P, H]) for k in range(2)]

        h_d = dram("h_d", [NT * P, D])
        tok_d = dram("tok_d", [P * 2 * SUPS0, 1], I32)
        y_d = dram("y_d", [SUPS0 * SUP, D])

        X = sb("X", [P, NT, D])
        RA = sb("RA", [P, NT * (XW + D)])
        RT = sb("RT", [P, 10 * 1280])
        RW = sb("RW", [P, 8192])
        RO = sb("RO", [P, TILES * P], BF16)
        RB = sb("RB", [P, 4 * 512])
        cf = sb("cf", [P, CFW])
        cb = sb("cb", [P, CBW], BF16)
        slots = sb("slots", [P, COLS, 4])
        nidx = sb("nidx", [P, NSUP], I32)
        gneg = sb("gneg", [P, NT, NSUP], BF16)
        idxr = sb("idxr", [P, 2 * UN], I32)
        st = sb("st", [P, NT, 6])
        mv = sb("mv", [P, NT, 2])
        std = sb("std", [P, NT])
        rstd = sb("rstd", [P, NT])
        sm = sb("sm", [P, 96])
        mm = sb("mm", [P, NT, H])
        PS = ctx.enter_context(nc.psum_tensor("PS", [P, 8 * 512], F32))

        def bank(b, w=512):
            return PS[:, b * 512:b * 512 + w]

        xT = RT[:, 0:8 * 1280].rearrange("p (c n) -> p c n", c=8)
        xlx = RA[:, 0:NT * XW].rearrange("p (n d) -> p n d", d=XW)
        hin = RA[:, NT * XW:NT * (XW + D)].rearrange("p (n d) -> p n d", d=D)
        hx = RA[:, 0:NT * HW].rearrange("p (n d) -> p n d", d=HW)
        hx4 = RA[:, 0:NT * HW].rearrange("p (n h c) -> p n h c", h=H, c=C + 1)
        hT = RA[:, 0:8 * 1280].rearrange("p (c n) -> p c n", c=8)
        ring0 = RT[:, 0:UN * XW].rearrange("p (t d) -> p t d", d=XW)
        ring1 = RT[:, 0:UN * HW].rearrange("p (t d) -> p t d", d=HW)
        xr3 = RT[:, 5120:12800].bitcast(BF16).rearrange("p (n a d) -> p n a d", n=NT, a=3)
        Oht = RO
        ident, iota, tri, ones = (cf[:, o:o + P] for o in (IDENT, IOTA, TRI, ONES))
        identb, bigid, negbig, onesb = cb[:, 0:P], cb[:, P:2 * P], cb[:, 2 * P:3 * P], cb[:, 3 * P:4 * P]
        ROf = RO[:, :].bitcast(F32)
        at = [0]

        def carve(region, n):
            v = region[:, at[0]:at[0] + n]
            at[0] += n
            return v

        GE = NT * EK
        r_dst, r_src = carve(ROf, EK).bitcast(I32), carve(ROf, EK).bitcast(I32)
        r_ea = carve(ROf, 2 * EK)
        r_gi, r_li = carve(ROf, EK).bitcast(I32), carve(ROf, EK).bitcast(I32)
        r_gf, r_pos, r_row = carve(ROf, EK), carve(ROf, EK), carve(ROf, EK)
        r_posi, r_rowi = carve(ROf, EK).bitcast(I32), carve(ROf, EK).bitcast(I32)
        r_reset, r_oh, r_inc, r_t = (carve(ROf, GE) for _ in range(4))
        r_rec = carve(ROf, 4 * EK)
        r_pad = carve(ROf, 4 * TILES)
        r_cmp = carve(ROf, NSUP * NT)
        scr = carve(ROf, 2 * 8 * 4)
        sci = carve(ROf, 2 * 8).bitcast(I32)
        assert at[0] <= TILES * P // 2
        Wl = RW[:, 0:2048].rearrange("p (c d) -> p c d", c=KC)
        Wr = RW[:, 2048:4096].rearrange("p (c d) -> p c d", c=KC)
        zr = RW[:, 0:1024].rearrange("p (b d) -> p b d", b=2)
        tmp880 = RW[:, 0:NT * NSUP].rearrange("p (n s) -> p n s", n=NT)
        wring = RW[:, 0:1024].rearrange("p (t d) -> p t d", t=UN)
        lp0 = RW[:, 1280:1544].bitcast(BF16)
        lrest0 = RW[:, 1544:1544 + TILES]
        lpT0 = RW[:, 1720:1784].bitcast(BF16)
        tabs = RW[:, 2048:2560]
        Rt, Wt = tabs[:, 0:COLS], tabs[:, 256:256 + COLS]
        parts0, whole0 = RW[:, 1024:1156].bitcast(BF16), RW[:, 1156:1156 + NSUP]
        eaT = RW[:, 4096:4096 + TILES // 4 * 64].bitcast(BF16)
        wez = RW[:, 6912:7936].bitcast(BF16).rearrange("p (q d) -> p q d", q=4)
        eaTs = RW[:, 7936:8128].bitcast(BF16)
        epf = RW[:, 0:2816]
        ep = epf.bitcast(BF16).rearrange("p (t c) -> p t c", c=32)
        ohr = RW[:, 2816:3456].bitcast(BF16).rearrange("p (b t d) -> p b t d", b=2, t=5)
        easum = RT[:, 0:NSUP * 32].rearrange("p (s c) -> p s c", c=32)
        werow, werem = RW[:, 0:512], RW[:, 512:1024]
        wep = RW[:, 1024:1792].bitcast(BF16).rearrange("p (b d) -> p b d", b=3)
        wsel = RW[:, 1792:2048].bitcast(BF16)
        bl, br, att = (RB[:, 512 * k:512 * k + 512] for k in range(3))
        we0, we1 = bl, br
        gamma, beta = bl, br
        bout = RB[:, 1536:2048]
        xrf, junk, small = bank(4), bank(5), bank(7)
        xr3f = RT[:, 5120:12800].bitcast(BF16)
        Mx = sb("Mx", [P, H, NSUP])
        Lal = sb("Lal", [P, COLS])
        esp = sb("esp", [P, 12, 32], BF16)
        W1 = RW[:, 0:4 * HC].rearrange("p (c d) -> p c d", c=4)
        W2 = RW[:, 0:8 * HC].rearrange("p (c d) -> p c d", c=8)
        Wfc = RW[:, 0:8 * D].rearrange("p (c d) -> p c d", c=8)
        asv, adv = RB[:, 0:HC], RB[:, HC:2 * HC]
        bfc = RT[:, 11264:11264 + D]
        gb = RT[:, 10240:10240 + HC]
        Et = RW[:, 0:COLS * H].rearrange("p (t h) -> p t h", h=H)
        Ew = RW[:, 768:768 + COLS * H].rearrange("p (t h) -> p t h", h=H)
        wring1 = RW[:, 1536:1536 + UN * H * P].rearrange("p (t h d) -> p t h d", t=UN, h=H)
        lp = RW[:, 6512:6560].bitcast(BF16)
        lpT = RW[:, 6560:6624].bitcast(BF16)
        lrest = RW[:, 6624:6624 + UN * H]
        parts1, whole1 = RW[:, 5632:6160].bitcast(BF16), RW[:, 6160:6160 + NSUP * H]
        tmp1 = RW[:, 6656:6656 + NT * NSUP].rearrange("p (n s) -> p n s", n=NT)
        asr = sb("asr", [P, UN, H])
        als, ald = sb("als", [P, NT, H]), sb("ald", [P, NT, H])
        wg = [r[:, 0:4096].rearrange("p (c d) -> p c d", c=KC) for r in (RW, RA)]
        wu = [r[:, 4096:8192].rearrange("p (c d) -> p c d", c=KC) for r in (RW, RA)]
        wd = [RT[:, 4096 * u:4096 * u + 4096].rearrange("p (c d) -> p c d", c=HB0) for u in range(2)]
        xg = RT[:, 8192:10240].rearrange("p (t d) -> p t d", d=D)
        xgT = RT[:, 10240:12288].rearrange("p (u c t) -> p u c t", u=2, c=KC)
        sg = RT[:, 12288:12800].rearrange("p (b d) -> p b d", b=2)
        hidden = RA[:, 8192:10240].rearrange("p (c t) -> p c t", c=HB0)
        yst = RB[:, 1024:2048].rearrange("p (t d) -> p t d", t=2)
        yg = RA[:, 0:PICKS * D].rearrange("p (k d) -> p k d", d=D)
        picks = RB[:, 384:384 + PICKS]
        place0 = RB[:, 404:404 + PICKS].bitcast(I32)
        row0 = RB[:, 424:424 + PICKS].bitcast(I32)
        pos0 = RB[:, 444:444 + PICKS]
        hi0 = RB[:, 464:464 + PICKS].bitcast(I32)
        lo0 = RB[:, 484:484 + PICKS].bitcast(I32)
        tokid = RB[:, 504:504 + NT].bitcast(I32)
        eidx = RB[:, 520:520 + SUPS0].bitcast(I32)
        tokens = RB[:, 560:560 + 2 * SUPS0].bitcast(I32)
        zeros = RB[:, 600:600 + 2 * SUPS0].bitcast(I32)
        p_oh, p_inc, p_t, p_reset = (RT[:, 8192 + 160 * j:8352 + 160 * j] for j in range(4))
        p_cmp = RT[:, 8832:8832 + SUPS0 * E0]
        rw = RB[:, 0:KC * 8].rearrange("p (c e) -> p c e", c=KC)
        brr = RB[:, 32:40]
        b1c = RB[:, 40:40 + E1 * 2]
        lg = RB[:, 64:144].rearrange("p (n e) -> p n e", e=8)
        v8 = RB[:, 144:224].rearrange("p (n e) -> p n e", e=8)
        i8 = RB[:, 224:304].bitcast(U32).rearrange("p (n e) -> p n e", e=8)
        i8f = RB[:, 304:384].rearrange("p (n e) -> p n e", e=8)
        dw = RB[:, 384:384 + 208]
        dwv = dw[:, 0:80].rearrange("p (n e) -> p n e", e=8)
        dw2 = RB[:, 600:680].rearrange("p (n e) -> p n e", e=8)
        b2p = RB[:, 1024:1536]
        cwT = RB[:, 1536:1536 + 2 * P].rearrange("p (b t) -> p b t", b=2)
        we1v = [RW[:, 2048 * u:2048 * u + 1024].rearrange("p (c d) -> p c d", c=KC) for u in range(2)]
        we2v = [RW[:, 2048 * u + 1024:2048 * u + 2048].rearrange("p (c d) -> p c d", c=2) for u in range(2)]

        s_const = sem("s_const")
        s_edges = sem("s_edges")
        s_x = sem("s_x")
        s_padded = sem("s_padded")
        s_padst = sem("s_padst")
        s_tot = sem("s_tot")
        s_pref = sem("s_pref")
        s_route = sem("s_route")
        s_sccopy = sem("s_sccopy")
        s_scat = [sem("s_scat0"), sem("s_scat1")]
        s_slots = sem("s_slots")
        s_var = sem("s_var")
        s_std = sem("s_std")
        s_h = sem("s_h")
        s_tp = sem("s_tp")
        s_tpc = sem("s_tpc")
        s_w = sem("s_w")
        s_bias = sem("s_bias")
        s_w2 = sem("s_w2")
        s_norm = sem("s_norm")
        s_bo = sem("s_bo")
        s_als = sem("s_als")
        s_proj = sem("s_proj")
        s_ev = sem("s_ev")
        s_rows = sem("s_rows")
        s_tab = sem("s_tab")
        s_oh = sem("s_oh")
        s_bt = sem("s_bt")
        s_btc = sem("s_btc")
        s_esp = sem("s_esp")
        s_est = sem("s_est")
        s_esc = sem("s_esc")
        s_wez = sem("s_wez")
        s_idx = sem("s_idx")
        s_pass = sem("s_pass")
        s_g = [sem(f"s_g{q}") for q in range(4)]
        s_slotA = sem("s_slotA")
        s_apass = sem("s_apass")
        s_nidx = sem("s_nidx")
        s_z = sem("s_z")
        s_zd = sem("s_zd")
        s_st = sem("s_st")
        s_L = sem("s_L")
        s_mx = sem("s_mx")
        s_mr = sem("s_mr")
        s_m3 = sem("s_m3")
        s_md = sem("s_md")
        s_we = sem("s_we")
        s_ex = sem("s_ex")
        s_self = sem("s_self")
        s_wb = sem("s_wb")
        s_wa = sem("s_wa")
        s_pb = sem("s_pb")
        s_ac = sem("s_ac")
        s_ad3 = sem("s_ad3")
        s_adp = sem("s_adp")
        s_h2 = sem("s_h2")
        s_lp = sem("s_lp")
        s_lt = sem("s_lt")
        s_ltc = sem("s_ltc")
        s_fc = sem("s_fc")
        s_fcd = sem("s_fcd")
        s_rt = sem("s_rt")
        s_re = sem("s_re")
        s_rx = sem("s_rx")
        s_rwl = sem("s_rwl")
        s_dw = sem("s_dw")
        s_hd_d = sem("s_hd_d")
        s_exp = sem("s_exp")
        s_ps = sem("s_ps")
        s_tok = sem("s_tok")
        s_xg = [sem("s_xg0"), sem("s_xg1")]
        s_xt = sem("s_xt")
        s_xc = sem("s_xc")
        s_yst = sem("s_yst")
        s_yg = [sem(f"s_yg{j}") for j in range(NT // 2)]
        s_wgu = [sem("s_wgu0"), sem("s_wgu1")]
        s_wdn = [sem("s_wdn0"), sem("s_wdn1")]
        s_gu = sem("s_gu")
        s_sg = sem("s_sg")
        s_ht = sem("s_ht")
        s_y = sem("s_y")
        s_ya = sem("s_ya")
        s_we1 = [sem("s_we10"), sem("s_we11")]
        s_hu = sem("s_hu")
        s_hd = sem("s_hd")
        s_yy = sem("s_yy")
        s_yd = sem("s_yd")
        s_ct = sem("s_ct")
        s_ctc = sem("s_ctc")
        s_cb = sem("s_cb")
        s_cbd = sem("s_cbd")
        s_dve = sem("s_dve")
        s_out = sem("s_out")

        block = ctx.enter_context(nc.Block())

        def finish(sp):
            sp.wait_ge(s_out, 1)
            sp.dma_start(out[0:(NT - 1) * P, :].rearrange("(n p) d -> p n d", p=P), X[:, 0:NT - 1, :]).then_inc(s_out, 16)
            sp.dma_start(out[(NT - 1) * P:N, :], X[0:LAST, NT - 1, :]).then_inc(s_out, 16)
            sp.wait_ge(s_out, 33)

        @block.sync
        def _(sp):
            sp.dma_start(r_dst[0:EP, :], a["dst"].rearrange("(p k) -> p k", k=EK)).then_inc(s_edges, 16)
            sp.dma_start(r_src[0:EP, :], a["src"].rearrange("(p k) -> p k", k=EK)).then_inc(s_edges, 16)
            sp.dma_start(r_ea[0:EP, :], a["edge_attr_2"].rearrange("(p k) c -> p (k c)", k=EK)).then_inc(s_edges, 16)
            sp.dma_start(r_reset[0:EP, :], a["reset"]).then_inc(s_edges, 16)
            sp.dma_start(cf[:, :], a["cf"]).then_inc(s_const, 16)
            sp.dma_start(cb[:, :], a["cb"]).then_inc(s_const, 16)
            sp.dma_start(X[:, 0:NT - 1, :], a["x"][0:(NT - 1) * P, :].rearrange("(n p) d -> p n d", p=P)).then_inc(s_x, 16)
            sp.wait_ge(s_padded, 1)
            sp.dma_start(X[0:LAST, NT - 1, :], a["x"][(NT - 1) * P:N, :]).then_inc(s_x, 16)
            sp.dma_start(slots_d.rearrange("(p t) c -> p (t c)", p=P), r_pad).then_inc(s_padst, 16)

            def store_rows(table, rows, before):
                for n in (0, NT // 2):
                    sp.wait_ge(s_rows, before + n + NT // 2)
                    sp.dma_start(table[n * P:(n + NT // 2) * P].rearrange("(n p) d -> p n d", p=P),
                                 rows[:, n:n + NT // 2, :]).then_inc(s_tab, 16)

            for k in range(3):
                if k:
                    sp.wait_ge(s_ac, 2 * HALVES * k + 2)
                sp.dma_start(Wl, a["L0_gnn_Wl"][k].rearrange("(c p) d -> p c d", p=P)).then_inc(s_w, 16)
                sp.dma_start(Wr, a["L0_gnn_Wr"][k].rearrange("(c p) d -> p c d", p=P)).then_inc(s_w, 16)
                if k:
                    sp.wait_ge(s_h, NT * k + NT)
                for to, of in ((bl, "L0_gnn_bl"), (br, "L0_gnn_br"), (att, "L0_gnn_att"), (bout, "L0_gnn_b_out")):
                    sp.dma_start(to, a[of][k].partition_broadcast(P)).then_inc(s_bias, 16)
                if k == 0:
                    for h in range(2):
                        sp.wait_ge(s_scat[h], EK // 2 * 16)
                    sp.dma_start(slots[:, 0:TILES, :].rearrange("p t c -> p (t c)"),
                                 slots_d.rearrange("(p t) c -> p (t c)", p=P)).then_inc(s_slots, 16)
                store_rows(xl_d[k], xlx, NT * k)
                sp.wait_ge(s_proj, NT * (k + 1))
                if k == 0:
                    sp.wait_ge(s_esp, 1)
                    sp.wait_ge(s_bt, HALVES + 2)
                sp.wait_ge(s_ev, NT * (k + 1))
                for to, c in ((we0, 0), (we1, 1)):
                    sp.dma_start(to, a["L0_gnn_We"][k, c].partition_broadcast(P)).then_inc(s_w2, 16)
                sp.dma_start(werow, a["we_rows"][k]).then_inc(s_w2, 16)
                sp.wait_ge(s_wez, k + 1)
                for to, of in ((gamma, "L0_gnn_gamma"), (beta, "L0_gnn_beta")):
                    sp.dma_start(to, a[of][k].partition_broadcast(P)).then_inc(s_norm, 16)
            sp.wait_ge(s_h, NT * 4)
            sp.dma_start(rw, a["router0"]).then_inc(s_rwl, 16)
            sp.dma_start(h_d.rearrange("(n p) d -> p n d", p=P), hin).then_inc(s_hd_d, 16)
            sp.wait_ge(s_dw, 1)
            sp.dma_start(tok_d.rearrange("(p t) c -> p (t c)", p=P), zeros).then_inc(s_hd_d, 16)
            sp.sem_inc(s_yst, 16)
            sp.wait_ge(s_exp, 1)
            sp.wait_ge(s_rt, 1)
            sp.wait_ge(s_hd_d, 32)

            def load_gate_up(t, u):
                e = sp.value_load(eidx[0:1, bass.ds(t, 1)], min_val=0, max_val=E0 - 1)
                sp.dma_start(wg[u], a["L0_ffn_w_gate"][bass.ds(e, 1)].rearrange("e (c p) d -> p (e c) d", p=P)).then_inc(s_wgu[u], 16)
                sp.dma_start(wu[u], a["L0_ffn_w_up"][bass.ds(e, 1)].rearrange("e (c p) d -> p (e c) d", p=P)).then_inc(s_wgu[u], 16)
                return e

            def load_down(e, u):
                sp.dma_start(wd[u], a["L0_ffn_w_down"][bass.ds(e, 1)].rearrange("e (c p) d -> p (e c) d", p=P)).then_inc(s_wdn[u], 16)

            def super_tile0(t, u, more):
                if more:
                    sp.wait_ge(s_gu, t * HB0 + HB0)
                    e = load_gate_up(t + 2, u)
                    sp.wait_ge(s_y, t * 2 + 4)
                    load_down(e, u)
                sp.wait_ge(s_ya, t * 2 + 4)
                sp.dma_start(y_d[bass.ds(t * SUP, SUP), :].rearrange("(j p) d -> p j d", p=P), yst).then_inc(s_yst, 16)

            first = load_gate_up(0, 0)
            sp.wait_ge(s_ps, 16 * PICKS)
            sp.dma_start(tokens, tok_d.rearrange("(p t) c -> p (t c)", p=P)).then_inc(s_tok, 16)
            load_down(first, 0)
            sp.wait_ge(s_xg[0], 32)
            load_down(load_gate_up(1, 1), 1)
            with sp.Fori(0, (SUPS0 - 3) // 2) as i:
                for u in range(2):
                    super_tile0(i * 2 + u, u, True)
            for t in range(SUPS0 - 3, SUPS0):
                super_tile0(t, t % 2, t + 2 < SUPS0)
            for k in range(2):
                if k == 0:
                    sp.wait_ge(s_y, 2 * SUPS0 + 2)
                    sp.dma_start(W1, a["L1_gnn_W1"].rearrange("(c p) d -> p c d", p=P)).then_inc(s_w, 16)
                    sp.dma_start(bfc, a["L1_gnn_bfc"].partition_broadcast(P)).then_inc(s_w, 16)
                else:
                    sp.wait_ge(s_ac, 2 * HALVES * 4 + 2)
                    sp.dma_start(W2, a["L1_gnn_W2"].rearrange("(c p) d -> p c d", p=P)).then_inc(s_w, 16)
                sp.wait_ge(s_h, NT * 5)
                sp.dma_start(asv, a[f"L1_gnn_a_src{k + 1}"].rearrange("h c -> (h c)").partition_broadcast(P)).then_inc(s_w, 16)
                sp.dma_start(adv, a[f"L1_gnn_a_dst{k + 1}"].rearrange("h c -> (h c)").partition_broadcast(P)).then_inc(s_w, 16)
                if k:
                    sp.wait_ge(s_h, NT * 6)
                sp.dma_start(gb, a[f"L1_gnn_b{k + 1}"].partition_broadcast(P)).then_inc(s_w, 16)
                sp.wait_ge(s_rows, NT * (4 + k))
                sp.dma_start(als_d[k].rearrange("(n p) h -> p n h", p=P), als[:, :, :]).then_inc(s_als, 16)
                store_rows(hx_d[k], hx, NT * (3 + k))
            sp.wait_ge(s_ac, 2 * HALVES * 5 + 2)
            sp.dma_start(Wfc, a["L1_gnn_Wfc"].rearrange("(c p) d -> p c d", p=P)).then_inc(s_w, 16)
            sp.wait_ge(s_fcd, NT)
            sp.dma_start(rw, a["router1"]).then_inc(s_rwl, 16)
            sp.dma_start(brr, a["L1_ffn_br"].partition_broadcast(P)).then_inc(s_rwl, 16)
            sp.dma_start(b1c, a["b1_cols"]).then_inc(s_rwl, 16)
            sp.dma_start(b2p, a["b2_rows"]).then_inc(s_rwl, 16)

            def experts1(i, again):
                for u in range(2):
                    if again:
                        sp.wait_ge(s_yy, i * (2 * NT) + u * NT)
                    sp.dma_start(we1v[u], a["L1_ffn_W1"][bass.ds(i * 2 + u, 1)].rearrange("e (c p) d -> p (e c) d", p=P)).then_inc(s_we1[u], 16)
                    sp.dma_start(we2v[u], a["L1_ffn_W2"][bass.ds(i * 2 + u, 1)].rearrange("e (c p) d -> p (e c) d", p=P)).then_inc(s_we1[u], 16)

            experts1(0, False)
            with sp.Fori(1, E1 // 2) as i:
                experts1(i, True)
            finish(sp)

        @block.gpsimd
        def _(pool):
            pool.wait_ge(s_route, 1)
            pool.wait_ge(s_padst, 16)
            def scatter(i, again):
                for h in range(2):
                    if again:
                        pool.wait_ge(s_scat[h], i * 128)
                    pool.sem_inc(s_pass, 1)
                    pool.tensor_copy(sci[0:EP, 8 * h:8 * h + 8], r_rowi[0:EP, bass.ds(i * 16 + 8 * h, 8)]).then_inc(s_sccopy, 1)
                    pool.tensor_copy(scr[0:EP, 32 * h:32 * h + 32], r_rec[0:EP, bass.ds(i * 64 + 32 * h, 32)]).then_inc(s_sccopy, 1)
                    pool.wait_ge(s_sccopy, i * 4 + 2 * h + 2)
                    pool.sem_inc(s_pass, 1)
                    for j in range(8):
                        pool.indirect_dma_start(
                            slots_d, bass.IndirectOffsetOnAxis(ap=sci[0:EP, 8 * h + j:8 * h + j + 1], axis=0),
                            scr[0:EP, 32 * h + 4 * j:32 * h + 4 * j + 4], None).then_inc(s_scat[h], 16)

            scatter(0, False)
            with pool.Fori(1, EK // 16) as i:
                scatter(i, True)
            pool.sem_inc(s_slotA, 4)
            pool.sem_inc(s_pb, 4)

            def gathers(nth, sums, table, ring):
                count = (STEPS + 1) * (2 * nth + sums) + SUPS0 * (nth > 2)

                def indices(step, u):
                    src = slots[:, bass.ds(step * UN, UN), 0:1].bitcast(I32)
                    pool.tensor_copy(idxr[:, UN * u:UN * u + UN], src.rearrange("p t c -> p (t c)")).then_inc(s_idx, 1)

                if count:
                    pool.wait_ge(s_idx, count)
                indices(0, 0)
                with pool.Fori(0, STEPS // 2) as i:
                    for u in range(2):
                        pool.wait_ge(s_idx, i * 2 + count + u + 1)
                        for q in range(4):
                            pool.wait_ge(s_pb if sums else s_slotA, i * 8 + NSUP * nth + 4 * u + q + 1)
                            pool.sem_inc(s_pass, 1)
                            if q == 3:
                                indices(i * 2 + (u + 1), 1 - u)
                            for j in (2 * q, 2 * q + 1):
                                index = idxr[:, UN * u + j:UN * u + j + 1]
                                pool.indirect_dma_start(ring[:, j, :], None, table,
                                                        bass.IndirectOffsetOnAxis(ap=index, axis=0)).then_inc(s_g[q], 16)

            pool.sem_inc(s_mx, 2)
            for k in range(3):
                pool.wait_ge(s_bias, 64 * (k + 1))
                for n in range(NT):
                    pool.wait_ge(s_tpc, NT * k + n + 1)
                    pool.tensor_tensor(hin[:, n, :], hin[:, n, :], bout, ALU.add).then_inc(s_bo, 1)
                pool.wait_ge(s_tab, 32 * (k + 1))
                pool.wait_ge(s_proj, NT * (k + 1))
                pool.wait_ge(s_slots, 16)
                pool.wait_ge(s_esp, 1)
                gathers(k, 0, xl_d[k], ring0)
                pool.wait_ge(s_L, k + 1)
                gathers(k, 1, xl_d[k], ring0)
            pool.wait_ge(s_exp, 1)
            pool.wait_ge(s_hd_d, 32)
            for k in range(PICKS):
                pool.indirect_dma_start(tok_d, bass.IndirectOffsetOnAxis(ap=row0[:, k:k + 1], axis=0),
                                        tokid[:, k % NT:k % NT + 1], None).then_inc(s_ps, 16)
            pool.wait_ge(s_tok, 16)
            pool.wait_ge(s_idx, 6 * (STEPS + 1))

            def tokens_of(t, u):
                pool.wait_ge(s_xt, t + 1)
                pool.sem_inc(s_pass, 1)
                pool.tensor_copy(idxr[:, 2 * u:2 * u + 2], tokens[:, bass.ds(t * 2, 2)]).then_inc(s_idx, 1)
                pool.wait_ge(s_idx, t + 6 * (STEPS + 1) + 1)
                pool.sem_inc(s_pass, 1)
                for j in (2 * u, 2 * u + 1):
                    pool.indirect_dma_start(xg[:, j, :], None, h_d,
                                            bass.IndirectOffsetOnAxis(ap=idxr[:, j:j + 1], axis=0)).then_inc(s_xg[u], 16)

            with pool.Fori(0, SUPS0 // 2) as i:
                for u in range(2):
                    tokens_of(i * 2 + u, u)
            tokens_of(SUPS0 - 1, 0)
            pool.wait_ge(s_yst, 16 * (SUPS0 + 1))
            for n in range(NT):
                for k in (n, NT + n):
                    pool.indirect_dma_start(yg[:, k, :], None, y_d,
                                            bass.IndirectOffsetOnAxis(ap=place0[:, k:k + 1], axis=0)).then_inc(s_yg[n // 2], 16)
            for k in range(2):
                pool.wait_ge(s_als, 16 * (k + 1))
                pool.wait_ge(s_proj, NT * (4 + k))
                gathers(3 + k, 0, als_d[k], asr[:, :, :])
                pool.wait_ge(s_slotA, NSUP * (4 + k) + 4)
                pool.wait_ge(s_tab, 32 * (4 + k))
                gathers(3 + k, 1, hx_d[k], ring1)

        @block.scalar
        def _(act):
            def root(k):
                act.wait_ge(s_var, k + 1)
                act.activation(std[:, :], mv[:, :, 1], ACT.Sqrt).then_inc(s_std, 1)

            def keep_transposed(g0, parts):
                for g in range(g0, g0 + parts * NT):
                    n, c = (g - g0) // parts, 4 * ((g - g0) % parts)
                    act.wait_ge(s_tp, g + 1)
                    act.copy(xT[:, c:c + 4, n * P:n * P + P],
                             bank(6 + g % 2).rearrange("p (c t) -> p c t", c=4)).then_inc(s_tpc, 1)

            def weights(nth, w, scaled):
                act.wait_ge(s_we, (STEPS + 1) * nth + 1)
                act.activation(w[:, TILES:COLS, :], w[:, TILES:COLS, :], ACT.Exp).then_inc(s_ex, 1)

                def exponentials(i):
                    act.wait_ge(s_we, i + (STEPS + 1) * nth + 2)
                    act.activation(w[:, bass.ds(i * UN, UN), :], w[:, bass.ds(i * UN, UN), :], ACT.Exp).then_inc(s_ex, 1)

                def scale(i):
                    act.wait_ge(s_ex, i + (STEPS + 1) * nth + 2)
                    for h in range(2):
                        act.wait_ge(s_wb, i * 2 + HALVES * nth + h + 1)
                        act.sem_inc(s_apass, 1)
                        for u in range(4 * h, 4 * h + 4):
                            for hd in (H - 2, H - 1):
                                last = act.activation(wring1[:, u, hd, :], wring1[:, u, H - 1, :], ACT.Copy,
                                                      scale=w[:, bass.ds(i * UN + u, 1), hd:hd + 1].rearrange("p t c -> p (t c)"))
                        last.then_inc(s_wa, 1)

                if not scaled:
                    with act.Fori(0, STEPS) as i:
                        exponentials(i)
                    return
                exponentials(0)
                act.wait_ge(s_ex, (STEPS + 1) * nth + 1)
                act.wait_ge(s_tab, 32 * (1 + nth))
                for n in range(NT):
                    for hd in (H - 2, H - 1):
                        last = act.activation(hx4[:, n, hd, :], hx4[:, n, hd, :], ACT.Copy, scale=w[:, TILES + n, hd:hd + 1])
                last.then_inc(s_self, 1)
                scale(0)
                with act.Fori(1, STEPS) as i:
                    exponentials(i)
                    scale(i)

            root(0)
            for k in range(3):
                keep_transposed(NT * k, 1)
                if k == 0:
                    with act.Fori(0, STEPS) as i:
                        for h in range(2):
                            act.wait_ge(s_bt, i * 2 + h + 3)
                            act.sem_inc(s_apass, 1)
                            tb = bank(h, 320).bitcast(BF16)
                            act.copy(Oht[:, bass.ds((i * 2 + h) * 512, 512)], tb[:, 0:512])
                            act.copy(eaT[:, bass.ds((i * 2 + h) * P, P)], tb[:, 512:640])
                            act.copy(RT[:, bass.ds((i * 2 + h) * 64, 64)], bank(2 + h, 64)).then_inc(s_btc, 1)
                    act.wait_ge(s_est, 1)
                    act.copy(eaTs, bank(2, 192).bitcast(BF16)).then_inc(s_esc, 1)
                with act.Fori(0, GROUPS) as g:
                    act.wait_ge(s_lt, g + GROUPS * k + 1)
                    act.copy(lpT0[0:3 * GT, :], bank(6, P)[0:3 * GT, :]).then_inc(s_ltc, 1)
                weights(k, Wt.unsqueeze(2), False)
                root(k + 1)
            root(4)
            keep_transposed(3 * NT, 1)
            act.wait_ge(s_re, 1)
            act.activation(sm[:, 30:40], sm[:, 20:30], ACT.Exp).then_inc(s_rx, 1)

            def keep_tokens(t, u):
                act.wait_ge(s_xt, t + 3)
                for j in range(2):
                    act.copy(xgT[:, u, :, j * P:j * P + P], bank(6 + j).rearrange("p (c t) -> p c t", c=KC)).then_inc(s_xc, 1)

            def gates(t):
                for b in range(HB0):
                    act.wait_ge(s_gu, t * HB0 + b + 1)
                    act.wait_ge(s_ht, t * HB0 + b + 1)
                    act.activation(sg[:, b % 2, :], bank(2 * (b % 2), SUP), ACT.Silu).then_inc(s_sg, 1)

            keep_tokens(0, 0)
            with act.Fori(0, SUPS0 // 2) as i:
                for u in range(2):
                    gates(i * 2 + u)
                    keep_tokens(i * 2 + (u + 1), 1 - u)
            gates(SUPS0 - 1)
            root(5)
            keep_transposed(4 * NT, 1)
            for k in range(2):
                for n in range(NT):
                    act.wait_ge(s_proj, NT * (3 + k) + n + 1)
                    act.copy(hx4[:, n, :, 0:C], PS[:, 1024 * (n % 2):1024 * (n % 2) + HC].rearrange("p (h c) -> p h c", h=H)).then_inc(s_h2, 1)
                with act.Fori(0, STEPS) as i:
                    act.wait_ge(s_lt, i + STEPS * k + 3 * GROUPS + 1)
                    act.copy(lpT[0:3 * UN * H, :], bank(6, 64).bitcast(BF16)[0:3 * UN * H, :]).then_inc(s_ltc, 1)
                weights(3 + k, Ew, True)
                keep_transposed(5 * NT + 2 * NT * k, 2)
            root(6)
            keep_transposed(9 * NT, 1)
            act.wait_ge(s_re, 2)
            act.activation(lg, lg, ACT.Exp).then_inc(s_rx, 1)

        @block.tensor
        def _(pe):
            mmul = nc.tensor.matmul

            def hin_block(n, c):
                return hin[:, n, c * P:c * P + P]

            def hx_block(n, c):
                return hx4[:, n, c // 2, c % 2 * P:c % 2 * P + P]

            def transposed(g0, parts, q, src):
                for g in range(g0, g0 + parts * NT):
                    n, c = (g - g0) // parts, 4 * ((g - g0) % parts)
                    pe.wait_ge(s_h, NT * q + n + 1)
                    if g >= 2:
                        pe.wait_ge(s_tpc, g - 1)
                    for j in range(4):
                        last = nc.tensor.transpose(bank(6 + g % 2)[:, j * P:j * P + P],
                                                   src(n, c + j), ident)
                    last.then_inc(s_tp, 1)

            def at_edges(i, parts, heads, to, done):
                w = 3 * heads
                for u in range(UN):
                    last = mmul(PS[:, to + u * w:to + u * w + w], Oht[:, bass.ds((i * UN + u) * P, P)],
                                parts[:, bass.ds((i * 4 + u // 2) * w, w)], start=True, stop=True)
                last.then_inc(done, 1)

            def maxima_at(i, nth, parts, heads, to):
                pe.wait_ge(s_we, i + (STEPS + 1) * nth + 1)
                at_edges(i, parts, heads, to, s_md)

            def mask(b, i, h):
                mmul(b, bigid, Oht[:, bass.ds((i * 2 + h) * 512, 512)], start=True, stop=False)
                mmul(b, negbig, onesb.unsqueeze(1).to_broadcast([P, 4, P]), start=False, stop=False)

            def masked_heads(k):
                rows = 3 * UN * H

                def transpose_parts(i, more):
                    pe.wait_ge(s_lp, i + STEPS * k + 4)
                    nc.tensor.transpose(bank(6, 64).bitcast(BF16)[0:rows, :], lp[:, 0:rows], identb).then_inc(s_lt, 1)
                    if more:
                        at_edges(i + 1, parts1, H, AT_ADP, s_adp)

                def heads_of(i):
                    for h in range(2):
                        for hd in range(H):
                            m = h * H + hd
                            pe.wait_ge(s_mr, i * (2 * H) + HALVES * (3 + H * k) + m + 1)
                            b = bank(m % 4)
                            mask(b, i, h)
                            if m == 0:
                                pe.wait_ge(s_ltc, i + STEPS * k + 3 * GROUPS + 1)
                            for j in range(4):
                                c = SEL + (4 * h + j) * H + hd
                                last = mmul(b[:, j * P:j * P + P], cb[0:rows, c:c + 1].to_broadcast([rows, P]), lpT[0:rows, :],
                                            start=False, stop=(j == 3))
                            last.then_inc(s_mx, 1)

                at_edges(0, parts1, H, AT_ADP, s_adp)
                transpose_parts(0, True)
                with pe.Fori(0, STEPS - 2) as i:
                    heads_of(i)
                    transpose_parts(i + 1, True)
                heads_of(STEPS - 2)
                transpose_parts(STEPS - 1, False)
                heads_of(STEPS - 1)

            def masked(k):
                rows = 3 * GT

                def transpose_group(g):
                    mmul(bank(6, P)[0:rows, :], lp0[:, bass.ds(g * rows, rows)], identb, start=True, stop=True).then_inc(s_lt, 1)

                def group(g):
                    for m in range(GT // 4):
                        pe.wait_ge(s_mr, g * (GT // 4) + HALVES * k + m + 1)
                        b = bank(m)
                        mask(b, g * 2 + m // 2, m % 2)
                        if m == 0:
                            pe.wait_ge(s_ltc, g + GROUPS * k + 1)
                        for j in range(4):
                            c = SEL0 + 4 * m + j
                            last = mmul(b[:, j * P:j * P + P], cb[0:rows, c:c + 1].to_broadcast([rows, P]), lpT0[0:rows, :],
                                        start=False, stop=(j == 3))
                        last.then_inc(s_mx, 1)

                pe.wait_ge(s_lp, k + 1)
                transpose_group(0)
                with pe.Fori(0, GROUPS - 1) as g:
                    group(g)
                    transpose_group(g + 1)
                group(GROUPS - 1)

            pe.wait_ge(s_const, 32)
            pe.wait_ge(s_tot, 1)
            mmul(bank(0, NT), tri[0:EP, 0:P], sm[0:EP, 0:NT], start=True, stop=True)
            mmul(bank(1, NT), ones[0:EP, :], sm[0:EP, 0:NT], start=True, stop=True).then_inc(s_pref, 1)
            pe.wait_ge(s_route, 1)
            pe.wait_ge(s_nidx, 1)
            pe.sem_inc(s_mr, 4)
            pe.sem_inc(s_ac, 2)
            for k in range(3):
                transposed(NT * k, 1, k, hin_block)
                pe.wait_ge(s_w, 32 * (k + 1))
                for n in range(NT):
                    pe.wait_ge(s_tpc, NT * k + n + 1)
                    if n >= 2:
                        pe.wait_ge(s_ev, NT * k + n - 1)
                    for side, w in enumerate((Wl, Wr)):
                        for c in range(KC):
                            last = mmul(bank(2 * (n % 2) + side), xT[:, c, n * P:n * P + P], w[:, c, :],
                                        start=(c == 0), stop=(c == KC - 1))
                    last.then_inc(s_proj, 1)
                if k == 0:
                    pe.wait_ge(s_ev, NT)
                    pe.sem_inc(s_btc, 2)
                    pe.sem_inc(s_bt, 2)
                    with pe.Fori(0, STEPS) as i:
                        for h in range(2):
                            pe.wait_ge(s_oh, i * 2 + h + 1)
                            pe.wait_ge(s_btc, i * 2 + h + 1)
                            tb = bank(h, 320).bitcast(BF16)
                            for j in range(5):
                                nc.tensor.transpose(tb[:, j * P:j * P + P], ohr[:, h, j, :], identb)
                            for q in range(2):
                                for j in range(2):
                                    t = i * UN + 4 * h + 2 * q + j
                                    last = mmul(bank(2 + h)[:, 32 * q:32 * q + 32], ohr[:, h, 2 * q + j, :],
                                                ep[:, bass.ds(t, 1), :].rearrange("p t c -> p (t c)"),
                                                start=(j == 0), stop=(j == 1))
                            last.then_inc(s_bt, 1)
                    pe.wait_ge(s_btc, HALVES + 2)
                    pe.wait_ge(s_esp, 1)
                    for j in range(3):
                        last = nc.tensor.transpose(bank(2, 192).bitcast(BF16)[:, j * P:j * P + P],
                                                   esp[:, 4 * j:4 * j + 4, :].rearrange("p t c -> p (t c)"), identb)
                    last.then_inc(s_est, 1)
                    pe.wait_ge(s_esc, 1)
                pe.wait_ge(s_wez, k + 1)
                pe.wait_ge(s_ev, NT * (k + 1))
                for n in range(NT):
                    if n >= 4:
                        pe.wait_ge(s_zd, ADDS * k + n - 3)
                    for b in range(3):
                        mmul(bank(n % 4), identb, xr3[:, n, b, :], start=(b == 0), stop=False)
                    mmul(bank(n % 4), eaTs[:, (n // 4) * P:(n // 4) * P + P], wez[:, n % 4, :],
                         start=False, stop=True).then_inc(s_z, 1)
                pe.wait_ge(s_zd, ADDS * k + NT)
                with pe.Fori(0, STEPS) as i:
                    for h in range(2):
                        for q in range(2):
                            n = pe.value_load(nidx[0:1, bass.ds(i * 4 + 2 * h + q, 1)], min_val=0, max_val=NT - 1)
                            for j in range(2):
                                u = 4 * h + 2 * q + j
                                direct = u % 4 == 3
                                if direct:
                                    pe.wait_ge(s_st, i * UN + COLS * k + NT + u - 3)
                                else:
                                    pe.wait_ge(s_zd, i * 6 + ADDS * k + NT + 3 * h + u % 4 - 2)
                                for b in range(3):
                                    mmul(bank(u % 4), Oht[:, bass.ds((i * UN + u) * P, P)],
                                         xr3f[:, bass.ds(n * (3 * D) + b * D, D)], start=(b == 0), stop=False)
                                last = mmul(bank(u % 4), eaT[:, bass.ds((i * 2 + h) * P, P)], wez[:, u % 4, :],
                                     start=False, stop=not direct)
                                if direct:
                                    pe.wait_ge(s_g[u // 2], i * 32 + 32 * (STEPS * 2 * k + 1))
                                    last = mmul(bank(3), ident, ring0[:, u, 0:D], start=False, stop=True)
                                last.then_inc(s_z, 1)
                masked(k)
                pe.wait_ge(s_m3, k + 1)
                pe.wait_ge(s_zd, ADDS * (k + 1))
                maxima_at(0, k, parts0, 1, AT_MAX0)

                def sums(i, more):
                    if more:
                        maxima_at(i + 1, k, parts0, 1, AT_MAX0)
                    for h in range(2):
                        pe.wait_ge(s_wb, i * 2 + HALVES * k + h + 1)
                        for q in range(2):
                            pe.wait_ge(s_g[2 * h + q], i * 32 + 32 * (STEPS * (2 * k + 1) + 1))
                            pe.wait_ge(s_ac, i * 4 + 2 * HALVES * k + 2 * h + q + 1)
                            for j in range(2):
                                u = 4 * h + 2 * q + j
                                mmul(bank(2 * q), wring[:, u, :], ring0[:, u, 0:D], start=(j == 0), stop=(j == 1))
                                last = mmul(bank(2 * q + 1, 2), wring[:, u, :], ring0[:, u, D:D + 2],
                                            start=(j == 0), stop=(j == 1))
                            last.then_inc(s_pb, 1)

                with pe.Fori(0, STEPS - 1) as i:
                    sums(i, True)
                sums(STEPS - 1, False)
            transposed(3 * NT, 1, 3, hin_block)

            def router(q):
                for n in range(NT):
                    pe.wait_ge(s_tpc, q + n + 1)
                    for c in range(KC):
                        last = mmul(bank(4)[:, 8 * n:8 * n + 8], xT[:, c, n * P:n * P + P], rw[:, c, :],
                                    start=(c == 0), stop=(c == KC - 1))
                last.then_inc(s_rt, 1)

            pe.wait_ge(s_rwl, 16)
            router(3 * NT)
            pe.wait_ge(s_tot, 2)
            mmul(bank(0, E0), tri, sm[:, 0:E0], start=True, stop=True)
            mmul(bank(1, E0), ones, sm[:, 0:E0], start=True, stop=True).then_inc(s_pref, 1)
            pe.wait_ge(s_exp, 1)
            pe.sem_inc(s_ht, 2)
            pe.sem_inc(s_ya, 2)
            pe.sem_inc(s_xt, 2)
            pe.sem_inc(s_y, 2)

            def transpose_tokens(t, u, fill):
                pe.wait_ge(s_xg[u], fill * 32)
                for j in range(2):
                    for c in range(KC):
                        last = nc.tensor.transpose(bank(6 + j)[:, c * P:c * P + P], xg[:, 2 * u + j, c * P:c * P + P], ident)
                last.then_inc(s_xt, 1)

            def expert(t, u, fill, more):
                pe.wait_ge(s_xc, t * 2 + 2)
                pe.wait_ge(s_wgu[u], fill * 32)
                for b in range(HB0):
                    pe.wait_ge(s_ht, t * HB0 + b + 1)
                    for side, wt in enumerate((wg[u], wu[u])):
                        for c in range(KC):
                            last = mmul(bank(2 * (b % 2) + side, SUP), wt[:, c, b * P:b * P + P], xgT[:, u, c, :],
                                        start=(c == 0), stop=(c == KC - 1))
                    last.then_inc(s_gu, 1)
                if more:
                    transpose_tokens(t + 1, 1 - u, fill + u)
                pe.wait_ge(s_ht, t * HB0 + HB0 + 2)
                pe.wait_ge(s_wdn[u], fill * 16)
                for j in range(2):
                    pe.wait_ge(s_ya, t * 2 + j + 1)
                    for hb in range(HB0):
                        last = mmul(bank(4 + j), hidden[:, hb, j * P:j * P + P], wd[u][:, hb, :],
                                    start=(hb == 0), stop=(hb == HB0 - 1))
                    last.then_inc(s_y, 1)

            transpose_tokens(0, 0, 1)
            with pe.Fori(0, SUPS0 // 2) as i:
                for u in range(2):
                    expert(i * 2 + u, u, i + 1, True)
            expert(SUPS0 - 1, 0, SUPS0 // 2 + 1, False)
            transposed(4 * NT, 1, 4, hin_block)
            for k in range(2):
                pe.wait_ge(s_w, 16 * (6 + 5 + 4 * k))
                pe.wait_ge(s_tpc, 5 * NT + 2 * NT * k)
                for n in range(NT):
                    if n >= 2:
                        pe.wait_ge(s_h2, NT * k + n - 1)
                    w, kc = (W1, 4) if k == 0 else (W2, 8)
                    for side in range(2):
                        for c in range(kc):
                            last = mmul(bank(2 * (n % 2) + side), xT[:, c, n * P:n * P + P], w[:, c, 512 * side:512 * side + 512],
                                        start=(c == 0), stop=(c == kc - 1))
                    last.then_inc(s_proj, 1)
                pe.wait_ge(s_h2, NT * (k + 1))
                pe.wait_ge(s_ad3, k + 1)
                masked_heads(k)
                pe.wait_ge(s_m3, 4 + k)
                maxima_at(0, 3 + k, parts1, H, AT_MAX1)

                def head_sums(i, more):
                    for h in range(2):
                        pe.wait_ge(s_wa, i * 2 + HALVES * k + h + 1)
                        for q in range(2):
                            pe.wait_ge(s_g[2 * h + q], i * 32 + 32 * (STEPS * (7 + 2 * k) + 1))
                            pe.wait_ge(s_ac, i * 4 + 2 * HALVES * (3 + k) + 2 * h + q + 1)
                            ahead = more and h == 0 and q == 1
                            if ahead:
                                maxima_at(i + 1, 3 + k, parts1, H, AT_MAX1)
                            for hd in range(H):
                                if ahead and hd == H - 1:
                                    pe.wait_ge(s_we, i + (STEPS + 1) * (3 + k) + 3)
                                for j in range(2):
                                    u = 4 * h + 2 * q + j
                                    last = mmul(bank(4 * q + hd, C + 1), wring1[:, u, hd, :],
                                                ring1[:, u, (C + 1) * hd:(C + 1) * hd + C + 1], start=(j == 0), stop=(j == 1))
                            last.then_inc(s_pb, 1)

                with pe.Fori(0, STEPS - 1) as i:
                    head_sums(i, True)
                head_sums(STEPS - 1, False)
                transposed(5 * NT + 2 * NT * k, 2, 5 + k, hx_block)
            pe.wait_ge(s_w, 16 * (6 + 10))
            for n in range(NT):
                pe.wait_ge(s_tpc, 7 * NT + 2 * n + 2)
                if n >= 2:
                    pe.wait_ge(s_fcd, n - 1)
                for c in range(8):
                    last = mmul(bank(n % 2), xT[:, c, n * P:n * P + P], Wfc[:, c, :], start=(c == 0), stop=(c == 7))
                last.then_inc(s_fc, 1)
            transposed(9 * NT, 1, 7, hin_block)
            pe.wait_ge(s_rwl, 16 * 5)
            router(9 * NT)
            pe.wait_ge(s_dw, 2)
            for n in range(NT):
                for m in ((0, 1) if n == 0 else (n + 1,)):
                    if m >= 2:
                        pe.wait_ge(s_ctc, m - 1)
                    if m < NT:
                        nc.tensor.transpose(bank(6 + m % 2)[:, 0:P], dw[:, 8 * m:8 * m + P], ident).then_inc(s_ct, 1)
                pe.wait_ge(s_ctc, n + 1)
                if n >= 2:
                    pe.wait_ge(s_cbd, n - 1)
                mmul(bank(4 + n % 2), cwT[:, n % 2, :], b2p, start=True, stop=True).then_inc(s_cb, 1)
            pe.wait_ge(s_cbd, NT)
            pe.sem_inc(s_hd, 2)
            pe.sem_inc(s_yd, 2)
            pe.sem_inc(s_yy, NT)
            with pe.Fori(0, E1 // 2) as i:
                for u in range(2):
                    pe.wait_ge(s_we1[u], i * 32 + 32)
                    for b in range(6):
                        t0, w = CHUNKS[b // 2]
                        pe.wait_ge(s_hd, i * 12 + 6 * u + b + 1)
                        for c in range(KC):
                            last = mmul(bank(b % 2, w), we1v[u][:, c, (b % 2) * P:(b % 2) * P + P], xT[:, c, t0:t0 + w],
                                        start=(c == 0), stop=(c == KC - 1))
                        last.then_inc(s_hu, 1)
                    pe.wait_ge(s_hd, i * 12 + 6 * u + 8)
                    for n in range(NT):
                        pe.wait_ge(s_yd, i * (2 * NT) + NT * u + n + 1)
                        for c in range(2):
                            last = mmul(bank(4 + n % 2), hT[:, c, n * P:n * P + P], we2v[u][:, c, :],
                                        start=(c == 0), stop=(c == 1))
                        last.then_inc(s_yy, 1)

        @block.vector
        def _(dve):
            v = nc.vector
            S = Steps(dve, s_dve)
            do, settle = S.step, S.settle

            def norm_stats(src):
                for n in range(NT):
                    do(v.bn_stats(st[:, n, :], src[:, n, :]))
                settle()
                for n in range(NT):
                    do(v.bn_aggr(mv[:, n, :], st[:, n, :]))
                settle()
                v.tensor_scalar(mv[:, :, 1], mv[:, :, 1], EPS, None, ALU.add).then_inc(s_var, 1)

            def root_back(k):
                dve.wait_ge(s_std, k + 1)
                do(v.reciprocal(rstd[:, :], std[:, :]))
                settle()

            def layer_norm(k):
                norm_stats(X)
                root_back(k)
                for n in range(NT):
                    v.tensor_scalar(hin[:, n, :], X[:, n, :], mv[:, n, 0:1], rstd[:, n:n + 1],
                                    ALU.subtract, ALU.mult).then_inc(s_h, 1)

            def split(dst3, src, rest):
                do(v.tensor_copy(dst3[0], src))
                settle()
                do(v.tensor_tensor(rest, src, dst3[0], ALU.subtract))
                settle()
                do(v.tensor_copy(dst3[1], rest))
                settle()
                do(v.tensor_tensor(dst3[2], rest, dst3[1], ALU.subtract))
                settle()

            do(v.memset(sm[:, :], 0.0))
            do(v.memset(r_pad, 0.0))
            do(v.memset(X[96:P, NT - 1, :], 0.0))
            settle()
            v.memset(r_pad.rearrange("p (t c) -> p t c", c=4)[:, :, 1], -1.0).then_inc(s_padded, 1)
            do(v.memset(slots[:, TILES:COLS, :], -1.0))
            dve.wait_ge(s_const, 32)
            dve.wait_ge(s_edges, 64)
            rows = slice(0, EP)
            do(v.tensor_scalar(r_gi[rows], r_dst[rows], 7, None, ALU.arith_shift_right))
            do(v.tensor_scalar(r_li[rows], r_dst[rows], 127, None, ALU.bitwise_and))
            settle()
            do(v.tensor_copy(r_gf[rows], r_gi[rows]))
            rec = r_rec.rearrange("p (k c) -> p k c", c=4)
            do(v.tensor_copy(rec[rows, :, 1], r_li[rows]))
            do(v.tensor_copy(rec[rows, :, 0].bitcast(I32), r_src[rows]))
            do(v.tensor_copy(rec[rows, :, 2:4], r_ea[rows].rearrange("p (k c) -> p k c", c=2)))
            settle()
            oh = r_oh.rearrange("p (g k) -> p g k", g=NT)
            inc = r_inc.rearrange("p (g k) -> p g k", g=NT)
            rt = r_t.rearrange("p (g k) -> p g k", g=NT)
            do(v.tensor_tensor(oh[rows], r_gf[rows].unsqueeze(1).to_broadcast([EP, NT, EK]),
                               cf[rows, GI:GI + NT].unsqueeze(2).to_broadcast([EP, NT, EK]), ALU.is_equal))
            settle()
            do(v.tensor_tensor_scan(r_inc[rows], r_reset[rows], r_oh[rows], 0.0, ALU.mult, ALU.add))
            settle()
            v.tensor_copy(sm[rows, 0:NT], inc[rows, :, EK - 1]).then_inc(s_tot, 1)
            dve.wait_ge(s_pref, 1)
            smi = sm[:, 10:20].bitcast(I32)
            do(v.tensor_scalar(smi, bank(1, NT), float(SUP - 1), None, ALU.add))
            do(v.tensor_copy(sm[:, 50:60], bank(0, NT)))
            settle()
            do(v.tensor_scalar(smi, smi, 8, None, ALU.arith_shift_right))
            settle()
            do(v.tensor_copy(sm[:, 20:30], smi))
            settle()
            do(v.tensor_tensor_scan(sm[:, 30:40], cf[:, ONES:ONES + NT], sm[:, 20:30], 0.0, ALU.mult, ALU.add))
            settle()
            do(v.tensor_tensor(sm[:, 40:50], sm[:, 30:40], sm[:, 20:30], ALU.subtract))
            settle()
            do(v.scalar_tensor_tensor(sm[:, 60:70], sm[:, 40:50], float(SUP), sm[:, 50:60], ALU.mult, ALU.add))
            settle()
            do(v.tensor_tensor(rt[rows], inc[rows], sm[rows, 60:70].unsqueeze(2).to_broadcast([EP, NT, EK]), ALU.add))
            settle()
            do(v.tensor_tensor(rt[rows], rt[rows], oh[rows], ALU.mult))
            settle()
            do(v.tensor_reduce(r_pos[rows], r_t.rearrange("p (g k) -> p k g", g=NT)[rows], AX.X, ALU.add))
            settle()
            do(v.tensor_scalar(r_posi[rows], r_pos[rows], -1.0, None, ALU.add))
            settle()
            do(v.tensor_scalar(r_gi[rows], r_posi[rows], 7, None, ALU.arith_shift_right))
            do(v.tensor_scalar(r_li[rows], r_posi[rows], 127, None, ALU.bitwise_and))
            settle()
            v.scalar_tensor_tensor(r_rowi[rows], r_li[rows], float(TILES), r_gi[rows], ALU.mult, ALU.add).then_inc(s_route, 1)
            cmp = r_cmp.rearrange("p (s g) -> p s g", g=NT)
            do(v.tensor_tensor(cmp, cf[:, SUPI:SUPI + NSUP].unsqueeze(2).to_broadcast([P, NSUP, NT]),
                               sm[:, 30:40].unsqueeze(1).to_broadcast([P, NSUP, NT]), ALU.is_ge))
            settle()
            nf = small[:, 0:NSUP]
            do(v.tensor_reduce(nf, cmp, AX.X, ALU.add))
            settle()
            do(v.tensor_scalar(nf, nf, float(NT - 1), None, ALU.min))
            settle()
            do(v.tensor_copy(nidx[:, :], nf))
            do(v.tensor_tensor(gneg[:, :, :], nf.unsqueeze(1).to_broadcast([P, NT, NSUP]),
                               cf[:, GI:GI + NT].unsqueeze(2).to_broadcast([P, NT, NSUP]), ALU.not_equal))
            settle()
            v.tensor_scalar(gneg[:, :, :], gneg[:, :, :], -BIG, None, ALU.mult).then_inc(s_nidx, 1)

            dve.wait_ge(s_x, 32)
            layer_norm(0)

            def ring_logits(k):
                for n in range(NT):
                    dve.wait_ge(s_z, COLS * k + n + 1)
                    if n >= 2:
                        dve.wait_ge(s_st, COLS * k + n - 1)
                    v.tensor_tensor(zr[:, n % 2, :], bank(n % 4), xlx[:, n, 0:D], ALU.add).then_inc(s_zd, 1)
                    dve.wait_ge(s_zd, ADDS * k + n + 1)
                    v.scalar_tensor_tensor(zr[:, n % 2, :], zr[:, n % 2, :], 0.0, att, ALU.max, ALU.mult,
                                           accum_out=Rt[:, TILES + n:TILES + n + 1]).then_inc(s_st, 1)
                dve.wait_ge(s_st, COLS * k + NT)
                with dve.Fori(0, STEPS) as i:
                    for h in range(2):
                        done = i * UN + COLS * k + NT + 4 * h
                        added = i * 6 + ADDS * k + NT + 3 * h

                        def add(j, used):
                            dve.wait_ge(s_z, done + j + 1)
                            dve.wait_ge(s_st, used)
                            v.tensor_tensor(zr[:, (h + j) % 2, :], bank(j), ring0[:, 4 * h + j, 0:D], ALU.add).then_inc(s_zd, 1)

                        def logit(j, z):
                            v.scalar_tensor_tensor(zr[:, (h + j) % 2, :] if j < 3 else junk, z, 0.0, att, ALU.max, ALU.mult,
                                                   accum_out=Rt[:, bass.ds(i * UN + 4 * h + j, 1)]).then_inc(s_st, 1)

                        def rows_used(pair):
                            u = 4 * h + 2 * pair
                            v.tensor_copy(Lal[:, bass.ds(i * UN + u, 2)], ring0[:, u:u + 2, D]).then_inc(s_slotA, 1)

                        dve.wait_ge(s_g[2 * h], i * 32 + 32 * (STEPS * 2 * k + 1))
                        add(0, done - 2)
                        add(1, done)
                        for j in range(2):
                            dve.wait_ge(s_zd, added + j + 1)
                            logit(j, zr[:, (h + j) % 2, :])
                        rows_used(0)
                        dve.wait_ge(s_g[2 * h + 1], i * 32 + 32 * (STEPS * 2 * k + 1))
                        add(2, done + 1)
                        dve.wait_ge(s_z, done + 4)
                        dve.wait_ge(s_st, done + 2)
                        logit(3, bank(3))
                        dve.wait_ge(s_zd, added + 3)
                        logit(2, zr[:, h % 2, :])
                        rows_used(1)

            def maxima(i, at, heads, first, banks):
                for h in range(2):
                    for hd in range(heads):
                        kk = h * heads + hd
                        dve.wait_ge(s_mx, i * (2 * heads) + at + kk + 3)
                        v.tensor_reduce(Mx[:, hd, bass.ds(i * 4 + 2 * h, 2)],
                                        bank(first + kk % banks).rearrange("p (s t) -> p s t", s=2), AX.X, ALU.max).then_inc(s_mr, 1)

            def to_supers(tmp, values, parts, whole, heads, done):
                w = whole.rearrange("p (s h) -> p s h", h=heads)
                for hd in range(heads):
                    do(v.tensor_tensor(tmp, values[:, :, hd:hd + 1].to_broadcast([P, NT, NSUP]), gneg[:, :, :], ALU.add))
                    settle()
                    do(v.tensor_reduce(w[:, :, hd], tmp.rearrange("p n s -> p s n"), AX.X, ALU.max))
                    settle()
                of = parts.rearrange("p (s h b) -> p s h b", h=heads, b=3)
                split([of[:, :, :, b] for b in range(3)], w, w)
                v.tensor_copy(sm[:, 0:1], sm[:, 1:2]).then_inc(done, 1)

            def at_edge(to, heads):
                return PS[:, to:to + UN * 3 * heads].rearrange("p (t h b) -> p t h b", h=heads, b=3)

            def exponents(i, nth, to, logits, w):
                at = bass.ds(i * UN, UN)
                dve.wait_ge(s_md, i + STEPS * nth + 1)
                do(v.tensor_reduce(w[:, at, :], at_edge(to, w.shape[2]), AX.X, ALU.add))
                settle()
                do(v.tensor_tensor(w[:, at, :], logits[:, at, :], w[:, at, :], ALU.subtract))
                settle()
                v.tensor_scalar(w[:, at, :], w[:, at, :], 0.0, None, ALU.min).then_inc(s_we, 1)

            def node_maxima(tmp, parts, whole, own, heads):
                for hd in range(heads):
                    do(v.tensor_tensor(tmp, Mx[:, hd, :].unsqueeze(1).to_broadcast([P, NT, NSUP]), gneg[:, :, :], ALU.add))
                    settle()
                    do(v.tensor_reduce(mm[:, :, hd], tmp, AX.X, ALU.max))
                    settle()
                do(v.tensor_tensor(mm[:, :, 0:heads], mm[:, :, 0:heads], own, ALU.max))
                settle()
                to_supers(tmp, mm, parts, whole, heads, s_m3)

            for k in range(3):
                dve.wait_ge(s_bias, 64 * (k + 1))
                do(v.memset(xlx[:, :, D:XW], 1.0))
                settle()
                for n in range(NT):
                    dve.wait_ge(s_proj, NT * k + n + 1)
                    p = 2 * (n % 2)
                    do(v.tensor_tensor(xlx[:, n, 0:D], bank(p), bl, ALU.add))
                    v.tensor_tensor(xrf, bank(p + 1), br, ALU.add).then_inc(s_ev, 1)
                    settle()
                    dve.wait_ge(s_ev, NT * k + n + 1)
                    v.scalar_tensor_tensor(junk, xlx[:, n, 0:D], SLOPE, att, ALU.mult, ALU.mult,
                                           accum_out=xlx[:, n, D:D + 1]).then_inc(s_rows, 1)
                    split([xr3[:, n, b, :] for b in range(3)], xrf, xrf)
                if k == 0:
                    dve.wait_ge(s_slots, 16)
                    dve.wait_ge(s_proj, NT)
                    do(v.memset(ep, 0.0))
                    settle()
                    do(v.memset(ep[:, :, 18], 1.0))
                    attr_parts(v, do, settle, ep, slots[:, 0:TILES, :], Lal[:, 0:TILES])
                    settle()
                    with dve.Fori(0, STEPS) as i:
                        for h in range(2):
                            dve.wait_ge(s_bt, i * 2 + h + 1)
                            v.tensor_tensor(ohr[:, h, 0:4, :], iota.unsqueeze(1).to_broadcast([P, 4, P]),
                                            slots[:, bass.ds(i * UN + 4 * h, 4), 1:2].to_broadcast([P, 4, P]), ALU.is_equal)
                            v.tensor_copy(ohr[:, h, 4, :], epf.bitcast(BF16)[:, bass.ds((i * 2 + h) * P, P)]).then_inc(s_oh, 1)
                    dve.wait_ge(s_btc, HALVES + 2)
                    for c in range(2):
                        whole = easum[:, :, 9 * c]
                        for b in (3, 6):
                            do(v.tensor_tensor(whole, whole, easum[:, :, 9 * c + b], ALU.add))
                            settle()
                    for c, to in ((18, sm[:, 70:80]), (0, slots[:, TILES:COLS, 2]), (9, slots[:, TILES:COLS, 3])):
                        do(v.scalar_tensor_tensor(tmp880, gneg[:, :, :], 0.0, easum[:, :, c].unsqueeze(1).to_broadcast([P, NT, NSUP]),
                                                  ALU.is_equal, ALU.mult))
                        settle()
                        do(v.tensor_reduce(to, tmp880, AX.X, ALU.add))
                        settle()
                    do(v.tensor_scalar(sm[:, 70:80], sm[:, 70:80], 1.0, None, ALU.max))
                    settle()
                    do(v.reciprocal(sm[:, 80:90], sm[:, 70:80]))
                    settle()
                    for c in range(2):
                        own = slots[:, TILES:COLS, 2 + c]
                        do(v.tensor_tensor(own, own, sm[:, 80:90], ALU.mult))
                    settle()
                    do(v.memset(esp[:, :, :], 0.0))
                    settle()
                    attr_parts(v, do, settle, esp[:, 0:NT, :], slots[:, TILES:COLS, :], Lal[:, 0:NT])
                    v.tensor_copy(sm[:, 0:1], sm[:, 1:2]).then_inc(s_esp, 1)
                dve.wait_ge(s_w2, 48 * (k + 1))
                split([wep[:, b, :] for b in range(3)], werow, werem)
                do(v.tensor_scalar(werem, wep[:, 0, :], cf[:, BSEL:BSEL + 1], None, ALU.mult))
                settle()
                do(v.scalar_tensor_tensor(werem, wep[:, 1, :], cf[:, BSEL + 1:BSEL + 2], werem, ALU.mult, ALU.add))
                settle()
                do(v.scalar_tensor_tensor(wsel, wep[:, 2, :], cf[:, BSEL + 2:BSEL + 3], werem, ALU.mult, ALU.add))
                settle()
                for q in range(4):
                    do(v.tensor_scalar(wez[:, q, :], wsel, cf[:, QSEL + q:QSEL + q + 1], None, ALU.mult))
                for c, w in enumerate((we0, we1)):
                    do(v.scalar_tensor_tensor(junk, w, SLOPE, att, ALU.mult, ALU.mult, accum_out=sm[:, 92 + c:93 + c]))
                    settle()
                v.tensor_copy(Lal[:, TILES:COLS], xlx[:, :, D]).then_inc(s_wez, 1)
                dve.wait_ge(s_wez, k + 1)
                ring_logits(k)
                dve.wait_ge(s_st, COLS * (k + 1))
                dve.wait_ge(s_slotA, NSUP * (k + 1) + 4)
                do(v.scalar_tensor_tensor(Rt, Rt, 1.0 - SLOPE, Lal[:, :], ALU.mult, ALU.add))
                settle()
                do(v.scalar_tensor_tensor(Rt, slots[:, :, 2], sm[:, 92:93], Rt, ALU.mult, ALU.add))
                settle()
                v.scalar_tensor_tensor(Rt, slots[:, :, 3], sm[:, 93:94], Rt, ALU.mult, ALU.add).then_inc(s_L, 1)
                dve.wait_ge(s_L, k + 1)
                group = lambda r: r.rearrange("p (g j) -> p g j", j=GT)
                of = lp0.rearrange("p (g b j) -> p g b j", b=3, j=GT)
                split([of[:, :, b, :] for b in range(3)], group(Rt[:, 0:TILES]), group(lrest0))
                v.tensor_copy(sm[:, 0:1], sm[:, 1:2]).then_inc(s_lp, 1)
                with dve.Fori(0, STEPS // 2) as i:
                    for u in range(2):
                        maxima(i * 2 + u, HALVES * k, 1, 2 * u, 2)
                dve.wait_ge(s_mr, HALVES * (k + 1) + 4)
                dve.wait_ge(s_L, k + 1)
                node_maxima(tmp880, parts0, whole0, Rt[:, TILES:COLS].unsqueeze(2), 1)
                v.tensor_tensor(Wt[:, TILES:COLS], Rt[:, TILES:COLS], mm[:, :, 0], ALU.subtract).then_inc(s_we, 1)
                R3, W3 = Rt.unsqueeze(2), Wt.unsqueeze(2)
                exponents(0, k, AT_MAX0, R3, W3)
                dve.wait_ge(s_ex, (STEPS + 1) * k + 1)
                dve.wait_ge(s_tab, 32 * (k + 1))
                for n in range(NT):
                    do(v.tensor_scalar(xlx[:, n, 0:D + 2], xlx[:, n, 0:D + 2], Wt[:, TILES + n:TILES + n + 1], None, ALU.mult))
                settle()

                def weigh(i, h):
                    t = i * UN + 4 * h
                    dve.wait_ge(s_ex, i + (STEPS + 1) * k + 2)
                    for j in range(4):
                        last = v.tensor_scalar(wring[:, 4 * h + j, :], iota, slots[:, bass.ds(t + j, 1), 1:2].rearrange("p t c -> p (t c)"),
                                               Wt[:, bass.ds(t + j, 1)], ALU.is_equal, ALU.mult)
                    last.then_inc(s_wb, 1)

                for h in range(2):
                    weigh(0, h)

                def add_sums(i, more):
                    if more:
                        exponents(i + 1, k, AT_MAX0, R3, W3)
                    for h in range(2):
                        for q in range(2):
                            s = 2 * h + q
                            n = dve.value_load(nidx[0:1, bass.ds(i * 4 + s, 1)], min_val=0, max_val=NT - 1)
                            sums = RA[:, bass.ds(n * XW, D + 2)]
                            dve.wait_ge(s_pb, i * 4 + 2 * HALVES * k + s + 5)
                            dve.wait_ge(s_ac, i * 4 + 2 * HALVES * k + s + 2)
                            v.tensor_tensor(sums, sums, PS[:, 1024 * q:1024 * q + D + 2], ALU.add).then_inc(s_ac, 1)
                        if more:
                            weigh(i + 1, h)

                with dve.Fori(0, STEPS - 1) as i, S.loop(i, STEPS - 1, 2):
                    add_sums(i, True)
                add_sums(STEPS - 1, False)
                dve.wait_ge(s_ac, 2 * HALVES * (k + 1) + 2)
                do(v.tensor_scalar(sm[:, 0:NT], xlx[:, :, D + 1], 1e-16, None, ALU.add))
                settle()
                do(v.reciprocal(sm[:, 10:20], sm[:, 0:NT]))
                settle()
                dve.wait_ge(s_bo, NT * (k + 1))
                for n in range(NT):
                    do(v.scalar_tensor_tensor(hin[:, n, :], xlx[:, n, 0:D], sm[:, 10 + n:11 + n], hin[:, n, :], ALU.mult, ALU.add))
                settle()
                norm_stats(hin)
                root_back(k + 1)
                dve.wait_ge(s_norm, 32 * (k + 1))
                for n in range(NT + 2):
                    inside = n < NT
                    if inside:
                        do(v.scalar_tensor_tensor(hin[:, n, :], hin[:, n, :], mv[:, n, 0:1], gamma, ALU.subtract, ALU.mult))
                    if 1 <= n <= NT:
                        m = n - 1
                        S.all_but(inside)
                        do(v.scalar_tensor_tensor(hin[:, m, :], hin[:, m, :], rstd[:, m:m + 1], beta, ALU.mult, ALU.add))
                    if n >= 2:
                        m = n - 2
                        S.all_but(2 * inside)
                        if k < 2:
                            v.tensor_scalar(hin[:, m, :], hin[:, m, :], 0.0, None, ALU.max).then_inc(s_h, 1)
                        else:
                            v.scalar_tensor_tensor(X[:, m, :], hin[:, m, :], 0.0, X[:, m, :], ALU.max, ALU.add).then_inc(s_x, 1)
                if k == 2:
                    dve.wait_ge(s_x, 32 + NT)
            layer_norm(4)

            def two_best():
                for n in range(NT):
                    do(v.max(v8[:, n, :], lg[:, n, :]))
                settle()
                for n in range(NT):
                    do(v.max_index(i8[:, n, :], v8[:, n, :], lg[:, n, :]))
                settle()
                do(v.tensor_copy(i8f, i8))
                settle()

            def place(first, second):
                eight = cf[:, XI:XI + 8].unsqueeze(1).to_broadcast([P, NT, 8])
                for to, c, val in ((dwv, 0, first), (dw2, 1, second)):
                    do(v.tensor_tensor(to, eight, i8f[:, :, c:c + 1].to_broadcast([P, NT, 8]), ALU.is_equal))
                    settle()
                    do(v.tensor_tensor(to, to, val.to_broadcast([P, NT, 8]), ALU.mult))
                    settle()
                v.tensor_tensor(dwv, dwv, dw2, ALU.add).then_inc(s_dw, 1)

            dve.wait_ge(s_rt, 1)
            do(v.tensor_copy(lg, bank(4, 80).rearrange("p (n e) -> p n e", e=8)))
            settle()
            two_best()
            v.tensor_tensor(sm[:, 20:30], v8[:, :, 1], v8[:, :, 0], ALU.subtract).then_inc(s_re, 1)
            dve.wait_ge(s_rx, 1)
            do(v.tensor_scalar(sm[:, 40:50], sm[:, 30:40], 1.0, None, ALU.add))
            settle()
            do(v.reciprocal(sm[:, 50:60], sm[:, 40:50]))
            settle()
            do(v.tensor_tensor(sm[:, 60:70], sm[:, 50:60], sm[:, 30:40], ALU.mult))
            settle()
            do(v.memset(p_reset, 1.0))
            do(v.tensor_copy(tokid, cf[:, TOK:TOK + NT]))
            for c in range(2):
                do(v.tensor_copy(picks[:, c * NT:c * NT + NT], i8f[:, :, c]))
            v.memset(zeros, 0).then_inc(s_dw, 1)
            settle()
            by = lambda r: r.rearrange("p (e k) -> p e k", e=E0)
            do(v.memset(by(p_reset)[:, :, 0:1], 0.0))
            do(v.tensor_tensor(by(p_oh), picks.unsqueeze(1).to_broadcast([P, E0, PICKS]),
                               cf[:, XI:XI + E0].unsqueeze(2).to_broadcast([P, E0, PICKS]), ALU.is_equal))
            settle()
            do(v.tensor_tensor_scan(p_inc, p_reset, p_oh, 0.0, ALU.mult, ALU.add))
            settle()
            v.tensor_copy(sm[:, 0:E0], by(p_inc)[:, :, PICKS - 1]).then_inc(s_tot, 1)
            dve.wait_ge(s_pref, 2)
            padded = sm[:, 10:18].bitcast(I32)
            do(v.tensor_scalar(padded, bank(1, E0), float(SUP - 1), None, ALU.add))
            settle()
            do(v.tensor_scalar(padded, padded, 8, None, ALU.arith_shift_right))
            settle()
            do(v.tensor_copy(sm[:, 20:28], padded))
            settle()
            do(v.tensor_tensor_scan(sm[:, 30:38], cf[:, ONES:ONES + E0], sm[:, 20:28], 0.0, ALU.mult, ALU.add))
            settle()
            do(v.tensor_tensor(sm[:, 40:48], sm[:, 30:38], sm[:, 20:28], ALU.subtract))
            settle()
            do(v.scalar_tensor_tensor(sm[:, 0:E0], sm[:, 40:48], float(SUP), bank(0, E0), ALU.mult, ALU.add))
            settle()
            do(v.tensor_tensor(by(p_t), by(p_inc), sm[:, 0:E0].unsqueeze(2).to_broadcast([P, E0, PICKS]), ALU.add))
            settle()
            do(v.tensor_tensor(p_t, p_t, p_oh, ALU.mult))
            settle()
            do(v.tensor_reduce(pos0, p_t.rearrange("p (e k) -> p k e", e=E0), AX.X, ALU.add))
            settle()
            do(v.tensor_scalar(place0, pos0, -1.0, None, ALU.add))
            settle()
            do(v.tensor_scalar(hi0, place0, 7, None, ALU.arith_shift_right))
            do(v.tensor_scalar(lo0, place0, 127, None, ALU.bitwise_and))
            settle()
            do(v.scalar_tensor_tensor(row0, lo0, float(2 * SUPS0), hi0, ALU.mult, ALU.add))
            se = p_cmp.rearrange("p (s e) -> p s e", e=E0)
            do(v.tensor_tensor(se, cf[:, SUPI:SUPI + SUPS0].unsqueeze(2).to_broadcast([P, SUPS0, E0]),
                               sm[:, 30:38].unsqueeze(1).to_broadcast([P, SUPS0, E0]), ALU.is_ge))
            settle()
            do(v.tensor_reduce(p_oh[:, 0:SUPS0], se, AX.X, ALU.add))
            settle()
            v.tensor_scalar(eidx, p_oh[:, 0:SUPS0], float(E0 - 1), None, ALU.min).then_inc(s_exp, 1)

            def hidden_and_out(t):
                for b in range(HB0):
                    dve.wait_ge(s_sg, t * HB0 + b + 1)
                    if b == 0:
                        dve.wait_ge(s_y, t * 2 + 2)
                    v.tensor_tensor(hidden[:, b, :], sg[:, b % 2, :], bank(2 * (b % 2) + 1, SUP), ALU.mult).then_inc(s_ht, 1)
                dve.wait_ge(s_yst, t * 16 + 16)
                for j in range(2):
                    dve.wait_ge(s_y, t * 2 + j + 3)
                    v.tensor_copy(yst[:, j, :], bank(4 + j)).then_inc(s_ya, 1)

            with dve.Fori(0, SUPS0 // 2) as i:
                for u in range(2):
                    hidden_and_out(i * 2 + u)
            hidden_and_out(SUPS0 - 1)
            for j in range(NT // 2):
                dve.wait_ge(s_yg[j], 64)
                for c in range(2):
                    for n in (2 * j, 2 * j + 1):
                        do(v.scalar_tensor_tensor(X[:, n, :], yg[:, c * NT + n, :], sm[:, 50 + 10 * c + n:51 + 10 * c + n],
                                                  X[:, n, :], ALU.mult, ALU.add))
                    settle()
            layer_norm(5)
            for k in range(2):
                dve.wait_ge(s_w, 16 * (6 + 5 + 4 * k))
                for n in range(NT):
                    dve.wait_ge(s_h2, NT * k + n + 1)
                    if n:
                        dve.wait_ge(s_rows, NT * (3 + k) + n)
                    v.memset(hx4[:, n, :, C:C + 1], 1.0)
                    for hd in range(H):
                        for side, (vec, to) in enumerate(((asv, als), (adv, ald))):
                            last = v.scalar_tensor_tensor(PS[:, 2048 + C * (2 * hd + side):2048 + C * (2 * hd + side + 1)], hx4[:, n, hd, 0:C], 1.0, vec[:, C * hd:C * hd + C],
                                                          ALU.mult, ALU.mult, accum_out=to[:, n, hd:hd + 1])
                    last.then_inc(s_rows, 1)
                dve.wait_ge(s_rows, NT * (4 + k))
                do(v.tensor_tensor(Et[:, TILES:COLS, :], als[:, :, :], ald[:, :, :], ALU.add))
                to_supers(tmp1, ald, parts1, whole1, H, s_ad3)
                own = Et[:, TILES:COLS, :]
                do(v.scalar_tensor_tensor(own, own, SLOPE, own, ALU.mult, ALU.max))
                parts = [lp[:, b * UN * H:(b + 1) * UN * H].rearrange("p (t h) -> p t h", h=H) for b in range(3)]
                rest = lrest.rearrange("p (t h) -> p t h", h=H)

                def edge_logits(i):
                    dve.wait_ge(s_adp, i + STEPS * k + 1)
                    do(v.tensor_reduce(Et[:, bass.ds(i * UN, UN), :], at_edge(AT_ADP, H), AX.X, ALU.add))
                    settle()
                    for q in range(4):
                        dve.wait_ge(s_g[q], i * 32 + 32 * (STEPS * (6 + 2 * k) + 1))
                        at = bass.ds(i * UN + 2 * q, 2)
                        v.tensor_tensor(Et[:, at, :], asr[:, 2 * q:2 * q + 2, :], Et[:, at, :], ALU.add).then_inc(s_slotA, 1)
                    dve.wait_ge(s_slotA, i * 4 + NSUP * (3 + k) + 8)
                    e8 = Et[:, bass.ds(i * UN, UN), :]
                    do(v.scalar_tensor_tensor(e8, e8, SLOPE, e8, ALU.mult, ALU.max))
                    settle()
                    do(v.tensor_scalar(parts[0], e8, 1.0, None, ALU.mult))
                    settle()
                    do(v.tensor_tensor(rest, e8, parts[0], ALU.subtract))
                    settle()
                    do(v.tensor_copy(parts[1], rest))
                    settle()
                    v.tensor_tensor(parts[2], rest, parts[1], ALU.subtract).then_inc(s_lp, 1)

                edge_logits(0)
                with dve.Fori(0, STEPS - 1) as i, S.loop(i, STEPS - 1, 5):
                    dve.wait_ge(s_lt, i + STEPS * k + 3 * GROUPS + 1)
                    edge_logits(i + 1)
                    maxima(i, HALVES * (3 + H * k), H, 0, 4)
                maxima(STEPS - 1, HALVES * (3 + H * k), H, 0, 4)
                dve.wait_ge(s_lp, STEPS * (k + 1) + 3)
                dve.wait_ge(s_mr, HALVES * (3 + H * (k + 1)) + 4)
                node_maxima(tmp1, parts1, whole1, Et[:, TILES:COLS, :], H)
                v.tensor_tensor(Ew[:, TILES:COLS, :], Et[:, TILES:COLS, :], mm[:, :, :], ALU.subtract).then_inc(s_we, 1)
                exponents(0, 3 + k, AT_MAX1, Et, Ew)
                dve.wait_ge(s_ex, (STEPS + 1) * (3 + k) + 1)
                dve.wait_ge(s_tab, 32 * (4 + k))
                for n in range(NT):
                    for hd in range(H - 2):
                        do(v.tensor_scalar(hx4[:, n, hd, :], hx4[:, n, hd, :],
                                           Ew[:, TILES + n, hd:hd + 1], None, ALU.mult))
                settle()

                def weigh1(i, h):
                    t = i * UN + 4 * h
                    dve.wait_ge(s_ex, i + (STEPS + 1) * (3 + k) + 2)
                    for j in range(4):
                        node = slots[:, bass.ds(t + j, 1), 1:2].rearrange("p t c -> p (t c)")
                        v.tensor_scalar(wring1[:, 4 * h + j, H - 1, :], iota, node, None, ALU.is_equal)
                        for hd in range(H - 2):
                            last = v.tensor_scalar(wring1[:, 4 * h + j, hd, :], iota,
                                                   slots[:, bass.ds(t + j, 1), 1:2].rearrange("p t c -> p (t c)"),
                                                   Ew[:, bass.ds(t + j, 1), hd:hd + 1].rearrange("p t c -> p (t c)"), ALU.is_equal, ALU.mult)
                    last.then_inc(s_wb, 1)

                for h in range(2):
                    weigh1(0, h)

                dve.wait_ge(s_self, k + 1)

                def add_head_sums(i, more):
                    for h in range(2):
                        for q in range(2):
                            if more and h == 0 and q == 0:
                                exponents(i + 1, 3 + k, AT_MAX1, Et, Ew)
                            s = 2 * h + q
                            n = dve.value_load(nidx[0:1, bass.ds(i * 4 + s, 1)], min_val=0, max_val=NT - 1)
                            sums = RA[:, bass.ds(n * HW, HW)].rearrange("p (h c) -> p h c", h=H)
                            dve.wait_ge(s_pb, i * 4 + 2 * HALVES * (3 + k) + s + 5)
                            dve.wait_ge(s_ac, i * 4 + 2 * HALVES * (3 + k) + s + 2)
                            v.tensor_tensor(sums, sums, PS[:, 2048 * q:2048 * q + 2048].rearrange("p (h c) -> p h c", h=H)[:, :, 0:C + 1],
                                            ALU.add).then_inc(s_ac, 1)
                        if more:
                            weigh1(i + 1, h)

                with dve.Fori(0, STEPS - 1) as i, S.loop(i, STEPS - 1, 2):
                    add_head_sums(i, True)
                add_head_sums(STEPS - 1, False)
                dve.wait_ge(s_ac, 2 * HALVES * (4 + k) + 2)
                do(v.reciprocal(mm[:, :, :], hx4[:, :, :, C]))
                settle()
                for n in range(NT):
                    for hd in range(H):
                        do(v.scalar_tensor_tensor(hx4[:, n, hd, 0:C], hx4[:, n, hd, 0:C], mm[:, n, hd:hd + 1],
                                                  gb[:, C * hd:C * hd + C], ALU.mult, ALU.add))
                    if n:
                        S.all_but(H)
                        v.tensor_scalar(hx4[:, n - 1, :, 0:C], hx4[:, n - 1, :, 0:C], 0.0, None, ALU.max).then_inc(s_h, 1)
                settle()
                v.tensor_scalar(hx4[:, NT - 1, :, 0:C], hx4[:, NT - 1, :, 0:C], 0.0, None, ALU.max).then_inc(s_h, 1)
            for n in range(NT):
                dve.wait_ge(s_fc, n + 1)
                do(v.tensor_tensor(X[:, n, :], X[:, n, :], bfc, ALU.add))
                settle()
                v.tensor_tensor(X[:, n, :], X[:, n, :], bank(n % 2), ALU.add).then_inc(s_fcd, 1)
            dve.wait_ge(s_fcd, NT)
            layer_norm(6)
            do(v.memset(dw, 0.0))
            dve.wait_ge(s_rwl, 16 * 5)
            dve.wait_ge(s_rt, 2)
            do(v.tensor_tensor(lg, bank(4, 80).rearrange("p (n e) -> p n e", e=8), brr.unsqueeze(1).to_broadcast([P, NT, 8]), ALU.add))
            settle()
            do(v.tensor_reduce(sm[:, 0:NT], lg, AX.X, ALU.max))
            settle()
            v.tensor_tensor(lg, lg, sm[:, 0:NT].unsqueeze(2).to_broadcast([P, NT, 8]), ALU.subtract).then_inc(s_re, 1)
            dve.wait_ge(s_rx, 2)
            do(v.tensor_reduce(sm[:, 10:20], lg, AX.X, ALU.add))
            settle()
            do(v.reciprocal(sm[:, 20:30], sm[:, 10:20]))
            settle()
            do(v.tensor_tensor(lg, lg, sm[:, 20:30].unsqueeze(2).to_broadcast([P, NT, 8]), ALU.mult))
            settle()
            two_best()
            place(v8[:, :, 0:1], v8[:, :, 1:2])
            dve.wait_ge(s_dw, 2)
            for n in range(NT):
                dve.wait_ge(s_ct, n + 1)
                v.tensor_copy(cwT[:, n % 2, :], bank(6 + n % 2, P)).then_inc(s_ctc, 1)
                dve.wait_ge(s_cb, n + 1)
                v.tensor_tensor(X[:, n, :], X[:, n, :], bank(4 + n % 2), ALU.add).then_inc(s_cbd, 1)
            dve.wait_ge(s_cbd, NT)
            with dve.Fori(0, E1 // 2) as i:
                for u in range(2):
                    for b in range(6):
                        t0, w = CHUNKS[b // 2]
                        dve.wait_ge(s_hu, i * 12 + 6 * u + b + 1)
                        v.tensor_scalar(hT[:, b % 2, t0:t0 + w], bank(b % 2, w), b1c[:, bass.ds(i * 4 + 2 * u + b % 2, 1)], 0.0,
                                        ALU.add, ALU.max).then_inc(s_hd, 1)
                    for n in range(NT):
                        dve.wait_ge(s_yy, i * (2 * NT) + NT * u + n + 1 + NT)
                        v.scalar_tensor_tensor(X[:, n, :], bank(4 + n % 2), dw[:, bass.ds(i * 2 + (u + 8 * n), 1)], X[:, n, :],
                                               ALU.mult, ALU.add).then_inc(s_yd, 1)
            dve.wait_ge(s_yd, E1 * NT + 2)
            v.tensor_copy(sm[:, 0:1], sm[:, 1:2]).then_inc(s_out, 1)


def attr_parts(v, do, settle, to, slots, rest):
    for c in range(2):
        src = slots[:, :, 2 + c]
        for a in range(3):
            cols = [to[:, :, c * 9 + a * 3 + b] for b in range(3)]
            for col in cols:
                do(v.tensor_copy(col, src))
            settle()
            if a < 2:
                do(v.tensor_tensor(rest, src, cols[0], ALU.subtract))
                settle()
                src = rest


_SHAPED = ("x", "src", "dst", "edge_attr_2", "L0_gnn_Wl", "L0_gnn_bl", "L0_gnn_Wr", "L0_gnn_br", "L0_gnn_We", "L0_gnn_att",
           "L0_gnn_b_out", "L0_gnn_gamma", "L0_gnn_beta", "L0_ffn_w_gate", "L0_ffn_w_up", "L0_ffn_w_down", "L1_gnn_W1",
           "L1_gnn_a_src1", "L1_gnn_a_dst1", "L1_gnn_b1", "L1_gnn_W2", "L1_gnn_a_src2", "L1_gnn_a_dst2", "L1_gnn_b2",
           "L1_gnn_Wfc", "L1_gnn_bfc", "L1_ffn_br", "L1_ffn_W1", "L1_ffn_W2")


def kernel(**inputs):
    import ml_dtypes
    import concourse.bacc as bacc
    from concourse.bass_utils import run_bass_kernel_spmd

    arrays = {k: np.ascontiguousarray(inputs[k]) for k in _SHAPED}
    cf, cb, reset = constants()
    arrays["cf"], arrays["cb"], arrays["reset"] = cf, cb.astype(ml_dtypes.bfloat16), reset
    We = np.asarray(inputs["L0_gnn_We"])
    rows = np.zeros((3, P, D), np.float32)
    for q in range(4):
        for c in range(2):
            rows[:, 32 * q + 9 * c:32 * q + 9 * c + 9] = We[:, c:c + 1]
    arrays["we_rows"] = rows
    inner = lambda w: np.ascontiguousarray(w.reshape(KC, P, 8).transpose(1, 0, 2).reshape(P, KC * 8))
    arrays["router0"] = inner(np.asarray(inputs["L0_ffn_router_w"]).T)
    arrays["router1"] = inner(np.asarray(inputs["L1_ffn_Wr"]))
    b1 = np.asarray(inputs["L1_ffn_b1"])
    arrays["b1_cols"] = np.ascontiguousarray(b1.reshape(E1 * 2, P).T)
    b2 = np.zeros((P, D), np.float32)
    b2[0:E1] = inputs["L1_ffn_b2"]
    arrays["b2_rows"] = b2

    nc = bacc.Bacc("TRN2", target_bir_lowering=False, num_devices=1)
    a = {k: nc.dram_tensor(f"in_{k}", v.shape, mybir.dt.from_np(v.dtype), kind="ExternalInput").ap() for k, v in arrays.items()}
    out = nc.dram_tensor("out", (N, D), F32, kind="ExternalOutput").ap()
    build(nc, a, out)
    r = run_bass_kernel_spmd(nc, [{f"in_{k}": v for k, v in arrays.items()}], core_ids=[0])
    return r.results[0]["out"]
```
